# Optimizing a Trainium2 kernel written in Bass

```python
import numpy as np
import jax
import jax.numpy as jnp

def _softmax(x, axis=-1):
    return jax.nn.softmax(x, axis=axis)

def _gelu(x):
    return jax.nn.gelu(x, approximate=True)

def _silu(x):
    return jax.nn.silu(x)

def _sigmoid(x):
    return jax.nn.sigmoid(x)

def _layernorm(x, axis=-1, eps=1e-05):
    m = jnp.mean(x, axis=axis, keepdims=True)
    v = jnp.var(x, axis=axis, keepdims=True)
    return (x - m) / jnp.sqrt(v + eps)

def _scatter_add(tgt, idx, src, axis=0):
    return tgt.at[idx].add(src)

def _segment_sum(src, seg, n):
    return jax.ops.segment_sum(src, seg, n)
kernel_name = 'mk_sandwich_d1_jaxref_r4_9a55c5'

def setup_inputs(seed: int=0):
    np.random.seed(seed)
    _w = jnp.asarray

    def _L0_attn_setup():
        import jax, jax.numpy as jnp
        import numpy as np
        import math
        B, L, D, H = (32, 128, 1024, 32)
        HD = D // H
        key = jax.random.key(seed)
        ks = jax.random.split(key, 9)
        s = 1.0 / math.sqrt(D)
        return {'x': jax.random.normal(ks[0], (B, L, D), jnp.float32), 'Wq': jax.random.normal(ks[1], (D, D), jnp.float32) * s, 'bq': jax.random.normal(ks[2], (D,), jnp.float32) * s, 'Wk': jax.random.normal(ks[3], (D, D), jnp.float32) * s, 'bk': jax.random.normal(ks[4], (D,), jnp.float32) * s, 'Wv': jax.random.normal(ks[5], (D, D), jnp.float32) * s, 'bv': jax.random.normal(ks[6], (D,), jnp.float32) * s, 'Wo': jax.random.normal(ks[7], (D, D), jnp.float32) * s, 'bo': jax.random.normal(ks[8], (D,), jnp.float32) * s}
    _L0_attn_in = _L0_attn_setup()

    def _L0_ffn_setup():
        import jax, jax.numpy as jnp
        import numpy as np
        HIDDEN = 1024
        INTER = 2752
        RANK = 256
        B, S = (2, 512)
        key = jax.random.key(seed)
        ks = jax.random.split(key, 7)
        sc = 0.02
        return {'x': jax.random.normal(ks[0], (B, S, HIDDEN), dtype=jnp.float32), 'U1': jax.random.normal(ks[1], (HIDDEN, RANK), dtype=jnp.float32) * sc, 'V1': jax.random.normal(ks[2], (RANK, 2 * INTER), dtype=jnp.float32) * sc, 'U2': jax.random.normal(ks[3], (INTER, RANK), dtype=jnp.float32) * sc, 'V2': jax.random.normal(ks[4], (RANK, HIDDEN), dtype=jnp.float32) * sc, 'b1': jax.random.normal(ks[5], (2 * INTER,), dtype=jnp.float32) * sc, 'b2': jax.random.normal(ks[6], (HIDDEN,), dtype=jnp.float32) * sc}
    _L0_ffn_in = _L0_ffn_setup()
    _d = {'L0_attn_x': _L0_attn_in['x'], 'L0_attn_Wq': _L0_attn_in['Wq'], 'L0_attn_bq': _L0_attn_in['bq'], 'L0_attn_Wk': _L0_attn_in['Wk'], 'L0_attn_bk': _L0_attn_in['bk'], 'L0_attn_Wv': _L0_attn_in['Wv'], 'L0_attn_bv': _L0_attn_in['bv'], 'L0_attn_Wo': _L0_attn_in['Wo'], 'L0_attn_bo': _L0_attn_in['bo'], 'L0_ffn_U1': _L0_ffn_in['U1'], 'L0_ffn_V1': _L0_ffn_in['V1'], 'L0_ffn_U2': _L0_ffn_in['U2'], 'L0_ffn_V2': _L0_ffn_in['V2'], 'L0_ffn_b1': _L0_ffn_in['b1'], 'L0_ffn_b2': _L0_ffn_in['b2']}
    _x0 = _d['L0_attn_x']
    _d['L0_attn_x'] = jax.random.normal(jax.random.fold_in(jax.random.key(seed), 1), (1, 2048, 1024), dtype=_x0.dtype)
    del _x0
    return _d

def reference(L0_attn_x, L0_attn_Wq, L0_attn_bq, L0_attn_Wk, L0_attn_bk, L0_attn_Wv, L0_attn_bv, L0_attn_Wo, L0_attn_bo, L0_ffn_U1, L0_ffn_V1, L0_ffn_U2, L0_ffn_V2, L0_ffn_b1, L0_ffn_b2):

    def _L0_attn_ref(x, Wq, bq, Wk, bk, Wv, bv, Wo, bo):
        import jax, jax.numpy as jnp
        import numpy as np
        import math
        B, L, D, H = (32, 128, 1024, 32)
        HD = D // H
        b, l, d = x.shape
        h, hd = (H, HD)
        q = (x @ Wq.T + bq).reshape(b, l, h, hd).transpose(0, 2, 1, 3)
        k = (x @ Wk.T + bk).reshape(b, l, h, hd).transpose(0, 2, 1, 3)
        v = (x @ Wv.T + bv).reshape(b, l, h, hd).transpose(0, 2, 1, 3)
        scores = jnp.einsum('bhqd,bhkd->bhqk', q, k) / math.sqrt(hd)
        causal = jnp.tril(jnp.ones((l, l), bool))
        scores = jnp.where(causal, scores, -jnp.inf)
        att = jax.nn.softmax(scores, axis=-1)
        out = jnp.einsum('bhqk,bhkd->bhqd', att, v)
        out = out.transpose(0, 2, 1, 3).reshape(b, l, d)
        return out @ Wo.T + bo

    def _L0_ffn_ref(x, U1, V1, U2, V2, b1, b2):
        import jax, jax.numpy as jnp
        import numpy as np
        HIDDEN = 1024
        INTER = 2752
        RANK = 256
        B, S = (2, 512)
        P = jnp.einsum('bsh,hr->bsr', x, U1)
        H = jnp.einsum('bsr,rf->bsf', P, V1) + b1
        gate, up = (H[..., :INTER], H[..., INTER:])
        act = jax.nn.silu(gate) * up
        Z = jnp.einsum('bsi,ir->bsr', act, U2)
        out = jnp.einsum('bsr,rh->bsh', Z, V2) + b2
        return out
    x = L0_attn_x
    x = x + _layernorm(_L0_attn_ref(_layernorm(x, axis=-1), L0_attn_Wq, L0_attn_bq, L0_attn_Wk, L0_attn_bk, L0_attn_Wv, L0_attn_bv, L0_attn_Wo, L0_attn_bo), axis=-1)
    x = x + _layernorm(_L0_ffn_ref(_layernorm(x, axis=-1), L0_ffn_U1, L0_ffn_V1, L0_ffn_U2, L0_ffn_V2, L0_ffn_b1, L0_ffn_b2), axis=-1)
    return x

_drawn_inputs = setup_inputs


def setup_inputs(seed=0):
    import zlib

    import numpy as np

    out = dict(_drawn_inputs(seed))
    spreads = {}
    factors = {'L0_attn_bq': 3.924, 'L0_attn_bk': 8.0}
    for name, (base, spread) in spreads.items():
        noise = np.random.default_rng([zlib.crc32(name.encode()), seed]).standard_normal(out[name].shape)
        drawn = base * np.exp(spread * noise) if base else spread * noise
        out[name] = jnp.asarray(drawn.astype(out[name].dtype))
    for name, factor in factors.items():
        out[name] = (out[name] * factor).astype(out[name].dtype)
    return out
```

```python
from contextlib import ExitStack

import concourse.bass as bass
from concourse import mybir

F32 = mybir.dt.float32
F16 = mybir.dt.float16
BF16 = mybir.dt.bfloat16
ALU = mybir.AluOpType
ACT = mybir.ActivationFunctionType
AX = mybir.AxisListType

P = 128
S = 2048
D = 1024
NH = 32
HD = D // NH
GH = P // HD
NG = NH // GH
KC = D // P
TT = S // P
CH = 512
NCH = S // CH
TPC = CH // P
RANK = 256
RC = RANK // P
INTER = 2752
FT = -(-INTER // P)
FLAST = INTER - (FT - 1) * P
EPS = 1e-5

WS = 16.0
MROW = 2048.0
EXP_SCALE = 1.0 / (WS * WS * HD ** 0.5)
NEG = -1e30

VW = 2 * HD + 1
STK = 3 * HD
ROWS = STK + 2

BLOCKS = []
for qc in range(NCH):
    for kt in range(TPC * (qc + 1)):
        q0 = max(CH * qc, P * kt)
        BLOCKS.append((qc, kt, q0, CH * (qc + 1) - q0, kt >= TPC * qc))
NB = len(BLOCKS)
GB = GH * NB
MBLOCKS = [(t, c, min(CH, (t + 1) * P - c * CH), c == t // TPC) for t in range(TT) for c in range(t // TPC + 1)]
MR = len(MBLOCKS) + 1
MSPAN = 34
LAG = 5
RING = 8
ST_BANKS = 3

QK_START, QK_EVERY, QK_SPAN = 4, 13, 12
V_START, V_EVERY, V_SPAN = 110, 12, 8
PER_GROUP = 2 * NCH + NCH
SPLIT_AT = {0: 0, 1: 30, 2: 60}


def hi_on_dve(s):
    return s % 4 == 1


def hi_on_act(s):
    return not hi_on_dve(s)


def lo_on_dve(s):
    return s % 4 == 3


def lo_on_pool(s):
    return not lo_on_dve(s)


def count(which, s):
    per = sum(map(which, range(GB)))
    return per * (s // GB) + sum(map(which, range(s % GB + 1)))


def same_bank_before(s):
    return max(x - GB if x > s - 1 else x for x in range(GB) if x % ST_BANKS == s % ST_BANKS and x != s) \
        if s < ST_BANKS else s - ST_BANKS


def max_blocks_at(i):
    return [a for a in range(len(MBLOCKS)) if a * MSPAN // len(MBLOCKS) == i]


def projections():
    out = [("qk"[n // NCH], n % NCH, QK_START + QK_EVERY * n, QK_SPAN) for n in range(2 * NCH)]
    return out + [("v", n, V_START + V_EVERY * n, V_SPAN) for n in range(NCH)]


PROJ = projections()

ENDS = [NB * j + max(i for i, bl in enumerate(BLOCKS) if bl[0] == qc) for j in range(GH) for qc in range(NCH)]


def chunks_at(s, delay):
    return [c for c, e in enumerate(ENDS) if e + delay == s]


def chunks_after(delay, last):
    return [c for c, e in enumerate(ENDS) if e + delay > last]


def steps_of(kind):
    parts = [("hi", "hi"), ("hi", "lo"), ("lo", "hi")]
    if kind == "v":
        return [(r, p, k) for r in range(TPC) for p in parts for k in range(KC)]
    return [(None, p, k) for p in parts for k in range(KC)]


def attention_phase(nc, x, wq, wk, wv, bq, bk, attn):
    ctx = ExitStack()
    with ctx:
        def sb(name, shape, dt):
            return ctx.enter_context(nc.sbuf_tensor(name, shape, dt))

        def ps(name, shape, dt=F32):
            return ctx.enter_context(nc.psum_tensor(name, shape, dt))

        def sem(name):
            return ctx.enter_context(nc.semaphore(name))

        ident = sb("ident", [P, P], F32)
        ident_h = sb("ident_h", [P, P], F16)
        ident_b = sb("ident_b", [P, P], BF16)
        mask_qk = sb("mask_qk", [P, P], BF16)
        mask_kq = sb("mask_kq", [P, P], BF16)
        neg_half = sb("neg_half", [P, 1], F32)
        xt = {"hi": sb("xt_hi", [P, KC, S], F16), "lo": sb("xt_lo", [P, KC, S], F16)}
        stats = sb("stats", [P, 2, 2, 6], F32)
        mv = sb("mv", [P, 2, 2], F32)
        rs = sb("rs", [P, 2, 4], F32)
        w_raw = [sb(f"w_raw{i}", [P, KC * P], F32) for i in range(3)]
        w = [{h: sb(f"w_{h}{i}", [P, KC, P], F16) for h in ("hi", "lo")} for i in range(3)]
        b_raw = [sb(f"b_raw{i}", [P, 1], F32) for i in range(2)]
        b_sc = [sb(f"b_sc{i}", [P, 1], F32) for i in range(2)]
        nat = [{h: sb(f"nat_{h}{i}", [P, S], F16) for h in ("hi", "lo")} for i in range(2)]
        q_st = [sb(f"q_st{j}", [P, S], F16) for j in range(GH)]
        k_st = [sb(f"k_st{j}", [P, S], F16) for j in range(GH)]
        v_next = sb("v_next", [P, GH, TT, VW], F16)
        v_cur = sb("v_cur", [P, GH, TT, VW], F16)
        p32 = sb("p32", [P, RING, CH], F32)
        p_hi = sb("p_hi", [P, RING, CH], F16)
        p_lo = sb("p_lo", [P, RING, CH], F16)
        m_part = sb("m_part", [P, TT, NCH], F32)
        m_all = sb("m_all", [P, TT], F32)
        m_cols = sb("m_cols", [P, 2 * TT], F16)
        m_rows = sb("m_rows", [2 * TT, P], F16)
        o_cp = sb("o_cp", [P, 2, TPC, VW], F32)
        o_rd = sb("o_rd", [P, 2, TPC], F32)
        o_sum = sb("o_sum", [P, 2, TPC, HD], F32)
        attn_g = sb("attn_g", [P, TT, P], F32)

        xin = p32[:, 0:3 * D // CH, :].rearrange("p (t h) n -> p t (h n)", t=3)
        xn = attn_g[:, :, :].rearrange("p (t a) n -> p t (a n)", t=2)

        st = [ps(f"st{i}", [P, CH]) for i in range(ST_BANKS)]
        mx = [ps(f"mx{i}", [P, CH]) for i in range(2)]
        av = [ps(f"av{i}", [P, CH]) for i in range(2)]
        pj = ps("pj", [P, CH])

        consts = sem("consts")
        consts_dve = sem("consts_dve")
        x_loaded = [sem(f"x_loaded{i}") for i in range(3)]
        x_stats = sem("x_stats")
        dve_step = sem("dve_step")
        pool_step = sem("pool_step")
        x_rstd = sem("x_rstd")
        x_normed = sem("x_normed")
        xt_psum = sem("xt_psum")
        xt_hi = sem("xt_hi")
        xt_lo = sem("xt_lo")
        w_loaded = [sem(f"w_loaded{i}") for i in range(3)]
        w_hi = [sem(f"w_hi{i}") for i in range(3)]
        w_lo = [sem(f"w_lo{i}") for i in range(3)]
        proj_psum = sem("proj_psum")
        proj_hi = sem("proj_hi")
        proj_lo = sem("proj_lo")
        stack_set = [sem(f"stack_set{j}") for j in range(GH)]
        v_set = [sem(f"v_set{j}") for j in range(GH)]
        m_psum = sem("m_psum")
        m_done = sem("m_done")
        m_chain = sem("m_chain")
        m_cols_set = sem("m_cols_set")
        m_rows_set = sem("m_rows_set")
        m_in_stack = sem("m_in_stack")
        st_psum = sem("st_psum")
        p32_set = sem("p32_set")
        hi_act = sem("hi_act")
        hi_dve = sem("hi_dve")
        lo_dve = sem("lo_dve")
        lo_pool = sem("lo_pool")
        av_psum = sem("av_psum")
        av_used = sem("av_used")
        rd_set = sem("rd_set")
        o_added = sem("o_added")
        o_done = sem("o_done")
        attn_free = sem("attn_free")

        x_t = x.rearrange("(t p) d -> t p d", p=P)
        attn_v = attn.rearrange("(t p) f -> p t f", p=P)
        w_dram = [wq, wk, wv]
        b_dram = [bq, bk]

        def proj_no(g, n):
            return g * PER_GROUP + n

        FIRST = [(kind, c) for c in range(NCH) for kind in "qkv"]
        first_banks = [pj, st[0], st[1], st[2]]

        def xt_after(no):
            c, a = no // 3, no % 3
            if c == NCH - 1:
                return []
            return [[TPC * (c + 1), TPC * (c + 1) + 1], [TPC * (c + 1) + 2], [TPC * (c + 1) + 3]][a]

        block = ctx.enter_context(nc.Block())

        @block.sync
        def _(sp):
            def load_w(i, g):
                sp.dma_start(w_raw[i][:, :], w_dram[i][bass.ds(g, 1), :, :].rearrange("a p n -> (a p) n")) \
                    .then_inc(w_loaded[i], 16)
                if i < 2:
                    sp.dma_start(b_raw[i][:, :], b_dram[i][bass.ds(g, 1), :, :].rearrange("a p n -> (a p) n")) \
                        .then_inc(w_loaded[i], 16)

            def set_stack(j):
                for r, (a, b) in enumerate((("hi", "hi"), ("hi", "lo"), ("lo", "hi"))):
                    sp.dma_start(q_st[j][HD * r:HD * (r + 1), :], nat[0][a][HD * j:HD * (j + 1), :]) \
                        .then_inc(stack_set[j], 16)
                    sp.dma_start(k_st[j][HD * r:HD * (r + 1), :], nat[1][b][HD * j:HD * (j + 1), :]) \
                        .then_inc(stack_set[j], 16)

            def set_max_rows(no, j):
                sp.wait_ge(m_rows_set, no + 1)
                for part in range(2):
                    sp.dma_start(q_st[j][STK + part:STK + part + 1, :].rearrange("a (t p) -> a t p", p=P),
                                 m_rows[TT * part:TT * (part + 1), :]) \
                        .then_inc(m_in_stack, 16)

            def set_v(j):
                sp.dma_start(v_cur[:, j, :, :], v_next[:, j, :, :]).then_inc(v_set[j], 16)

            sp.dma_start(xin[:, 0, :], x_t[0]).then_inc(x_loaded[0], 16)
            load_w(0, 0)
            sp.dma_start(xin[:, 1, :], x_t[1]).then_inc(x_loaded[1], 16)
            load_w(1, 0)
            sp.dma_start(xin[:, 2, :], x_t[2]).then_inc(x_loaded[2], 16)
            load_w(2, 0)
            for t in range(3, TT):
                sp.wait_ge(x_normed, t - 2)
                sp.dma_start(xin[:, t % 3, :], x_t[t]).then_inc(x_loaded[t % 3], 16)
            for i in range(3):
                sp.wait_ge(w_lo[i], 1)
                load_w(i, 1)
            sp.wait_ge(proj_lo, PER_GROUP)
            for j in range(GH):
                set_stack(j)
            for j in range(GH):
                set_v(j)
            set_max_rows(0, 0)

            def group(g, more):
                def load_next(i):
                    sp.wait_ge(w_lo[i], g + 2)
                    load_w(i, g + 2)

                if more == 2:
                    load_next(0)
                set_max_rows(g * GH + 1, 1)
                if more == 2:
                    load_next(1)
                    load_next(2)
                set_max_rows(g * GH + 2, 2)
                if more:
                    sp.wait_ge(proj_lo, proj_no(g + 1, 2 * NCH))
                    set_stack(0)
                set_max_rows(g * GH + 3, 3)
                if more:
                    set_stack(1)
                    sp.wait_ge(st_psum, g * GB + 3 * NB)
                    set_stack(2)
                    set_max_rows(g * GH + 4, 0)
                    sp.wait_ge(proj_lo, proj_no(g + 2, 0))
                    for j in range(GH - 1):
                        set_v(j)
                    sp.wait_ge(st_psum, g * GB + 4 * NB)
                    set_stack(3)
                    sp.wait_ge(av_psum, g * GH * NCH + GH * NCH)
                    set_v(GH - 1)
                sp.wait_ge(o_done, g * GH * NCH + GH * NCH + 2)
                if more:
                    sp.dma_start(attn_v[:, :, bass.ds(g * P, P)], attn_g[:, :, :]).then_inc(attn_free, 16)
                else:
                    sp.dma_start(attn_v[:, :, g * P:(g + 1) * P], attn_g[:, :, :]).then_inc(attn_free, 16)

            with sp.Fori(0, NG - 2) as g:
                group(g, 2)
            group(NG - 2, 1)
            group(NG - 1, 0)
            sp.wait_ge(attn_free, 16 * NG + 16)

        @block.gpsimd
        def _(pool):
            n_step = [0]

            def step(ins):
                n_step[0] += 1
                ins.then_inc(pool_step, 1)
                pool.wait_ge(pool_step, n_step[0])

            for m in (ident, ident_h, ident_b):
                step(nc.gpsimd.memset(m[:, :], 0.0))
                step(nc.gpsimd.affine_select(out=m[:, :], in_=m[:, :], compare_op=ALU.not_equal, fill=1.0,
                                             base=0, pattern=[[-1, P]], channel_multiplier=1))
            for m, sign in ((mask_qk, 1), (mask_kq, -1)):
                step(nc.gpsimd.memset(m[:, :], 0.0))
                step(nc.gpsimd.affine_select(out=m[:, :], in_=m[:, :], compare_op=ALU.is_ge, fill=NEG,
                                             base=0, pattern=[[-sign, P]], channel_multiplier=sign))
            step(nc.gpsimd.memset(neg_half[:, :], -0.5))
            nc.gpsimd.memset(v_next[:, :, :, HD:HD + 1], 1.0).then_inc(consts, 1)
            for t in range(TT):
                b = t % 2
                pool.wait_ge(x_stats, t + 1)
                if t >= 2:
                    pool.wait_ge(x_normed, t - 1)
                step(nc.gpsimd.tensor_scalar(rs[:, b, 0:1], mv[:, b, 1:2], EPS, None, ALU.add))
                step(nc.gpsimd.tensor_tensor(rs[:, b, 1:2], rs[:, b, 0:1], neg_half[:, :], ALU.pow))
                step(nc.gpsimd.tensor_tensor(rs[:, b, 2:3], mv[:, b, 0:1], rs[:, b, 1:2], ALU.mult))
                nc.gpsimd.tensor_scalar(rs[:, b, 3:4], rs[:, b, 2:3], -1.0, None, ALU.mult).then_inc(x_rstd, 1)

            nc.gpsimd.sem_inc(o_done, 2)
            nc.gpsimd.sem_inc(attn_free, 16)

            def group(g):
                def low_part(s):
                    if hi_on_dve(s):
                        pool.wait_ge(hi_dve, g * count(hi_on_dve, GB - 1) + count(hi_on_dve, s))
                    else:
                        pool.wait_ge(hi_act, g * count(hi_on_act, GB - 1) + count(hi_on_act, s) + ST_BANKS)
                    wd = BLOCKS[s % NB][3]
                    r = s % RING
                    nc.gpsimd.tensor_tensor(p_lo[:, r, 0:wd], p32[:, r, 0:wd], p_hi[:, r, 0:wd],
                                            ALU.subtract).then_inc(lo_pool, 1)

                def output(c):
                    j, qc = c // NCH, c % NCH
                    no = g * GH * NCH + c
                    b = c % 2
                    pool.wait_ge(rd_set, no + 1)
                    if c == 0:
                        pool.wait_ge(attn_free, 16 * g + 16)
                    nc.gpsimd.tensor_tensor(o_sum[:, b, :, :], o_cp[:, b, :, 0:HD], o_cp[:, b, :, HD + 1:VW],
                                            ALU.add).then_inc(o_added, 1)
                    pool.wait_ge(o_added, no + 1)
                    rd = o_rd[:, b, :].rearrange("p (r a) -> p r a", a=1).broadcast_to([P, TPC, HD])
                    nc.gpsimd.tensor_tensor(attn_g[:, qc * TPC:(qc + 1) * TPC, j * HD:(j + 1) * HD],
                                            o_sum[:, b, :, :], rd, ALU.mult).then_inc(o_done, 1)

                for s in range(GB + 1):
                    if s and not lo_on_dve(s - 1):
                        low_part(s - 1)
                    for c in chunks_at(s, LAG + 3):
                        output(c)
                for c in chunks_after(LAG + 3, GB):
                    output(c)

            with pool.Fori(0, NG) as g:
                group(g)

        @block.scalar
        def _(act):
            def split_w(i, g):
                act.wait_ge(w_loaded[i], (g + 1) * (32 if i < 2 else 16))
                if not (isinstance(g, int) and g == 0):
                    act.wait_ge(proj_lo, proj_no(g, 0))
                nc.scalar.activation(w[i]["hi"][:, :, :].rearrange("p k n -> p (k n)"), w_raw[i][:, :],
                                     ACT.Copy, scale=WS).then_inc(w_hi[i], 1)
                if i < 2:
                    nc.scalar.activation(b_sc[i][:, :], b_raw[i][:, :], ACT.Copy, scale=WS).then_inc(w_hi[i], 1)

            def take_proj(kind, c, bank, no):
                act.wait_ge(proj_psum, no + 1)
                if kind == "v":
                    o = v_next[:, :, c * TPC:(c + 1) * TPC, 0:HD].rearrange("p j t f -> p t j f")
                    i_ = bank[:, :].rearrange("p (t j f) -> p t j f", t=TPC, j=GH)
                    nc.scalar.activation(o, i_, ACT.Copy).then_inc(proj_hi, 1)
                else:
                    i = "qk".index(kind)
                    nc.scalar.activation(nat[i]["hi"][:, c * CH:(c + 1) * CH], bank[:, :], ACT.Identity,
                                         bias=b_sc[i][:, 0:1]).then_inc(proj_hi, 1)

            act.wait_ge(consts, 1)

            def norm_tile(t):
                act.wait_ge(x_rstd, t + 1)
                if t >= 2:
                    act.wait_ge(xt_psum, t - 1)
                nc.scalar.activation(xn[:, t % 2, :], xin[:, t % 3, :], ACT.Identity, bias=rs[:, t % 2, 3:4],
                                     scale=rs[:, t % 2, 1:2]).then_inc(x_normed, 1)

            def take_xt(t):
                act.wait_ge(xt_psum, t + 1)
                for h in range(2):
                    bank = (mx, av)[t % 2][h]
                    ins = nc.scalar.activation(xt["hi"][:, 4 * h:4 * h + 4, t * P:(t + 1) * P],
                                               bank[:, :].rearrange("p (k n) -> p k n", k=4), ACT.Copy)
                ins.then_inc(xt_hi, 1)

            for i in range(3):
                if i == 0:
                    norm_tile(0)
                split_w(i, 0)
            for t in range(1, TPC + 1):
                norm_tile(t)
                take_xt(t - 1)
            for c in range(NCH):
                for a in range(3):
                    no = 3 * c + a
                    take_proj(*FIRST[no], first_banks[no % 4], no)
                    for t in xt_after(no):
                        if t + 1 < TT:
                            norm_tile(t + 1)
                        take_xt(t)

            def group(g, more):
                def exps(s):
                    wd = BLOCKS[s % NB][3]
                    r = s % RING
                    act.wait_ge(st_psum, g * GB + s + 1)
                    nc.scalar.activation(p32[:, r, 0:wd], st[s % ST_BANKS][:, 0:wd], ACT.Exp,
                                         scale=EXP_SCALE).then_inc(p32_set, 1)
                    if hi_on_act(s):
                        nc.scalar.activation(p_hi[:, r, 0:wd], st[s % ST_BANKS][:, 0:wd], ACT.Exp,
                                             scale=EXP_SCALE).then_inc(hi_act, 1)

                def copy_out(c):
                    no = g * GH * NCH + c
                    act.wait_ge(av_psum, no + 1)
                    act.wait_ge(o_done, no + 1)
                    nc.scalar.activation(o_cp[:, c % 2, :, :].rearrange("p t f -> p (t f)"),
                                         av[c % 2][:, 0:TPC * VW], ACT.Copy).then_inc(av_used, 1)

                for s in range(GB):
                    if more:
                        for i, at in SPLIT_AT.items():
                            if at == s:
                                split_w(i, g + 1)
                    exps(s)
                    if more:
                        for n, (kind, c, start, span) in enumerate(PROJ):
                            if start + span == s:
                                if (kind, c) in (("q", 0), ("v", 0)):
                                    for j in range(GH):
                                        act.wait_ge((v_set if kind == "v" else stack_set)[j],
                                                    (16 if kind == "v" else 96) * (g + 1))
                                take_proj(kind, c, pj, proj_no(g + 1, n))
                    for c in chunks_at(s, LAG + 1):
                        copy_out(c)
                for c in chunks_after(LAG + 1, GB - 1):
                    copy_out(c)

            nc.scalar.sem_inc(p32_set, ST_BANKS)
            nc.scalar.sem_inc(hi_act, ST_BANKS)
            nc.scalar.sem_inc(av_used, 2)
            with act.Fori(0, NG - 1) as g:
                group(g, True)
            group(NG - 1, False)

        @block.vector
        def _(dve):
            n_step = [0]

            def step(ins):
                n_step[0] += 1
                ins.then_inc(dve_step, 1)
                dve.wait_ge(dve_step, n_step[0])

            def split_w(i, g):
                dve.wait_ge(w_hi[i], (g + 1) * (2 if i < 2 else 1))
                nc.vector.scalar_tensor_tensor(out=w[i]["lo"][:, :, :].rearrange("p k n -> p (k n)"),
                                               in0=w_raw[i][:, :], scalar=WS,
                                               in1=w[i]["hi"][:, :, :].rearrange("p k n -> p (k n)"),
                                               op0=ALU.mult, op1=ALU.subtract).then_inc(w_lo[i], 1)

            def take_proj(kind, c, bank, no):
                dve.wait_ge(proj_hi, no + 1)
                if kind == "v":
                    o = v_next[:, :, c * TPC:(c + 1) * TPC, HD + 1:VW].rearrange("p j t f -> p t j f")
                    h = v_next[:, :, c * TPC:(c + 1) * TPC, 0:HD].rearrange("p j t f -> p t j f")
                    i_ = bank[:, :].rearrange("p (t j f) -> p t j f", t=TPC, j=GH)
                    nc.vector.tensor_tensor(o, i_, h, ALU.subtract).then_inc(proj_lo, 1)
                else:
                    i = "qk".index(kind)
                    nc.vector.scalar_tensor_tensor(out=nat[i]["lo"][:, c * CH:(c + 1) * CH], in0=bank[:, :],
                                                   scalar=b_sc[i][:, 0:1], in1=nat[i]["hi"][:, c * CH:(c + 1) * CH],
                                                   op0=ALU.add, op1=ALU.subtract).then_inc(proj_lo, 1)

            for j in range(GH):
                nc.vector.memset(q_st[j][STK:P, :], 0.0).then_inc(consts_dve, 1)
                nc.vector.memset(k_st[j][STK:P, :], MROW).then_inc(consts_dve, 1)
            step(nc.vector.memset(m_part[:, :, :], -3e38))

            def stats_tile(t):
                dve.wait_ge(x_loaded[t % 3], 16 * (t // 3 + 1))
                if t >= 2:
                    dve.wait_ge(x_rstd, t - 1)
                for h in range(2):
                    ins = nc.vector.bn_stats(stats[:, t % 2, h, :], xin[:, t % 3, h * CH:(h + 1) * CH])
                step(ins)
                nc.vector.bn_aggr(mv[:, t % 2, :], stats[:, t % 2, :, :].rearrange("p a b -> p (a b)")) \
                    .then_inc(x_stats, 1)

            def take_xt(t):
                dve.wait_ge(xt_hi, t + 1)
                for h in range(2):
                    bank = (mx, av)[t % 2][h]
                    ins = nc.vector.tensor_tensor(xt["lo"][:, 4 * h:4 * h + 4, t * P:(t + 1) * P],
                                                  bank[:, :].rearrange("p (k n) -> p k n", k=4),
                                                  xt["hi"][:, 4 * h:4 * h + 4, t * P:(t + 1) * P], ALU.subtract)
                ins.then_inc(xt_lo, 1)

            stats_tile(0)
            for i in range(3):
                split_w(i, 0)
            stats_tile(1)
            for t in range(TPC):
                stats_tile(t + 2)
                take_xt(t)
            for c in range(NCH):
                for a in range(3):
                    no = 3 * c + a
                    take_proj(*FIRST[no], first_banks[no % 4], no)
                    for t in xt_after(no):
                        if t + 2 < TT:
                            stats_tile(t + 2)
                        take_xt(t)

            def max_columns(no):
                dve.wait_ge(m_done, (no + 1) * len(MBLOCKS))
                nc.vector.tensor_reduce(m_all[:, :], m_part[:, :, :], AX.X, ALU.max).then_inc(m_chain, 1)
                dve.wait_ge(m_chain, 2 * no + 1)
                nc.vector.tensor_scalar(m_cols[:, 0:TT], m_all[:, :], -1.0 / MROW, None, ALU.mult).then_inc(m_chain, 1)
                dve.wait_ge(m_chain, 2 * no + 2)
                nc.vector.scalar_tensor_tensor(out=m_cols[:, TT:2 * TT], in0=m_all[:, :], scalar=-1.0 / MROW,
                                               in1=m_cols[:, 0:TT], op0=ALU.mult, op1=ALU.subtract) \
                    .then_inc(m_cols_set, 1)

            def head_max(n, i, use0, no):
                for a in max_blocks_at(i):
                    t, c, wd, _ = MBLOCKS[a]
                    dve.wait_ge(m_psum, use0 + a + 1)
                    nc.vector.tensor_reduce(m_part[:, t, c:c + 1], mx[(n + a) % 2][:, 0:wd], AX.X, ALU.max) \
                        .then_inc(m_done, 1)
                if i == MSPAN:
                    max_columns(no)
                if i == MSPAN + 1:
                    dve.wait_ge(m_psum, use0 + MR)
                    if not (isinstance(no, int) and no == 0):
                        dve.wait_ge(m_in_stack, 32 * no)
                    bank = mx[(n + MR - 1) % 2][0:2 * TT, 0:P // 2].bitcast(F16)
                    nc.vector.tensor_copy(m_rows[:, :], bank).then_inc(m_rows_set, 1)

            for i in range(MSPAN + 2):
                head_max(0, i, 0, 0)

            def group(g, more):
                def cast(s):
                    dve.wait_ge(p32_set, g * GB + s + 1 + ST_BANKS)
                    wd = BLOCKS[s % NB][3]
                    r = s % RING
                    nc.vector.tensor_copy(p_hi[:, r, 0:wd], p32[:, r, 0:wd]).then_inc(hi_dve, 1)

                def low_part(s):
                    dve.wait_ge(hi_act, g * count(hi_on_act, GB - 1) + count(hi_on_act, s) + ST_BANKS)
                    wd = BLOCKS[s % NB][3]
                    r = s % RING
                    nc.vector.tensor_tensor(p_lo[:, r, 0:wd], p32[:, r, 0:wd], p_hi[:, r, 0:wd],
                                            ALU.subtract).then_inc(lo_dve, 1)

                def reciprocal(c):
                    no = g * GH * NCH + c
                    dve.wait_ge(av_used, no + 1 + 2)
                    nc.vector.reciprocal(o_rd[:, c % 2, :], o_cp[:, c % 2, :, HD]).then_inc(rd_set, 1)

                for s in range(GB + 1):
                    j, i = s // NB, s % NB
                    if s < GB and more and s - 1 in SPLIT_AT.values():
                        split_w({v: k for k, v in SPLIT_AT.items()}[s - 1], g + 1)
                    if s < GB and (more or j < GH - 1):
                        head_max((j + 1) * MR, i, MR + g * GH * MR + j * MR, g * GH + j + 1)
                    if s and hi_on_dve(s - 1):
                        cast(s - 1)
                    if s and lo_on_dve(s - 1):
                        low_part(s - 1)
                    if more:
                        for n, (kind, c, start, span) in enumerate(PROJ):
                            if start + span + 1 == s:
                                take_proj(kind, c, pj, proj_no(g + 1, n))
                    for c in chunks_at(s, LAG + 2):
                        reciprocal(c)
                for c in chunks_after(LAG + 2, GB):
                    reciprocal(c)

            with dve.Fori(0, NG - 1) as g:
                group(g, True)
            group(NG - 1, False)

        @block.tensor
        def _(pe):
            def transpose_x(t):
                pe.wait_ge(x_normed, t + 1)
                if t >= 2:
                    pe.wait_ge(xt_lo, t - 1)
                for k in range(KC):
                    ins = nc.tensor.transpose((mx, av)[t % 2][k // 4][:, (k % 4) * P:(k % 4 + 1) * P],
                                              xn[:, t % 2, k * P:(k + 1) * P], ident[:, :])
                ins.then_inc(xt_psum, 1)

            def project(kind, c, bank, lo, hi):
                i = "qkv".index(kind)
                steps = steps_of(kind)
                for m in range(lo, min(hi, len(steps))):
                    r, (a, b), k = steps[m]
                    first, last = (a, b, k) == ("hi", "hi", 0), (a, b, k) == ("lo", "hi", KC - 1)
                    if kind == "v":
                        t = c * TPC + r
                        ins = nc.tensor.matmul(bank[:, r * P:(r + 1) * P], xt[a][:, k, t * P:(t + 1) * P],
                                               w[i][b][:, k, :], start=first, stop=last)
                    else:
                        ins = nc.tensor.matmul(bank[:, :], w[i][b][:, k, :], xt[a][:, k, c * CH:(c + 1) * CH],
                                               start=first, stop=last)
                    if m == len(steps) - 1:
                        ins.then_inc(proj_psum, 1)

            def head_max(n, i, j, no):
                for a in max_blocks_at(i):
                    t, c, wd, diagonal = MBLOCKS[a]
                    if a >= 2:
                        pe.wait_ge(m_done, no * len(MBLOCKS) + a - 1)
                    elif not (isinstance(no, int) and no == 0):
                        if a == 0:
                            pe.wait_ge(m_done, no * len(MBLOCKS))
                        else:
                            pe.wait_ge(m_rows_set, no)
                    bank = mx[(n + a) % 2]
                    ins = nc.tensor.matmul(bank[:, 0:wd], q_st[j][0:STK, t * P:(t + 1) * P],
                                           k_st[j][0:STK, c * CH:c * CH + wd], start=True, stop=not diagonal)
                    if diagonal:
                        ins = nc.tensor.matmul(bank[:, wd - P:wd], ident_b[:, :], mask_qk[:, :],
                                               start=False, stop=True)
                    ins.then_inc(m_psum, 1)
                if i == MSPAN + 1:
                    pe.wait_ge(m_cols_set, no + 1)
                    nc.tensor.transpose(mx[(n + MR - 1) % 2][0:2 * TT, 0:P // 2].bitcast(F16), m_cols[:, :],
                                        ident_h[:, :]).then_inc(m_psum, 1)

            pe.wait_ge(consts, 1)
            for t in range(TPC):
                transpose_x(t)
            for c in range(NCH):
                pe.wait_ge(xt_lo, TPC * (c + 1))
                for a in range(3):
                    no = 3 * c + a
                    kind, _ = FIRST[no]
                    if c == 0:
                        pe.wait_ge(w_lo[a], 1)
                    if no >= 4:
                        pe.wait_ge(proj_lo, no - 3)
                    project(kind, c, first_banks[no % 4], 0, 1 << 30)
                    for t in xt_after(no):
                        transpose_x(t)
            pe.wait_ge(proj_lo, PER_GROUP)
            pe.wait_ge(consts_dve, 2 * GH)
            pe.wait_ge(stack_set[0], 96)
            for i in range(MSPAN + 2):
                head_max(0, i, 0, 0)

            def group(g, more):
                def scores(s):
                    j, i = s // NB, s % NB
                    qc, kt, q0, wd, diagonal = BLOCKS[i]
                    if i == 0:
                        pe.wait_ge(m_in_stack, 32 * (g * GH + j + 1))
                    before = same_bank_before(s)
                    if hi_on_dve(before):
                        pe.wait_ge(p32_set, g * GB + before + 1 + ST_BANKS)
                    else:
                        pe.wait_ge(hi_act, g * count(hi_on_act, GB - 1) + count(hi_on_act, before) + ST_BANKS)
                    bank = st[s % ST_BANKS]
                    ins = nc.tensor.matmul(bank[:, 0:wd], k_st[j][0:ROWS, kt * P:(kt + 1) * P],
                                           q_st[j][0:ROWS, q0:q0 + wd], start=True, stop=not diagonal)
                    if diagonal:
                        ins = nc.tensor.matmul(bank[:, 0:P], ident_b[:, :], mask_kq[:, :], start=False, stop=True)
                    ins.then_inc(st_psum, 1)

                def values(s):
                    j, i = s // NB, s % NB
                    qc, kt, q0, wd, _ = BLOCKS[i]
                    r = s % RING
                    c = j * NCH + qc
                    if i == 0:
                        pe.wait_ge(v_set[j], 16 * (g + 1))
                    if kt == 0:
                        pe.wait_ge(av_used, g * GH * NCH + c + 1)
                    if lo_on_dve(s):
                        pe.wait_ge(lo_dve, g * count(lo_on_dve, GB - 1) + count(lo_on_dve, s))
                    else:
                        pe.wait_ge(lo_pool, g * count(lo_on_pool, GB - 1) + count(lo_on_pool, s))
                    first = True
                    for n in range(wd // P):
                        t = (q0 + n * P) // P - qc * TPC
                        o = av[c % 2][:, t * VW:(t + 1) * VW]
                        stop = kt == qc * TPC + t
                        nc.tensor.matmul(o, p_hi[:, r, n * P:(n + 1) * P], v_cur[:, j, kt, :],
                                         start=(kt == 0 and n == 0), stop=False, skip_group_check=True)
                        ins = nc.tensor.matmul(o[:, 0:HD + 1], p_lo[:, r, n * P:(n + 1) * P],
                                               v_cur[:, j, kt, 0:HD + 1], start=False, stop=stop,
                                               skip_group_check=True)
                    if s in ENDS:
                        ins.then_inc(av_psum, 1)

                for s in range(GB):
                    j, i = s // NB, s % NB
                    scores(s)
                    if more or j < GH - 1:
                        jn = (j + 1) % GH
                        if i == 0:
                            pe.wait_ge(stack_set[jn], 96 * (g + 1 if jn else g + 2))
                        head_max((j + 1) * MR, i, jn, g * GH + j + 1)
                    if more:
                        for n, (kind, c, start, span) in enumerate(PROJ):
                            if start <= s < start + span:
                                per = len(steps_of(kind)) // span
                                if s == start:
                                    pe.wait_ge(proj_lo, proj_no(g + 1, n))
                                    if c == 0:
                                        pe.wait_ge(w_lo["qkv".index(kind)], g + 2)
                                project(kind, c, pj, per * (s - start), per * (s - start + 1))
                    if s >= LAG:
                        values(s - LAG)
                for s in range(GB - LAG, GB):
                    values(s)

            with pe.Fori(0, NG - 1) as g:
                group(g, True)
            group(NG - 1, False)


W_AT = [2, 7, 12, 17]
W_BACK = 4
Z_LAG = 2
PAIR_USES = RC + FT + TPC
assert RC % 2 == FT % 2 == TPC % 2 == 0
PIECE = 1024


def weight_pieces(w, dram):
    out = []

    def add(name, index, src, shape):
        rows, k, n = shape
        out.append((w[name]["hi"][index], w[name]["lo"][index], src, k, n, rows))

    wo, u1, v1, u2, v2 = (dram[n] for n in ("wo", "u1", "v1", "u2", "v2"))
    for k in range(KC):
        add("wo", (slice(0, P), slice(k, k + 1), slice(0, D)),
            wo[k * P:(k + 1) * P, :].rearrange("(k p) n -> p k n", p=P), (P, 1, D))
    for k in range(0, KC, 4):
        add("u1", (slice(0, P), slice(k, k + 4), slice(0, RANK)),
            u1[k * P:(k + 4) * P, :].rearrange("(k p) n -> p k n", p=P), (P, 4, RANK))
    for at in range(0, INTER, PIECE // 2):
        n = min(PIECE // 2, INTER - at)
        for base in (0, INTER):
            add("v1", (slice(0, P), slice(0, RC), slice(base + at, base + at + n)),
                v1[:, base + at:base + at + n].rearrange("(k p) n -> p k n", p=P), (P, RC, n))
    for f in range(0, FT - 1, 4):
        n = min(4, FT - 1 - f)
        add("u2", (slice(0, P), slice(f, f + n), slice(0, RANK)),
            u2[f * P:(f + n) * P, :].rearrange("(k p) n -> p k n", p=P), (P, n, RANK))
    add("u2", (slice(0, FLAST), slice(FT - 1, FT), slice(0, RANK)),
        u2[(FT - 1) * P:INTER, :].rearrange("(k p) n -> p k n", p=FLAST), (FLAST, 1, RANK))
    for k in range(RC):
        add("v2", (slice(0, P), slice(k, k + 1), slice(0, D)),
            v2[k * P:(k + 1) * P, :].rearrange("(k p) n -> p k n", p=P), (P, 1, D))
    return out


def ffn_phase(nc, x, attn, dram, bv, bo, b1g, b1u, b2, x1, out):
    ctx = ExitStack()
    with ctx:
        def sb(name, shape, dt):
            return ctx.enter_context(nc.sbuf_tensor(name, shape, dt))

        def ps(name, shape, dt=F32):
            return ctx.enter_context(nc.psum_tensor(name, shape, dt))

        def sem(name):
            return ctx.enter_context(nc.semaphore(name))

        shapes = {"wo": [P, KC, D], "u1": [P, KC, RANK], "v1": [P, RC, 2 * INTER], "u2": [P, FT, RANK],
                  "v2": [P, RC, D]}
        w = {n: {h: sb(f"{n}_{h}", s, F16) for h in ("hi", "lo")} for n, s in shapes.items()}
        pieces = weight_pieces(w, dram)
        used = {"wo": KC, "u1": KC + 2}
        used["v1"] = used["u1"] + 2 * (-(-INTER // (PIECE // 2)))
        used["u2"] = used["v1"] + -(-(FT - 1) // 4) + 1
        used["v2"] = len(pieces)
        raw = sb("raw", [P, 2, PIECE], F32)
        ident2 = sb("ident2", [P, P], F32)
        neg_half2 = sb("neg_half2", [P, 1], F32)
        eps_c = sb("eps_c", [P, 1], F32)
        minus_one = sb("minus_one", [P, 1], F32)
        bv_b = sb("bv_b", [P, D], F32)
        bo_b = sb("bo_b", [P, D], F32)
        b2_b = sb("b2_b", [P, D], F32)
        b1g_c = sb("b1g_c", [P, FT], F32)
        b1u_c = sb("b1u_c", [P, FT], F32)
        at_in = sb("at_in", [P, 1, D], F32)
        at_t = {h: sb(f"at_{h}", [P, KC, P], F16) for h in ("hi", "lo")}
        x_in = sb("x_in", [P, D], F32)
        y = sb("y", [P, D], F32)
        xn1 = sb("xn1", [P, D], F32)
        x1t = {h: sb(f"x1t_{h}", [P, KC, CH], F16) for h in ("hi", "lo")}
        p1t = {h: sb(f"p1t_{h}", [P, RC, CH], F16) for h in ("hi", "lo")}
        sg = sb("sg", [P, 2, CH], F32)
        a32 = sb("a32", [P, 3, CH], F32)
        act_t = {h: sb(f"act_{h}", [P, 3, CH], F16) for h in ("hi", "lo")}
        zt = {h: sb(f"zt_{h}", [P, RC, CH], F16) for h in ("hi", "lo")}
        yo = sb("yo", [P, 2, D], F32)
        x1_in = sb("x1_in", [P, D], F32)
        ln = {n: [(sb(f"st_{n}{i}", [P, 2, 6], F32), sb(f"mv_{n}{i}", [P, 2], F32), sb(f"rs_{n}{i}", [P, 4], F32))
                  for i in range(2 if n == "out" else 1)] for n in ("y", "x1", "out")}

        pair = [[ps(f"pair{i}{h}", [P, CH]) for h in range(2)] for i in range(2)]
        wp = [ps(f"wp{h}", [P, CH]) for h in range(2)]
        zp = [ps(f"zp{r}", [P, CH]) for r in range(RC)]

        pool_chain = sem("pool_chain")
        biases = sem("biases")
        bias_scaled = sem("bias_scaled")
        raw_loaded = [sem(f"raw_loaded{i}") for i in range(2)]
        piece_hi = sem("piece_hi")
        piece_lo = sem("piece_lo")
        attn_loaded = sem("attn_loaded")
        attn_biased = sem("attn_biased")
        x_loaded2 = sem("x_loaded2")
        w_psum = sem("w_psum")
        w_used = sem("w_used")
        at_hi = sem("at_hi")
        ln_stats = {n: sem(f"ln_stats_{n}") for n in ln}
        wait_carrier = sem("wait_carrier")
        ln_chain = {n: sem(f"ln_chain_{n}") for n in ln}
        ln_rstd = {n: sem(f"ln_rstd_{n}") for n in ln}
        y_normed = sem("y_normed")
        x1_set = sem("x1_set")
        x1_stored = sem("x1_stored")
        x1_normed = sem("x1_normed")
        x1t_hi = sem("x1t_hi")
        pair_psum = sem("pair_psum")
        p1_lo = sem("p1_lo")
        out_taken = sem("out_taken")
        p1_hi = sem("p1_hi")
        sg_set = sem("sg_set")
        a32_set = sem("a32_set")
        act_hi_set = sem("act_hi_set")
        act_lo_set = sem("act_lo_set")
        z_psum = sem("z_psum")
        z_hi = sem("z_hi")
        z_lo = sem("z_lo")
        yo_normed = sem("yo_normed")
        x1_loaded = sem("x1_loaded")
        out_set = sem("out_set")
        out_stored = [sem(f"out_stored{i}") for i in range(2)]

        def w_use(t, i):
            return 3 * t + i

        def rows(t):
            return (bass.ds(t * P, P), slice(0, D))

        def inner(f):
            return FLAST if f == FT - 1 else P

        def w_steps(f):
            found = []
            for r, at in enumerate(W_AT):
                for stage, off in (("turn", 0), ("project", 1), ("norm", 2), ("back", W_BACK)):
                    if f == at + off:
                        found.append((r, stage))
            return found

        W_STAGES = ("turn", "project", "norm", "back")

        block = ctx.enter_context(nc.Block())

        @block.sync
        def _(sp):
            for b, src in ((bv_b, bv), (bo_b, bo), (b2_b, b2)):
                sp.dma_start(b[:, :], src.broadcast_to([P, D])).then_inc(biases, 16)
            sp.dma_start(b1g_c[:, :], b1g).then_inc(biases, 16)
            sp.dma_start(b1u_c[:, :], b1u).then_inc(biases, 16)

            def load_piece(n):
                hi, lo, src, k, cols, rws = pieces[n]
                if n >= 2:
                    sp.wait_ge(piece_lo, n - 1)
                sp.dma_start(raw[0:rws, n % 2, 0:k * cols].rearrange("p (k n) -> p k n", k=k), src) \
                    .then_inc(raw_loaded[n % 2], 16)

            def load_tile(t, first=False):
                if not first:
                    sp.wait_ge(w_psum, w_use(t, 0) - 2)
                sp.dma_start(at_in[:, 0, :], attn[rows(t)]).then_inc(attn_loaded, 16)
                if not first:
                    sp.wait_ge(x1_set, t)
                sp.dma_start(x_in[:, :], x[rows(t)]).then_inc(x_loaded2, 16)

            def store_x1(t):
                sp.wait_ge(x1_set, t + 1)
                sp.dma_start(x1[rows(t)], y[:, :]).then_inc(x1_stored, 16)

            load_tile(0, first=True)
            order = iter(range(len(pieces)))
            for n in order:
                load_piece(n)
                if n == used["wo"] - 1:
                    break
            for t in range(TPC):
                if t:
                    load_tile(t)
                for _, n in zip(range(6), order):
                    load_piece(n)
                store_x1(t)
            for n in order:
                load_piece(n)

            def chunk(c, more):
                if more:
                    for r in range(TPC):
                        load_tile((c + 1) * TPC + r)
                        store_x1((c + 1) * TPC + r)
                sp.wait_ge(x1_stored, 16 * TPC * (c + 1))
                for r in range(TPC):
                    finish_tile(c, r)

            def finish_tile(c, r):
                t = c * TPC + r
                sp.wait_ge(out_set, t + 1)
                sp.dma_start(x1_in[:, :], x1[rows(t)]).then_inc(x1_loaded, 16)
                sp.wait_ge(out_set, t + 2)
                sp.dma_start(out[rows(t)], yo[:, r % 2, :]).then_inc(out_stored[r % 2], 16)

            with sp.Fori(0, NCH - 1) as c:
                chunk(c, True)
            chunk(NCH - 1, False)
            for i in range(2):
                sp.wait_ge(out_stored[i], 16 * (TT // 2) + 16)

        @block.gpsimd
        def _(pool):
            nc.gpsimd.memset(ident2[:, :], 0.0).then_inc(pool_chain, 1)
            pool.wait_ge(pool_chain, 1)
            nc.gpsimd.affine_select(out=ident2[:, :], in_=ident2[:, :], compare_op=ALU.not_equal, fill=1.0,
                                    base=0, pattern=[[-1, P]], channel_multiplier=1).then_inc(pool_chain, 1)
            for c, value in ((neg_half2, -0.5), (eps_c, EPS), (minus_one, -1.0)):
                nc.gpsimd.memset(c[:, :], value).then_inc(pool_chain, 1)
            pool.wait_ge(pool_chain, 5)
            nc.gpsimd.sem_inc(out_set, 1)
            for i in range(2):
                nc.gpsimd.sem_inc(out_stored[i], 16)
            pool.wait_ge(bias_scaled, 1)

            def bias_tile(t):
                pool.wait_ge(attn_loaded, 16 * (t + 1))
                nc.gpsimd.tensor_tensor(at_in[:, 0, :], at_in[:, 0, :], bv_b[:, :], ALU.add) \
                    .then_inc(attn_biased, 1)

            def rstd(n, t, b=0):
                _, mv, rs = ln[n][b]
                s = ln_rstd[n]
                pool.wait_ge(ln_stats[n], t + 1)
                nc.gpsimd.tensor_tensor(rs[:, 0:1], mv[:, 1:2], eps_c[:, :], ALU.add).then_inc(s, 1)
                pool.wait_ge(s, 4 * t + 1)
                nc.gpsimd.tensor_tensor(rs[:, 1:2], rs[:, 0:1], neg_half2[:, :], ALU.pow).then_inc(s, 1)
                pool.wait_ge(s, 4 * t + 2)
                nc.gpsimd.tensor_tensor(rs[:, 2:3], mv[:, 0:1], rs[:, 1:2], ALU.mult).then_inc(s, 1)
                pool.wait_ge(s, 4 * t + 3)
                nc.gpsimd.tensor_tensor(rs[:, 3:4], rs[:, 2:3], minus_one[:, :], ALU.mult).then_inc(s, 1)

            def stage(t, name):
                if name == "turn":
                    bias_tile(t)
                if name == "norm":
                    rstd("y", t)
                    rstd("x1", t)

            for t in range(TPC):
                for name in W_STAGES:
                    stage(t, name)

            def chunk(c, more):
                if more:
                    for f in range(FT):
                        for r, name in w_steps(f):
                            stage((c + 1) * TPC + r, name)
                for r in range(TPC):
                    t = c * TPC + r
                    rstd("out", t, r % 2)
                    pool.wait_ge(yo_normed, t + 1)
                    pool.wait_ge(x1_loaded, 16 * (t + 1))
                    nc.gpsimd.tensor_tensor(yo[:, r % 2, :], yo[:, r % 2, :], x1_in[:, :], ALU.add) \
                        .then_inc(out_set, 1)

            with pool.Fori(0, NCH - 1) as c:
                chunk(c, True)
            chunk(NCH - 1, False)

        @block.scalar
        def _(act):
            act.wait_ge(biases, 16 * 5)
            nc.scalar.activation(bv_b[:, :], bv_b[:, :], ACT.Copy, scale=WS).then_inc(bias_scaled, 1)
            nc.scalar.activation(b1u_c[:, :], b1u_c[:, :], ACT.Copy, scale=WS * WS).then_inc(bias_scaled, 1)

            def split(n):
                hi, _, _, k, cols, rws = pieces[n]
                act.wait_ge(raw_loaded[n % 2], 16 * (n // 2 + 1))
                nc.scalar.activation(hi, raw[0:rws, n % 2, 0:k * cols].rearrange("p (k n) -> p k n", k=k),
                                     ACT.Copy, scale=WS).then_inc(piece_hi, 1)

            def stage(t, r, name):
                if name in ("turn", "back"):
                    act.wait_ge(w_psum, w_use(t, 0 if name == "turn" else 2) + 1)
                    dst, s = (at_t["hi"], at_hi) if name == "turn" else (x1t["hi"], x1t_hi)
                    cols = slice(0, P) if name == "turn" else slice(r * P, (r + 1) * P)
                    for h in range(2):
                        nc.scalar.activation(dst[:, 4 * h:4 * h + 4, cols],
                                             wp[h][:, :].rearrange("p (k n) -> p k n", k=4),
                                             ACT.Copy).then_inc(s, 1)
                if name == "norm":
                    act.wait_ge(ln_rstd["y"], 4 * t + 4)
                    nc.scalar.activation(y[:, :], y[:, :], ACT.Identity, bias=ln["y"][0][2][:, 3:4],
                                         scale=ln["y"][0][2][:, 1:2]).then_inc(y_normed, 1)
                    act.wait_ge(ln_rstd["x1"], 4 * t + 4)
                    nc.scalar.activation(xn1[:, :], y[:, :], ACT.Identity, bias=ln["x1"][0][2][:, 3:4],
                                         scale=ln["x1"][0][2][:, 1:2]).then_inc(x1_normed, 1)

            order = iter(range(len(pieces)))
            for _, n in zip(range(used["wo"]), order):
                split(n)
            for t in range(TPC):
                for i, name in enumerate(W_STAGES):
                    stage(t, t, name)
                    if i == 1:
                        for _, n in zip(range(6), order):
                            split(n)
            for n in order:
                split(n)

            def chunk(c, more):
                for r in range(RC):
                    act.wait_ge(pair_psum, PAIR_USES * c + r + 1)
                    nc.scalar.activation(p1t["hi"][:, r, :], pair[r][0][:, :], ACT.Copy).then_inc(p1_hi, 1)

                def high(f):
                    act.wait_ge(a32_set, FT * c + f + 1)
                    m = inner(f)
                    nc.scalar.activation(act_t["hi"][0:m, f % 3, :], a32[0:m, f % 3, :], ACT.Copy,
                                         scale=1.0 / WS).then_inc(act_hi_set, 1)

                for f in range(FT):
                    m = inner(f)
                    act.wait_ge(pair_psum, PAIR_USES * c + RC + f + 1)
                    nc.scalar.activation(sg[0:m, f % 2, :], pair[f % 2][0][0:m, :], ACT.Silu,
                                         bias=b1g_c[0:m, f:f + 1], scale=1.0 / (WS * WS)).then_inc(sg_set, 1)
                    if f:
                        high(f - 1)
                    if more:
                        for r, name in w_steps(f):
                            stage((c + 1) * TPC + r, r, name)
                high(FT - 1)
                act.wait_ge(z_psum, c + 1)
                for r in range(RC):
                    nc.scalar.activation(zt["hi"][:, r, :], zp[r][:, :], ACT.Copy, scale=1.0 / WS).then_inc(z_hi, 1)
                for r in range(TPC):
                    act.wait_ge(ln_rstd["out"], 4 * (c * TPC + r) + 4)
                    nc.scalar.activation(yo[:, r % 2, :], yo[:, r % 2, :], ACT.Identity,
                                         bias=ln["out"][r % 2][2][:, 3:4], scale=ln["out"][r % 2][2][:, 1:2]) \
                        .then_inc(yo_normed, 1)

            with act.Fori(0, NCH - 1) as c:
                chunk(c, True)
            chunk(NCH - 1, False)

        @block.vector
        def _(dve):
            nc.vector.sem_inc(out_taken, TPC)
            dve.wait_ge(bias_scaled, 2)

            def split(n):
                hi, lo, _, k, cols, rws = pieces[n]
                dve.wait_ge(piece_hi, n + 1)
                nc.vector.scalar_tensor_tensor(
                    out=lo, in0=raw[0:rws, n % 2, 0:k * cols].rearrange("p (k n) -> p k n", k=k), scalar=WS,
                    in1=hi, op0=ALU.mult, op1=ALU.subtract).then_inc(piece_lo, 1)

            def evacuate(banks, dst, bias, s):
                for h in range(2):
                    ins = nc.vector.scalar_tensor_tensor(
                        out=dst[:, h * CH:(h + 1) * CH], in0=banks[h][:, :], scalar=1.0 / (WS * WS),
                        in1=bias[:, h * CH:(h + 1) * CH], op0=ALU.mult, op1=ALU.add)
                ins.then_inc(s, 1)

            def statistics(n, t, src, b=0):
                stt, mv, _ = ln[n][b]
                for h in range(2):
                    ins = nc.vector.bn_stats(stt[:, h, :], src[:, h * CH:(h + 1) * CH])
                ins.then_inc(ln_chain[n], 1)
                dve.wait_ge(ln_chain[n], t + 1)
                nc.vector.sem_inc(wait_carrier, 1)
                nc.vector.bn_aggr(mv[:, :], stt[:, :, :].rearrange("p a b -> p (a b)")).then_inc(ln_stats[n], 1)

            def stage(t, r, name):
                if name in ("turn", "back"):
                    dst, s = (at_t, at_hi) if name == "turn" else (x1t, x1t_hi)
                    cols = slice(0, P) if name == "turn" else slice(r * P, (r + 1) * P)
                    for h in range(2):
                        dve.wait_ge(s, 2 * t + h + 1)
                        ins = nc.vector.tensor_tensor(dst["lo"][:, 4 * h:4 * h + 4, cols],
                                                      wp[h][:, :].rearrange("p (k n) -> p k n", k=4),
                                                      dst["hi"][:, 4 * h:4 * h + 4, cols], ALU.subtract)
                    ins.then_inc(w_used, 1)
                if name == "norm":
                    dve.wait_ge(w_psum, w_use(t, 1) + 1)
                    if not (isinstance(t, int) and t == 0):
                        dve.wait_ge(x1_normed, t)
                        dve.wait_ge(x1_stored, 16 * t)
                    evacuate(wp, y, bo_b, w_used)
                    dve.wait_ge(w_used, w_use(t, 1) + 1)
                    statistics("y", t, y)
                    dve.wait_ge(y_normed, t + 1)
                    dve.wait_ge(x_loaded2, 16 * (t + 1))
                    nc.vector.tensor_tensor(y[:, :], y[:, :], x_in[:, :], ALU.add).then_inc(x1_set, 1)
                    dve.wait_ge(x1_set, t + 1)
                    statistics("x1", t, y)

            order = iter(range(len(pieces)))
            for _, n in zip(range(used["wo"]), order):
                split(n)
            for t in range(TPC):
                for i, name in enumerate(W_STAGES):
                    stage(t, t, name)
                    if i == 1:
                        for _, n in zip(range(6), order):
                            split(n)
            for n in order:
                split(n)

            def chunk(c, more):
                for r in range(RC):
                    dve.wait_ge(p1_hi, RC * c + r + 1)
                    nc.vector.tensor_tensor(p1t["lo"][:, r, :], pair[r][0][:, :], p1t["hi"][:, r, :],
                                            ALU.subtract).then_inc(p1_lo, 1)

                def low(f):
                    dve.wait_ge(act_hi_set, FT * c + f + 1)
                    m = inner(f)
                    nc.vector.scalar_tensor_tensor(out=act_t["lo"][0:m, f % 3, :], in0=a32[0:m, f % 3, :],
                                                   scalar=1.0 / WS, in1=act_t["hi"][0:m, f % 3, :],
                                                   op0=ALU.mult, op1=ALU.subtract).then_inc(act_lo_set, 1)

                for f in range(FT):
                    m = inner(f)
                    dve.wait_ge(sg_set, FT * c + f + 1)
                    nc.vector.scalar_tensor_tensor(out=a32[0:m, f % 3, :], in0=pair[f % 2][1][0:m, :],
                                                   scalar=b1u_c[0:m, f:f + 1], in1=sg[0:m, f % 2, :],
                                                   op0=ALU.add, op1=ALU.mult).then_inc(a32_set, 1)
                    if f:
                        low(f - 1)
                    if more:
                        for r, name in w_steps(f):
                            stage((c + 1) * TPC + r, r, name)
                low(FT - 1)
                for r in range(RC):
                    dve.wait_ge(z_hi, RC * c + r + 1)
                    nc.vector.scalar_tensor_tensor(out=zt["lo"][:, r, :], in0=zp[r][:, :], scalar=1.0 / WS,
                                                   in1=zt["hi"][:, r, :], op0=ALU.mult,
                                                   op1=ALU.subtract).then_inc(z_lo, 1)
                for r in range(TPC):
                    t = c * TPC + r
                    dve.wait_ge(pair_psum, PAIR_USES * c + RC + FT + r + 1)
                    dve.wait_ge(out_stored[r % 2], 16 * (c * (TPC // 2) + r // 2) + 16)
                    evacuate(pair[r % 2], yo[:, r % 2, :], b2_b, out_taken)
                    dve.wait_ge(out_taken, t + 1 + TPC)
                    statistics("out", t, yo[:, r % 2, :], r % 2)

            with dve.Fori(0, NCH - 1) as c:
                chunk(c, True)
            chunk(NCH - 1, False)

        @block.tensor
        def _(pe):
            pe.wait_ge(pool_chain, 2)
            parts = [("hi", "hi"), ("hi", "lo"), ("lo", "hi")]

            def stage(t, r, name):
                if name == "norm":
                    return
                use = w_use(t, ("turn", "project", "back").index(name))
                if not (isinstance(use, int) and use == 0):
                    pe.wait_ge(w_used, use)
                if name == "project":
                    pe.wait_ge(piece_lo, used["wo"])
                    for h in range(2):
                        for a, b in parts:
                            for k in range(KC):
                                ins = nc.tensor.matmul(wp[h][:, :], at_t[a][:, k, :],
                                                       w["wo"][b][:, k, h * CH:(h + 1) * CH],
                                                       start=(a, b, k) == ("hi", "hi", 0),
                                                       stop=(a, b, k) == ("lo", "hi", KC - 1))
                else:
                    src = at_in[:, 0, :] if name == "turn" else xn1[:, :]
                    if name == "turn":
                        pe.wait_ge(attn_biased, t + 1)
                    else:
                        pe.wait_ge(x1_normed, t + 1)
                    for k in range(KC):
                        ins = nc.tensor.transpose(wp[k // 4][:, (k % 4) * P:(k % 4 + 1) * P],
                                                  src[:, k * P:(k + 1) * P], ident2[:, :])
                ins.then_inc(w_psum, 1)

            for t in range(TPC):
                for name in W_STAGES:
                    stage(t, t, name)

            def chunk(c, more):
                pe.wait_ge(w_used, w_use((c + 1) * TPC, 0))
                pe.wait_ge(piece_lo, used["u1"])
                for r in range(RC):
                    pe.wait_ge(out_taken, TPC * c + RC + r + 1)
                    for a, b in parts:
                        for k in range(KC):
                            ins = nc.tensor.matmul(pair[r][0][:, :], w["u1"][b][:, k, r * P:(r + 1) * P],
                                                   x1t[a][:, k, :], start=(a, b, k) == ("hi", "hi", 0),
                                                   stop=(a, b, k) == ("lo", "hi", KC - 1))
                    ins.then_inc(pair_psum, 1)
                pe.wait_ge(p1_lo, RC * (c + 1))

                def gate_up(f):
                    m = inner(f)
                    if f >= 2:
                        pe.wait_ge(a32_set, FT * c + f - 1)
                    pe.wait_ge(piece_lo, used["u1"] + 2 * ((f * P + m - 1) // (PIECE // 2) + 1))
                    for i, base in enumerate((0, INTER)):
                        for a, b in parts:
                            for k in range(RC):
                                ins = nc.tensor.matmul(pair[f % 2][i][0:m, :],
                                                       w["v1"][b][:, k, base + f * P:base + f * P + m],
                                                       p1t[a][:, k, :], start=(a, b, k) == ("hi", "hi", 0),
                                                       stop=(a, b, k) == ("lo", "hi", RC - 1))
                    ins.then_inc(pair_psum, 1)

                def down(f):
                    m = inner(f)
                    if f == 0:
                        pe.wait_ge(piece_lo, used["u2"])
                    pe.wait_ge(act_lo_set, FT * c + f + 1)
                    for r in range(RC):
                        for a, b in parts:
                            ins = nc.tensor.matmul(zp[r][:, :], w["u2"][b][0:m, f, r * P:(r + 1) * P],
                                                   act_t[a][0:m, f % 3, :], start=f == 0 and (a, b) == parts[0],
                                                   stop=f == FT - 1 and (a, b) == parts[-1])
                    if f == FT - 1:
                        ins.then_inc(z_psum, 1)

                for f in range(FT):
                    gate_up(f)
                    if f >= Z_LAG:
                        down(f - Z_LAG)
                    if more:
                        for r, name in w_steps(f):
                            stage((c + 1) * TPC + r, r, name)
                for f in range(FT - Z_LAG, FT):
                    down(f)
                pe.wait_ge(z_lo, RC * (c + 1))
                pe.wait_ge(piece_lo, used["v2"])
                for r in range(TPC):
                    if r < 2:
                        pe.wait_ge(a32_set, FT * c + FT - 1 + r)
                    else:
                        pe.wait_ge(out_taken, TPC * c + r - 1 + TPC)
                    for h in range(2):
                        for a, b in parts:
                            for k in range(RC):
                                ins = nc.tensor.matmul(pair[r % 2][h][:, :], zt[a][:, k, r * P:(r + 1) * P],
                                                       w["v2"][b][:, k, h * CH:(h + 1) * CH],
                                                       start=(a, b, k) == ("hi", "hi", 0),
                                                       stop=(a, b, k) == ("lo", "hi", RC - 1))
                    ins.then_inc(pair_psum, 1)

            with pe.Fori(0, NCH - 1) as c:
                chunk(c, True)
            chunk(NCH - 1, False)


def block_kernel(nc, x, wq, bq, wk, bk, wv, bv, wo, bo, u1, v1, u2, v2, b1g, b1u, b2, out):
    attn = nc.dram_tensor("attn_scratch", (S, D), F32).ap()
    x1 = nc.dram_tensor("x1_scratch", (S, D), F32).ap()
    attention_phase(nc, x, wq, wk, wv, bq, bk, attn)
    ffn_phase(nc, x, attn, {"wo": wo, "u1": u1, "v1": v1, "u2": u2, "v2": v2}, bv, bo, b1g, b1u, b2, x1, out)


def kernel(L0_attn_x, L0_attn_Wq, L0_attn_bq, L0_attn_Wk, L0_attn_bk, L0_attn_Wv, L0_attn_bv, L0_attn_Wo,
           L0_attn_bo, L0_ffn_U1, L0_ffn_V1, L0_ffn_U2, L0_ffn_V2, L0_ffn_b1, L0_ffn_b2):
    import numpy as np
    import concourse.bacc as bacc
    from concourse.bass_utils import run_bass_kernel_spmd

    def by_group(w):
        w = np.asarray(w).T.reshape(KC, P, NG, P)
        return np.ascontiguousarray(w.transpose(2, 1, 0, 3).reshape(NG, P, KC * P))

    def columns(b):
        padded = np.zeros(FT * P, b.dtype)
        padded[:INTER] = b
        return np.ascontiguousarray(padded.reshape(FT, P).T)

    b1 = np.asarray(L0_ffn_b1)
    arrays = {
        "x": np.asarray(L0_attn_x).reshape(S, D),
        "wq": by_group(L0_attn_Wq), "bq": np.asarray(L0_attn_bq).reshape(NG, P, 1),
        "wk": by_group(L0_attn_Wk), "bk": np.asarray(L0_attn_bk).reshape(NG, P, 1),
        "wv": by_group(L0_attn_Wv), "bv": np.asarray(L0_attn_bv).reshape(1, D),
        "wo": np.ascontiguousarray(np.asarray(L0_attn_Wo).T), "bo": np.asarray(L0_attn_bo).reshape(1, D),
        "u1": np.asarray(L0_ffn_U1), "v1": np.asarray(L0_ffn_V1),
        "u2": np.asarray(L0_ffn_U2), "v2": np.asarray(L0_ffn_V2),
        "b1g": columns(b1[:INTER]), "b1u": columns(b1[INTER:]), "b2": np.asarray(L0_ffn_b2).reshape(1, D),
    }
    arrays = {n: np.ascontiguousarray(a) for n, a in arrays.items()}
    nc = bacc.Bacc("TRN2", target_bir_lowering=False, num_devices=1)
    args = {n: nc.dram_tensor(f"in_{n}", a.shape, mybir.dt.from_np(a.dtype), kind="ExternalInput").ap()
            for n, a in arrays.items()}
    out = nc.dram_tensor("out", (S, D), F32, kind="ExternalOutput").ap()
    block_kernel(nc, **args, out=out)
    r = run_bass_kernel_spmd(nc, [{f"in_{n}": a for n, a in arrays.items()}], core_ids=[0])
    return r.results[0]["out"].reshape(1, S, D)
```

```python
from contextlib import ExitStack

import concourse.bass as bass
from concourse import mybir

F32 = mybir.dt.float32
F16 = mybir.dt.float16
BF16 = mybir.dt.bfloat16
ALU = mybir.AluOpType
ACT = mybir.ActivationFunctionType
AX = mybir.AxisListType

P = 128
S = 2048
D = 1024
NH = 32
HD = D // NH
GH = P // HD
NG = NH // GH
KC = D // P
TT = S // P
CH = 512
NCH = S // CH
TPC = CH // P
RANK = 256
RC = RANK // P
INTER = 2752
FT = -(-INTER // P)
FLAST = INTER - (FT - 1) * P
EPS = 1e-5

WS = 16.0
MROW = 2048.0
EXP_SCALE = 1.0 / (WS * WS * HD ** 0.5)
NEG = -1e30

VW = 2 * HD + 1
STK = 3 * HD
ROWS = STK + 2

BLOCKS = []
for qc in range(NCH):
    for kt in range(TPC * (qc + 1)):
        q0 = max(CH * qc, P * kt)
        BLOCKS.append((qc, kt, q0, CH * (qc + 1) - q0, kt >= TPC * qc))
NB = len(BLOCKS)
GB = GH * NB
MBLOCKS = [(t, c, min(CH, (t + 1) * P - c * CH), c == t // TPC) for t in range(TT) for c in range(t // TPC + 1)]
MR = len(MBLOCKS) + 1
MSPAN = 36
LAG = 5
RING = 8
ST_BANKS = 3
MX_BANKS = 3

QK_START, QK_EVERY, QK_SPAN = 6, 13, 8
V_START, V_EVERY, V_SPAN = 112, 12, 8
PER_GROUP = 2 * NCH + NCH
SPLIT_AT = {0: 0, 1: 30, 2: 60}


def hi_on_dve(s):
    return s % 4 == 1


def hi_on_act(s):
    return not hi_on_dve(s)


def lo_on_dve(s):
    return s % 4 == 3


def lo_on_pool(s):
    return not lo_on_dve(s)


def count(which, s):
    per = sum(map(which, range(GB)))
    return per * (s // GB) + sum(map(which, range(s % GB + 1)))


def same_bank_before(s, banks, uses):
    return s - banks if s >= banks else max(x for x in range(uses) if x % banks == s % banks) - uses


def early_at(n):
    return 4 + 7 * n


def max_blocks_at(i):
    return [a for a in range(len(MBLOCKS)) if a * MSPAN // len(MBLOCKS) == i]


def projections():
    out = [("qk"[n // NCH], n % NCH, QK_START + QK_EVERY * n, QK_SPAN) for n in range(2 * NCH)]
    return out + [("v", n, V_START + V_EVERY * n, V_SPAN) for n in range(NCH)]


PROJ = projections()

ENDS = [NB * j + max(i for i, bl in enumerate(BLOCKS) if bl[0] == qc) for j in range(GH) for qc in range(NCH)]


def values_at(s):
    at = [v + LAG + (BLOCKS[v % NB][1] == 0) for v in range(GB)]
    return [v for v in range(GB) if at[v] == s or (s == GB and at[v] > s)]


def chunks_at(s, delay):
    return [c for c, e in enumerate(ENDS) if e + delay == s]


def chunks_after(delay, last):
    return [c for c, e in enumerate(ENDS) if e + delay > last]


def steps_of(kind):
    parts = [("hi", "hi"), ("hi", "lo"), ("lo", "hi")]
    if kind == "v":
        return [(r, p, k) for r in range(TPC) for p in parts for k in range(KC)]
    return [(None, p, k) for p in parts for k in range(KC)]


def attention_phase(nc, shared, vectors, x, wq, wk, wv, bq, bk, attn, later, later_biases):
    ctx = ExitStack()
    with ctx:
        def sb(name, shape, dt):
            return ctx.enter_context(nc.sbuf_tensor(name, shape, dt))

        def ps(name, shape, dt=F32):
            return ctx.enter_context(nc.psum_tensor(name, shape, dt))

        def sem(name):
            return ctx.enter_context(nc.semaphore(name))

        ident = sb("ident", [P, P], F32)
        ident_h = sb("ident_h", [P, P], F16)
        ident_b = sb("ident_b", [P, P], BF16)
        mask_qk = sb("mask_qk", [P, P], BF16)
        mask_kq = sb("mask_kq", [P, P], BF16)
        neg_half = sb("neg_half", [P, 1], F32)
        xt = {h: shared[:, n * KC * S:(n + 1) * KC * S].rearrange("p (k n) -> p k n", k=KC)
              for n, h in enumerate(("hi", "lo"))}
        stats = sb("stats", [P, 2, 2, 6], F32)
        mv = sb("mv", [P, 2, 2], F32)
        rs = sb("rs", [P, 2, 4], F32)
        w_raw = [sb(f"w_raw{i}", [P, KC * P], F32) for i in range(3)]
        w_all = vectors[:, :].bitcast(F16).rearrange("p (i h k n) -> p i h k n", i=3, h=2, k=KC)
        w = [{h: w_all[:, i, n, :, :] for n, h in enumerate(("hi", "lo"))} for i in range(3)]
        b_raw = [sb(f"b_raw{i}", [P, 1], F32) for i in range(2)]
        b_sc = [sb(f"b_sc{i}", [P, 1], F32) for i in range(2)]
        nat = [{h: sb(f"nat_{h}{i}", [P, S], F16) for h in ("hi", "lo")} for i in range(2)]
        q_st = [sb(f"q_st{j}", [P, S], F16) for j in range(GH)]
        k_st = [sb(f"k_st{j}", [P, S], F16) for j in range(GH)]
        v_next = sb("v_next", [P, GH, TT, VW], F16)
        v_cur = sb("v_cur", [P, GH, TT, VW], F16)
        p32 = sb("p32", [P, RING, CH], F32)
        p_hi = sb("p_hi", [P, RING, CH], F16)
        p_lo = sb("p_lo", [P, RING, CH], F16)
        m_part = sb("m_part", [P, TT, NCH], F32)
        m_all = sb("m_all", [P, TT], F32)
        m_cols = sb("m_cols", [P, 2 * TT], F16)
        m_rows = sb("m_rows", [2 * TT, P], F16)
        o_cp = sb("o_cp", [P, 2, TPC, VW], F32)
        o_rd = sb("o_rd", [P, 2, TPC], F32)
        o_sum = sb("o_sum", [P, 2, TPC, HD], F32)
        attn_g = sb("attn_g", [P, TT, P], F32)

        xin = p32[:, 0:3 * D // CH, :].rearrange("p (t h) n -> p t (h n)", t=3)
        xn = attn_g[:, :, :].rearrange("p (t a) n -> p t (a n)", t=2)

        st = [ps(f"st{i}", [P, CH]) for i in range(ST_BANKS)]
        mx = [ps(f"mx{i}", [P, CH]) for i in range(MX_BANKS)]
        av = ps("av", [P, CH])
        pj = ps("pj", [P, CH])

        consts = sem("consts")
        consts_dve = sem("consts_dve")
        x_loaded = [sem(f"x_loaded{i}") for i in range(3)]
        x_stats = sem("x_stats")
        dve_step = sem("dve_step")
        pool_step = sem("pool_step")
        x_rstd = sem("x_rstd")
        x_normed = sem("x_normed")
        xt_psum = sem("xt_psum")
        xt_hi = sem("xt_hi")
        xt_lo = sem("xt_lo")
        w_loaded = [sem(f"w_loaded{i}") for i in range(3)]
        w_hi = [sem(f"w_hi{i}") for i in range(3)]
        w_lo = [sem(f"w_lo{i}") for i in range(3)]
        proj_psum = sem("proj_psum")
        proj_hi = sem("proj_hi")
        proj_lo = sem("proj_lo")
        stack_set = [sem(f"stack_set{j}") for j in range(GH)]
        v_set = [sem(f"v_set{j}") for j in range(GH)]
        m_psum = sem("m_psum")
        m_done = sem("m_done")
        m_chain = sem("m_chain")
        m_cols_set = sem("m_cols_set")
        m_rows_set = sem("m_rows_set")
        m_in_stack = sem("m_in_stack")
        st_psum = sem("st_psum")
        p32_set = sem("p32_set")
        hi_act = sem("hi_act")
        hi_dve = sem("hi_dve")
        lo_dve = sem("lo_dve")
        lo_pool = sem("lo_pool")
        av_psum = sem("av_psum")
        av_used = sem("av_used")
        rd_set = sem("rd_set")
        o_added = sem("o_added")
        o_done = sem("o_done")
        attn_free = sem("attn_free")

        early_loaded = [sem(f"early_loaded{i}") for i in range(3)]
        early_hi = sem("early_hi")
        early_lo = sem("early_lo")
        biases_loaded = sem("biases_loaded")

        early = early_pieces(weights_in(shared), later)
        x_t = x.rearrange("(t p) d -> t p d", p=P)
        attn_v = attn.rearrange("(t p) f -> p t f", p=P)
        w_dram = [wq, wk, wv]
        b_dram = [bq, bk]

        def proj_no(g, n):
            return g * PER_GROUP + n

        FIRST = [(kind, c) for c in range(NCH) for kind in "qkv"]
        first_banks = [pj, st[0], st[1]]
        turn = [[mx[0], mx[1]], [mx[2], av]]

        def xt_after(no):
            c, a = no // 3, no % 3
            if c == NCH - 1:
                return []
            return [[TPC * (c + 1), TPC * (c + 1) + 1], [TPC * (c + 1) + 2], [TPC * (c + 1) + 3]][a]

        block = ctx.enter_context(nc.Block())

        @block.sync
        def _(sp):
            def load_w(i, g):
                sp.dma_start(w_raw[i][:, :], w_dram[i][bass.ds(g, 1), :, :].rearrange("a p n -> (a p) n")) \
                    .then_inc(w_loaded[i], 16)
                if i < 2:
                    sp.dma_start(b_raw[i][:, :], b_dram[i][bass.ds(g, 1), :, :].rearrange("a p n -> (a p) n")) \
                        .then_inc(w_loaded[i], 16)

            def set_stack(j):
                for r, (a, b) in enumerate((("hi", "hi"), ("hi", "lo"), ("lo", "hi"))):
                    sp.dma_start(q_st[j][HD * r:HD * (r + 1), :], nat[0][a][HD * j:HD * (j + 1), :]) \
                        .then_inc(stack_set[j], 16)
                    sp.dma_start(k_st[j][HD * r:HD * (r + 1), :], nat[1][b][HD * j:HD * (j + 1), :]) \
                        .then_inc(stack_set[j], 16)

            def set_max_rows(no, j):
                sp.wait_ge(m_rows_set, no + 1)
                for part in range(2):
                    sp.dma_start(q_st[j][STK + part:STK + part + 1, :].rearrange("a (t p) -> a t p", p=P),
                                 m_rows[TT * part:TT * (part + 1), :]) \
                        .then_inc(m_in_stack, 16)

            def set_v(j):
                sp.dma_start(v_cur[:, j, :, :], v_next[:, j, :, :]).then_inc(v_set[j], 16)

            sp.dma_start(xin[:, 0, :], x_t[0]).then_inc(x_loaded[0], 16)
            load_w(0, 0)
            sp.dma_start(xin[:, 1, :], x_t[1]).then_inc(x_loaded[1], 16)
            load_w(1, 0)
            sp.dma_start(xin[:, 2, :], x_t[2]).then_inc(x_loaded[2], 16)
            load_w(2, 0)
            for t in range(3, TT):
                sp.wait_ge(x_normed, t - 2)
                sp.dma_start(xin[:, t % 3, :], x_t[t]).then_inc(x_loaded[t % 3], 16)
            for i in range(3):
                sp.wait_ge(w_lo[i], 1)
                load_w(i, 1)
            sp.wait_ge(proj_lo, PER_GROUP)
            for j in range(GH):
                set_stack(j)
            for j in range(GH):
                set_v(j)
            set_max_rows(0, 0)

            def group(g, more):
                def load_next(i):
                    sp.wait_ge(w_lo[i], g + 2)
                    load_w(i, g + 2)

                if not more:
                    last_group()
                    return
                if more == 2:
                    load_next(0)
                set_max_rows(g * GH + 1, 1)
                if more == 2:
                    load_next(1)
                    load_next(2)
                set_max_rows(g * GH + 2, 2)
                if more:
                    sp.wait_ge(proj_lo, proj_no(g + 1, 2 * NCH))
                    set_stack(0)
                set_max_rows(g * GH + 3, 3)
                if more:
                    set_stack(1)
                    sp.wait_ge(st_psum, g * GB + 3 * NB)
                    set_stack(2)
                    set_max_rows(g * GH + 4, 0)
                    sp.wait_ge(proj_lo, proj_no(g + 2, 0))
                    for j in range(GH - 1):
                        set_v(j)
                    sp.wait_ge(st_psum, g * GB + 4 * NB)
                    set_stack(3)
                    sp.wait_ge(av_psum, g * GH * NCH + GH * NCH)
                    set_v(GH - 1)
                sp.wait_ge(o_done, g * GH * NCH + GH * NCH + 2)
                sp.dma_start(attn_v[:, :, bass.ds(g * P, P)], attn_g[:, :, :]).then_inc(attn_free, 16)

            def last_group():
                def load_early(n):
                    if n >= 3:
                        sp.wait_ge(early_lo, n - 2)
                    _, _, src, k, cols, rws = early[n]
                    sp.dma_start(w_raw[n % 3][0:rws, 0:k * cols].rearrange("p (k n) -> p k n", k=k), src) \
                        .then_inc(early_loaded[n % 3], 16)

                g = NG - 1
                for n in range(3):
                    load_early(n)
                for n, bias in enumerate(later_biases):
                    sp.dma_start(vectors[:, n * D:(n + 1) * D], bias.broadcast_to([P, D])).then_inc(biases_loaded, 16)
                for s in range(GB):
                    for n in range(3, len(early)):
                        if early_at(n - 3) == s:
                            load_early(n)
                    if s % NB == MSPAN + 1 and s < GB - NB:
                        set_max_rows(g * GH + s // NB + 1, s // NB + 1)
                sp.wait_ge(biases_loaded, 16 * len(later_biases))
                sp.wait_ge(o_done, GH * NCH * NG + 2)
                sp.dma_start(attn_v[:, :, g * P:(g + 1) * P], attn_g[:, :, :]).then_inc(attn_free, 16)

            with sp.Fori(0, NG - 2) as g:
                group(g, 2)
            group(NG - 2, 1)
            group(NG - 1, 0)
            sp.wait_ge(attn_free, 16 * NG + 16)

        @block.gpsimd
        def _(pool):
            n_step = [0]

            def step(ins):
                n_step[0] += 1
                ins.then_inc(pool_step, 1)
                pool.wait_ge(pool_step, n_step[0])

            for m in (ident, ident_h, ident_b):
                step(nc.gpsimd.memset(m[:, :], 0.0))
                step(nc.gpsimd.affine_select(out=m[:, :], in_=m[:, :], compare_op=ALU.not_equal, fill=1.0,
                                             base=0, pattern=[[-1, P]], channel_multiplier=1))
            for m, sign in ((mask_qk, 1), (mask_kq, -1)):
                step(nc.gpsimd.memset(m[:, :], 0.0))
                step(nc.gpsimd.affine_select(out=m[:, :], in_=m[:, :], compare_op=ALU.is_ge, fill=NEG,
                                             base=0, pattern=[[-sign, P]], channel_multiplier=sign))
            step(nc.gpsimd.memset(neg_half[:, :], -0.5))
            nc.gpsimd.memset(v_next[:, :, :, HD:HD + 1], 1.0).then_inc(consts, 1)
            for t in range(TT):
                b = t % 2
                pool.wait_ge(x_stats, t + 1)
                if t >= 2:
                    pool.wait_ge(x_normed, t - 1)
                step(nc.gpsimd.tensor_scalar(rs[:, b, 0:1], mv[:, b, 1:2], EPS, None, ALU.add))
                step(nc.gpsimd.tensor_tensor(rs[:, b, 1:2], rs[:, b, 0:1], neg_half[:, :], ALU.pow))
                step(nc.gpsimd.tensor_tensor(rs[:, b, 2:3], mv[:, b, 0:1], rs[:, b, 1:2], ALU.mult))
                nc.gpsimd.tensor_scalar(rs[:, b, 3:4], rs[:, b, 2:3], -1.0, None, ALU.mult).then_inc(x_rstd, 1)

            nc.gpsimd.sem_inc(o_done, 2)
            nc.gpsimd.sem_inc(attn_free, 16)

            def group(g):
                def low_part(s):
                    if hi_on_dve(s):
                        pool.wait_ge(hi_dve, g * count(hi_on_dve, GB - 1) + count(hi_on_dve, s))
                    else:
                        pool.wait_ge(hi_act, g * count(hi_on_act, GB - 1) + count(hi_on_act, s) + ST_BANKS)
                    wd = BLOCKS[s % NB][3]
                    r = s % RING
                    nc.gpsimd.tensor_tensor(p_lo[:, r, 0:wd], p32[:, r, 0:wd], p_hi[:, r, 0:wd],
                                            ALU.subtract).then_inc(lo_pool, 1)

                def output(c):
                    j, qc = c // NCH, c % NCH
                    no = g * GH * NCH + c
                    b = c % 2
                    pool.wait_ge(rd_set, no + 1)
                    if c == 0:
                        pool.wait_ge(attn_free, 16 * g + 16)
                    nc.gpsimd.tensor_tensor(o_sum[:, b, :, :], o_cp[:, b, :, 0:HD], o_cp[:, b, :, HD + 1:VW],
                                            ALU.add).then_inc(o_added, 1)
                    pool.wait_ge(o_added, no + 1)
                    rd = o_rd[:, b, :].rearrange("p (r a) -> p r a", a=1).broadcast_to([P, TPC, HD])
                    nc.gpsimd.tensor_tensor(attn_g[:, qc * TPC:(qc + 1) * TPC, j * HD:(j + 1) * HD],
                                            o_sum[:, b, :, :], rd, ALU.mult).then_inc(o_done, 1)

                for s in range(GB + 1):
                    if s and not lo_on_dve(s - 1):
                        low_part(s - 1)
                    for c in chunks_at(s, LAG + 3):
                        output(c)
                for c in chunks_after(LAG + 3, GB):
                    output(c)

            with pool.Fori(0, NG) as g:
                group(g)

        @block.scalar
        def _(act):
            def split_w(i, g):
                act.wait_ge(w_loaded[i], (g + 1) * (32 if i < 2 else 16))
                if not (isinstance(g, int) and g == 0):
                    act.wait_ge(proj_lo, proj_no(g, 0))
                nc.scalar.activation(w[i]["hi"][:, :, :].rearrange("p k n -> p (k n)"), w_raw[i][:, :],
                                     ACT.Copy, scale=WS).then_inc(w_hi[i], 1)
                if i < 2:
                    nc.scalar.activation(b_sc[i][:, :], b_raw[i][:, :], ACT.Copy, scale=WS).then_inc(w_hi[i], 1)

            def take_proj(kind, c, bank, no):
                act.wait_ge(proj_psum, no + 1)
                if kind == "v":
                    o = v_next[:, :, c * TPC:(c + 1) * TPC, 0:HD].rearrange("p j t f -> p t j f")
                    i_ = bank[:, :].rearrange("p (t j f) -> p t j f", t=TPC, j=GH)
                    nc.scalar.activation(o, i_, ACT.Copy).then_inc(proj_hi, 1)
                else:
                    i = "qk".index(kind)
                    nc.scalar.activation(nat[i]["hi"][:, c * CH:(c + 1) * CH], bank[:, :], ACT.Identity,
                                         bias=b_sc[i][:, 0:1]).then_inc(proj_hi, 1)

            act.wait_ge(consts, 1)

            def norm_tile(t):
                act.wait_ge(x_rstd, t + 1)
                if t >= 2:
                    act.wait_ge(xt_psum, t - 1)
                nc.scalar.activation(xn[:, t % 2, :], xin[:, t % 3, :], ACT.Identity, bias=rs[:, t % 2, 3:4],
                                     scale=rs[:, t % 2, 1:2]).then_inc(x_normed, 1)

            def take_xt(t):
                act.wait_ge(xt_psum, t + 1)
                for h in range(2):
                    bank = turn[t % 2][h]
                    ins = nc.scalar.activation(xt["hi"][:, 4 * h:4 * h + 4, t * P:(t + 1) * P],
                                               bank[:, :].rearrange("p (k n) -> p k n", k=4), ACT.Copy)
                ins.then_inc(xt_hi, 1)

            for i in range(3):
                if i == 0:
                    norm_tile(0)
                split_w(i, 0)
            for t in range(1, TPC + 1):
                norm_tile(t)
                take_xt(t - 1)
            for c in range(NCH):
                for a in range(3):
                    no = 3 * c + a
                    take_proj(*FIRST[no], first_banks[no % 3], no)
                    for t in xt_after(no):
                        if t + 1 < TT:
                            norm_tile(t + 1)
                        take_xt(t)

            def group(g, more):
                def exps(s):
                    wd = BLOCKS[s % NB][3]
                    r = s % RING
                    act.wait_ge(st_psum, g * GB + s + 1)
                    nc.scalar.activation(p32[:, r, 0:wd], st[s % ST_BANKS][:, 0:wd], ACT.Exp,
                                         scale=EXP_SCALE).then_inc(p32_set, 1)
                    if hi_on_act(s):
                        nc.scalar.activation(p_hi[:, r, 0:wd], st[s % ST_BANKS][:, 0:wd], ACT.Exp,
                                             scale=EXP_SCALE).then_inc(hi_act, 1)

                def copy_out(c):
                    no = g * GH * NCH + c
                    act.wait_ge(av_psum, no + 1)
                    act.wait_ge(o_done, no + 1)
                    nc.scalar.activation(o_cp[:, c % 2, :, :].rearrange("p t f -> p (t f)"),
                                         av[:, 0:TPC * VW], ACT.Copy).then_inc(av_used, 1)

                for s in range(GB):
                    if more:
                        for i, at in SPLIT_AT.items():
                            if at == s:
                                split_w(i, g + 1)
                    for c in chunks_at(s, LAG + 1):
                        copy_out(c)
                    exps(s)
                    if more:
                        for n, (kind, c, start, span) in enumerate(PROJ):
                            if start + span == s:
                                if (kind, c) in (("q", 0), ("v", 0)):
                                    for j in range(GH):
                                        act.wait_ge((v_set if kind == "v" else stack_set)[j],
                                                    (16 if kind == "v" else 96) * (g + 1))
                                take_proj(kind, c, pj, proj_no(g + 1, n))
                for c in chunks_after(LAG + 1, GB - 1):
                    copy_out(c)

            nc.scalar.sem_inc(p32_set, ST_BANKS)
            nc.scalar.sem_inc(hi_act, ST_BANKS)
            nc.scalar.sem_inc(av_used, 1)
            with act.Fori(0, NG - 1) as g:
                group(g, True)
            group(NG - 1, False)

        @block.vector
        def _(dve):
            n_step = [0]

            def step(ins):
                n_step[0] += 1
                ins.then_inc(dve_step, 1)
                dve.wait_ge(dve_step, n_step[0])

            def split_w(i, g):
                dve.wait_ge(w_hi[i], (g + 1) * (2 if i < 2 else 1))
                nc.vector.scalar_tensor_tensor(out=w[i]["lo"][:, :, :].rearrange("p k n -> p (k n)"),
                                               in0=w_raw[i][:, :], scalar=WS,
                                               in1=w[i]["hi"][:, :, :].rearrange("p k n -> p (k n)"),
                                               op0=ALU.mult, op1=ALU.subtract).then_inc(w_lo[i], 1)

            def take_proj(kind, c, bank, no):
                dve.wait_ge(proj_hi, no + 1)
                if kind == "v":
                    o = v_next[:, :, c * TPC:(c + 1) * TPC, HD + 1:VW].rearrange("p j t f -> p t j f")
                    h = v_next[:, :, c * TPC:(c + 1) * TPC, 0:HD].rearrange("p j t f -> p t j f")
                    i_ = bank[:, :].rearrange("p (t j f) -> p t j f", t=TPC, j=GH)
                    nc.vector.tensor_tensor(o, i_, h, ALU.subtract).then_inc(proj_lo, 1)
                else:
                    i = "qk".index(kind)
                    nc.vector.scalar_tensor_tensor(out=nat[i]["lo"][:, c * CH:(c + 1) * CH], in0=bank[:, :],
                                                   scalar=b_sc[i][:, 0:1], in1=nat[i]["hi"][:, c * CH:(c + 1) * CH],
                                                   op0=ALU.add, op1=ALU.subtract).then_inc(proj_lo, 1)

            for j in range(GH):
                nc.vector.memset(q_st[j][STK:P, :], 0.0).then_inc(consts_dve, 1)
                nc.vector.memset(k_st[j][STK:P, :], MROW).then_inc(consts_dve, 1)
            step(nc.vector.memset(m_part[:, :, :], -3e38))

            def stats_tile(t):
                dve.wait_ge(x_loaded[t % 3], 16 * (t // 3 + 1))
                if t >= 2:
                    dve.wait_ge(x_rstd, t - 1)
                for h in range(2):
                    ins = nc.vector.bn_stats(stats[:, t % 2, h, :], xin[:, t % 3, h * CH:(h + 1) * CH])
                step(ins)
                nc.vector.bn_aggr(mv[:, t % 2, :], stats[:, t % 2, :, :].rearrange("p a b -> p (a b)")) \
                    .then_inc(x_stats, 1)

            def take_xt(t):
                dve.wait_ge(xt_hi, t + 1)
                for h in range(2):
                    bank = turn[t % 2][h]
                    ins = nc.vector.tensor_tensor(xt["lo"][:, 4 * h:4 * h + 4, t * P:(t + 1) * P],
                                                  bank[:, :].rearrange("p (k n) -> p k n", k=4),
                                                  xt["hi"][:, 4 * h:4 * h + 4, t * P:(t + 1) * P], ALU.subtract)
                ins.then_inc(xt_lo, 1)

            stats_tile(0)
            for i in range(3):
                split_w(i, 0)
            stats_tile(1)
            for t in range(TPC):
                stats_tile(t + 2)
                take_xt(t)
            for c in range(NCH):
                for a in range(3):
                    no = 3 * c + a
                    take_proj(*FIRST[no], first_banks[no % 3], no)
                    for t in xt_after(no):
                        if t + 2 < TT:
                            stats_tile(t + 2)
                        take_xt(t)

            def max_columns(no):
                dve.wait_ge(m_done, (no + 1) * len(MBLOCKS))
                nc.vector.tensor_reduce(m_all[:, :], m_part[:, :, :], AX.X, ALU.max).then_inc(m_chain, 1)
                dve.wait_ge(m_chain, 2 * no + 1)
                nc.vector.tensor_scalar(m_cols[:, 0:TT], m_all[:, :], -1.0 / MROW, None, ALU.mult).then_inc(m_chain, 1)
                dve.wait_ge(m_chain, 2 * no + 2)
                nc.vector.scalar_tensor_tensor(out=m_cols[:, TT:2 * TT], in0=m_all[:, :], scalar=-1.0 / MROW,
                                               in1=m_cols[:, 0:TT], op0=ALU.mult, op1=ALU.subtract) \
                    .then_inc(m_cols_set, 1)

            def head_max(n, i, use0, no):
                for a in max_blocks_at(i):
                    t, c, wd, _ = MBLOCKS[a]
                    dve.wait_ge(m_psum, use0 + a + 1)
                    nc.vector.tensor_reduce(m_part[:, t, c:c + 1], mx[(n + a) % MX_BANKS][:, 0:wd], AX.X, ALU.max) \
                        .then_inc(m_done, 1)
                if i == MSPAN:
                    max_columns(no)
                if i == MSPAN + 1:
                    dve.wait_ge(m_psum, use0 + MR)
                    if not (isinstance(no, int) and no == 0):
                        dve.wait_ge(m_in_stack, 32 * no)
                    bank = mx[(n + MR - 1) % MX_BANKS][0:2 * TT, 0:P // 2].bitcast(F16)
                    nc.vector.tensor_copy(m_rows[:, :], bank).then_inc(m_rows_set, 1)

            for i in range(MSPAN + 2):
                head_max((GH - 1) * MR, i, 0, 0)

            def group(g, more):
                def cast(s):
                    dve.wait_ge(p32_set, g * GB + s + 1 + ST_BANKS)
                    wd = BLOCKS[s % NB][3]
                    r = s % RING
                    nc.vector.tensor_copy(p_hi[:, r, 0:wd], p32[:, r, 0:wd]).then_inc(hi_dve, 1)

                def low_part(s):
                    dve.wait_ge(hi_act, g * count(hi_on_act, GB - 1) + count(hi_on_act, s) + ST_BANKS)
                    wd = BLOCKS[s % NB][3]
                    r = s % RING
                    nc.vector.tensor_tensor(p_lo[:, r, 0:wd], p32[:, r, 0:wd], p_hi[:, r, 0:wd],
                                            ALU.subtract).then_inc(lo_dve, 1)

                def reciprocal(c):
                    no = g * GH * NCH + c
                    dve.wait_ge(av_used, no + 1 + 1)
                    nc.vector.reciprocal(o_rd[:, c % 2, :], o_cp[:, c % 2, :, HD]).then_inc(rd_set, 1)

                def split_early(n):
                    hi, lo, _, k, cols, rws = early[n]
                    raw = w_raw[n % 3][0:rws, 0:k * cols].rearrange("p (k n) -> p k n", k=k)
                    dve.wait_ge(early_loaded[n % 3], 16 * (n // 3 + 1))
                    nc.vector.tensor_scalar(hi, raw, WS, None, ALU.mult).then_inc(early_hi, 1)
                    dve.wait_ge(early_hi, n + 1)
                    nc.vector.scalar_tensor_tensor(out=lo, in0=raw, scalar=WS, in1=hi, op0=ALU.mult,
                                                   op1=ALU.subtract).then_inc(early_lo, 1)

                for s in range(GB + 1):
                    j, i = s // NB, s % NB
                    if not more:
                        for n in range(len(early)):
                            if early_at(n) == s:
                                split_early(n)
                        if s == GB - NB:
                            dve.wait_ge(biases_loaded, 16 * len(later_biases))
                            nc.vector.tensor_scalar(vectors[:, 0:D], vectors[:, 0:D], WS, None, ALU.mult)
                    if s < GB and more and s - 1 in SPLIT_AT.values():
                        split_w({v: k for k, v in SPLIT_AT.items()}[s - 1], g + 1)
                    if s < GB and (more or j < GH - 1):
                        head_max(j * MR, i, MR + g * GH * MR + j * MR, g * GH + j + 1)
                    if s and hi_on_dve(s - 1):
                        cast(s - 1)
                    if s and lo_on_dve(s - 1):
                        low_part(s - 1)
                    if more:
                        for n, (kind, c, start, span) in enumerate(PROJ):
                            if start + span + 1 == s:
                                take_proj(kind, c, pj, proj_no(g + 1, n))
                    for c in chunks_at(s, LAG + 2):
                        reciprocal(c)
                for c in chunks_after(LAG + 2, GB):
                    reciprocal(c)

            with dve.Fori(0, NG - 1) as g:
                group(g, True)
            group(NG - 1, False)

        @block.tensor
        def _(pe):
            def transpose_x(t):
                pe.wait_ge(x_normed, t + 1)
                if t >= 2:
                    pe.wait_ge(xt_lo, t - 1)
                for k in range(KC):
                    ins = nc.tensor.transpose(turn[t % 2][k // 4][:, (k % 4) * P:(k % 4 + 1) * P],
                                              xn[:, t % 2, k * P:(k + 1) * P], ident[:, :])
                ins.then_inc(xt_psum, 1)

            def project(kind, c, bank, lo, hi):
                i = "qkv".index(kind)
                steps = steps_of(kind)
                for m in range(lo, min(hi, len(steps))):
                    r, (a, b), k = steps[m]
                    first, last = (a, b, k) == ("hi", "hi", 0), (a, b, k) == ("lo", "hi", KC - 1)
                    if kind == "v":
                        t = c * TPC + r
                        ins = nc.tensor.matmul(bank[:, r * P:(r + 1) * P], xt[a][:, k, t * P:(t + 1) * P],
                                               w[i][b][:, k, :], start=first, stop=last)
                    else:
                        ins = nc.tensor.matmul(bank[:, :], w[i][b][:, k, :], xt[a][:, k, c * CH:(c + 1) * CH],
                                               start=first, stop=last)
                    if m == len(steps) - 1:
                        ins.then_inc(proj_psum, 1)

            def head_max(n, i, j, no):
                for a in max_blocks_at(i):
                    t, c, wd, diagonal = MBLOCKS[a]
                    back, b = divmod(same_bank_before(n + a, MX_BANKS, GH * MR), MR)
                    head = no + back - n // MR
                    if not (isinstance(head, int) and head < 0):
                        if b < MR - 1:
                            pe.wait_ge(m_done, head * len(MBLOCKS) + b + 1)
                        else:
                            pe.wait_ge(m_rows_set, head + 1)
                    bank = mx[(n + a) % MX_BANKS]
                    ins = nc.tensor.matmul(bank[:, 0:wd], q_st[j][0:STK, t * P:(t + 1) * P],
                                           k_st[j][0:STK, c * CH:c * CH + wd], start=True, stop=not diagonal)
                    if diagonal:
                        ins = nc.tensor.matmul(bank[:, wd - P:wd], ident_b[:, :], mask_qk[:, :],
                                               start=False, stop=True)
                    ins.then_inc(m_psum, 1)
                if i == MSPAN + 1:
                    pe.wait_ge(m_cols_set, no + 1)
                    nc.tensor.transpose(mx[(n + MR - 1) % MX_BANKS][0:2 * TT, 0:P // 2].bitcast(F16), m_cols[:, :],
                                        ident_h[:, :]).then_inc(m_psum, 1)

            pe.wait_ge(consts, 1)
            for t in range(TPC):
                transpose_x(t)
            for c in range(NCH):
                pe.wait_ge(xt_lo, TPC * (c + 1))
                for a in range(3):
                    no = 3 * c + a
                    kind, _ = FIRST[no]
                    if c == 0:
                        pe.wait_ge(w_lo[a], 1)
                    if no >= 3:
                        pe.wait_ge(proj_lo, no - 2)
                    project(kind, c, first_banks[no % 3], 0, 1 << 30)
                    for t in xt_after(no):
                        transpose_x(t)
            pe.wait_ge(proj_lo, PER_GROUP)
            pe.wait_ge(consts_dve, 2 * GH)
            pe.wait_ge(stack_set[0], 96)
            for i in range(MSPAN + 2):
                head_max((GH - 1) * MR, i, 0, 0)

            def group(g, more):
                def scores(s):
                    j, i = s // NB, s % NB
                    qc, kt, q0, wd, diagonal = BLOCKS[i]
                    if i == 0:
                        pe.wait_ge(m_in_stack, 32 * (g * GH + j + 1))
                    before = same_bank_before(s, ST_BANKS, GB)
                    if hi_on_dve(before):
                        pe.wait_ge(p32_set, g * GB + before + 1 + ST_BANKS)
                    else:
                        pe.wait_ge(hi_act, g * count(hi_on_act, GB - 1) + count(hi_on_act, before) + ST_BANKS)
                    bank = st[s % ST_BANKS]
                    ins = nc.tensor.matmul(bank[:, 0:wd], k_st[j][0:ROWS, kt * P:(kt + 1) * P],
                                           q_st[j][0:ROWS, q0:q0 + wd], start=True, stop=not diagonal)
                    if diagonal:
                        ins = nc.tensor.matmul(bank[:, 0:P], ident_b[:, :], mask_kq[:, :], start=False, stop=True)
                    ins.then_inc(st_psum, 1)

                def values(s):
                    j, i = s // NB, s % NB
                    qc, kt, q0, wd, _ = BLOCKS[i]
                    r = s % RING
                    c = j * NCH + qc
                    if i == 0:
                        pe.wait_ge(v_set[j], 16 * (g + 1))
                    if kt == 0:
                        pe.wait_ge(av_used, g * GH * NCH + c + 1)
                    if lo_on_dve(s):
                        pe.wait_ge(lo_dve, g * count(lo_on_dve, GB - 1) + count(lo_on_dve, s))
                    else:
                        pe.wait_ge(lo_pool, g * count(lo_on_pool, GB - 1) + count(lo_on_pool, s))
                    first = True
                    for n in range(wd // P):
                        t = (q0 + n * P) // P - qc * TPC
                        o = av[:, t * VW:(t + 1) * VW]
                        stop = kt == qc * TPC + t
                        nc.tensor.matmul(o, p_hi[:, r, n * P:(n + 1) * P], v_cur[:, j, kt, :],
                                         start=(kt == 0 and n == 0), stop=False, skip_group_check=True)
                        ins = nc.tensor.matmul(o[:, 0:HD + 1], p_lo[:, r, n * P:(n + 1) * P],
                                               v_cur[:, j, kt, 0:HD + 1], start=False, stop=stop,
                                               skip_group_check=True)
                    if s in ENDS:
                        ins.then_inc(av_psum, 1)

                for s in range(GB):
                    j, i = s // NB, s % NB
                    scores(s)
                    if more or j < GH - 1:
                        jn = (j + 1) % GH
                        if i == 0:
                            pe.wait_ge(stack_set[jn], 96 * (g + 1 if jn else g + 2))
                        head_max(j * MR, i, jn, g * GH + j + 1)
                    if more:
                        for n, (kind, c, start, span) in enumerate(PROJ):
                            if start <= s < start + span:
                                per = len(steps_of(kind)) // span
                                if s == start:
                                    pe.wait_ge(proj_lo, proj_no(g + 1, n))
                                    if c == 0:
                                        pe.wait_ge(w_lo["qkv".index(kind)], g + 2)
                                project(kind, c, pj, per * (s - start), per * (s - start + 1))
                    for v in values_at(s):
                        values(v)
                for v in values_at(GB):
                    values(v)

            with pe.Fori(0, NG - 1) as g:
                group(g, True)
            group(NG - 1, False)


W_STEPS = ("turn", "project", "y", "add", "norm", "back")
W_START = [-2, 4, 10, FT + 1 - len(W_STEPS)]
W_FIRST = [("fetch", 0), ("turn", 0), ("fetch", 1), ("turn", 1), ("fetch", 2), ("project", 0), ("turn", 2),
           ("fetch", 3), 4,
           ("y", 0), 1, ("add", 0), 1, ("norm", 0), ("project", 1), ("turn", 3),
           ("y", 1), 1, ("add", 1), 1, ("norm", 1), ("project", 2), ("back", 0),
           ("y", 2), 1, ("add", 2), 1, ("norm", 2), ("project", 3), ("back", 1),
           ("y", 3), 1, ("add", 3), 1, ("norm", 3), ("back", 2), ("back", 3)]
Z_LAG = 2
PAIR_USES = FT + TPC
assert RC % 2 == FT % 2 == TPC % 2 == 0
PIECE = 1024


def weights_in(shared):
    flat = shared[:, :]
    w, at = {}, 0
    for name, k, n in (("wo", KC, D), ("u1", KC, RANK), ("u2", FT, RANK)):
        w[name] = {}
        for h in ("hi", "lo"):
            w[name][h] = flat[:, at:at + k * n].rearrange("p (k n) -> p k n", k=k)
            at += k * n
    return w


def early_pieces(w, dram):
    out = []

    def add(name, index, src, shape):
        rows, k, n = shape
        out.append((w[name]["hi"][index], w[name]["lo"][index], src, k, n, rows))

    wo, u1, u2 = (dram[n] for n in ("wo", "u1", "u2"))
    for k in range(KC):
        add("wo", (slice(0, P), slice(k, k + 1), slice(0, D)),
            wo[k * P:(k + 1) * P, :].rearrange("(k p) n -> p k n", p=P), (P, 1, D))
    for k in range(0, KC, 4):
        add("u1", (slice(0, P), slice(k, k + 4), slice(0, RANK)),
            u1[k * P:(k + 4) * P, :].rearrange("(k p) n -> p k n", p=P), (P, 4, RANK))
    for f in range(0, FT - 1, 4):
        n = min(4, FT - 1 - f)
        add("u2", (slice(0, P), slice(f, f + n), slice(0, RANK)),
            u2[f * P:(f + n) * P, :].rearrange("(k p) n -> p k n", p=P), (P, n, RANK))
    add("u2", (slice(0, FLAST), slice(FT - 1, FT), slice(0, RANK)),
        u2[(FT - 1) * P:INTER, :].rearrange("(k p) n -> p k n", p=FLAST), (FLAST, 1, RANK))
    return out


def late_pieces(w, dram):
    out = []

    def add(name, index, src, shape):
        rows, k, n = shape
        out.append((w[name]["hi"][index], w[name]["lo"][index], src, k, n, rows))

    v1, v2 = dram["v1"], dram["v2"]
    for at in range(0, INTER, PIECE // 2):
        n = min(PIECE // 2, INTER - at)
        for base in (0, INTER):
            add("v1", (slice(0, P), slice(0, RC), slice(base + at, base + at + n)),
                v1[:, base + at:base + at + n].rearrange("(k p) n -> p k n", p=P), (P, RC, n))
    for k in range(RC):
        add("v2", (slice(0, P), slice(k, k + 1), slice(0, D)),
            v2[k * P:(k + 1) * P, :].rearrange("(k p) n -> p k n", p=P), (P, 1, D))
    return out


def ffn_phase(nc, shared, vectors, x, attn, dram, b1g, b1u, x1, out):
    ctx = ExitStack()
    with ctx:
        def sb(name, shape, dt):
            return ctx.enter_context(nc.sbuf_tensor(name, shape, dt))

        def ps(name, shape, dt=F32):
            return ctx.enter_context(nc.psum_tensor(name, shape, dt))

        def sem(name):
            return ctx.enter_context(nc.semaphore(name))

        w = weights_in(shared)
        for name, shape in (("v1", [P, RC, 2 * INTER]), ("v2", [P, RC, D])):
            w[name] = {h: sb(f"{name}_{h}", shape, F16) for h in ("hi", "lo")}
        pieces = late_pieces(w, dram)
        v1_pieces = 2 * (-(-INTER // (PIECE // 2)))
        raw = sb("raw", [P, 2, PIECE], F32)
        ident2 = sb("ident2", [P, P], F32)
        neg_half2 = sb("neg_half2", [P, 1], F32)
        eps_c = sb("eps_c", [P, 1], F32)
        minus_one = sb("minus_one", [P, 1], F32)
        bv_b, bo_b, b2_b = (vectors[:, n * D:(n + 1) * D] for n in range(3))
        b1g_c = sb("b1g_c", [P, FT], F32)
        b1u_c = sb("b1u_c", [P, FT], F32)
        at_in = sb("at_in", [P, 1, D], F32)
        at_t = {h: sb(f"at_{h}", [P, KC, P], F16) for h in ("hi", "lo")}
        x_in = sb("x_in", [P, D], F32)
        y = sb("y", [P, D], F32)
        xn1 = sb("xn1", [P, D], F32)
        x1t = {h: sb(f"x1t_{h}", [P, KC, CH], F16) for h in ("hi", "lo")}
        spare = shared[:, 2 * KC * S - RC * CH:].rearrange("p (k n) -> p k n", k=RC)
        p1t = {"hi": spare, "lo": sb("p1t_lo", [P, RC, CH], F16)}
        sg = sb("sg", [P, 2, CH], F32)
        a32 = sb("a32", [P, 3, CH], F32)
        act_t = {h: sb(f"act_{h}", [P, 3, CH], F16) for h in ("hi", "lo")}
        zt = {h: sb(f"zt_{h}", [P, RC, CH], F16) for h in ("hi", "lo")}
        yo = sb("yo", [P, 2, D], F32)
        x1_in = sb("x1_in", [P, D], F32)
        ln = {n: [(sb(f"st_{n}{i}", [P, 2, 6], F32), sb(f"mv_{n}{i}", [P, 2], F32), sb(f"rs_{n}{i}", [P, 4], F32))
                  for i in range(2 if n == "out" else 1)] for n in ("y", "x1", "out")}

        pair = [[ps(f"pair{i}{h}", [P, CH]) for h in range(2)] for i in range(2)]
        wp = [ps(f"wp{h}", [P, CH]) for h in range(2)]
        zp = [ps(f"zp{r}", [P, CH]) for r in range(RC)]

        pool_chain = sem("pool_chain")
        biases = sem("biases")
        bias_scaled = sem("bias_scaled")
        raw_loaded = [sem(f"raw_loaded{i}") for i in range(2)]
        piece_hi = sem("piece_hi")
        piece_lo = sem("piece_lo")
        attn_loaded = sem("attn_loaded")
        attn_biased = sem("attn_biased")
        x_loaded2 = sem("x_loaded2")
        turn_psum = sem("turn_psum")
        turn_taken = sem("turn_taken")
        project_psum = sem("project_psum")
        y_taken = sem("y_taken")
        back_psum = sem("back_psum")
        back_taken = sem("back_taken")
        at_hi = sem("at_hi")
        ln_stats = {n: sem(f"ln_stats_{n}") for n in ln}
        wait_carrier = sem("wait_carrier")
        ln_chain = {n: sem(f"ln_chain_{n}") for n in ln}
        ln_rstd = {n: sem(f"ln_rstd_{n}") for n in ln}
        y_normed = sem("y_normed")
        x1_set = sem("x1_set")
        x1_stored = sem("x1_stored")
        x1_normed = sem("x1_normed")
        x1t_hi = sem("x1t_hi")
        p1_psum = sem("p1_psum")
        pair_psum = sem("pair_psum")
        p1_lo = sem("p1_lo")
        out_taken = sem("out_taken")
        p1_hi = sem("p1_hi")
        sg_set = sem("sg_set")
        a32_set = sem("a32_set")
        act_hi_set = sem("act_hi_set")
        act_lo_set = sem("act_lo_set")
        z_psum = sem("z_psum")
        z_hi = sem("z_hi")
        z_lo = sem("z_lo")
        yo_normed = sem("yo_normed")
        x1_loaded = sem("x1_loaded")
        out_set = sem("out_set")
        out_stored = [sem(f"out_stored{i}") for i in range(2)]

        def rows(t):
            return (bass.ds(t * P, P), slice(0, D))

        def inner(f):
            return FLAST if f == FT - 1 else P

        def w_steps(f):
            fetched = [("fetch", r + 1) for r in range(TPC - 1) if W_START[r] + W_STEPS.index("project") == f]
            return fetched + [(name, r) for r, at in enumerate(W_START) for n, name in enumerate(W_STEPS)
                              if at + n == f]

        def w_banks(name, t):
            if isinstance(t, int) and t < TPC:
                return {"turn": zp, "project": pair[t % 2], "back": wp}[name]
            return wp

        def turned(t):
            if isinstance(t, int) and t < TPC and t % 2:
                return {h: x1t[h][:, :, CH - P:CH] for h in ("hi", "lo")}
            return {h: at_t[h][:, :, :] for h in ("hi", "lo")}

        block = ctx.enter_context(nc.Block())

        @block.sync
        def _(sp):
            def load_piece(n):
                hi, lo, src, k, cols, rws = pieces[n]
                if n >= 2:
                    sp.wait_ge(piece_lo, n - 1)
                sp.dma_start(raw[0:rws, n % 2, 0:k * cols].rearrange("p (k n) -> p k n", k=k), src) \
                    .then_inc(raw_loaded[n % 2], 16)

            def step(name, t):
                if name == "fetch":
                    if not (isinstance(t, int) and t == 0):
                        sp.wait_ge(turn_psum, t)
                    sp.dma_start(at_in[:, 0, :], attn[rows(t)]).then_inc(attn_loaded, 16)
                if name == "y":
                    if not (isinstance(t, int) and t == 0):
                        sp.wait_ge(x1_set, t)
                    sp.dma_start(x_in[:, :], x[rows(t)]).then_inc(x_loaded2, 16)
                if name == "norm":
                    sp.wait_ge(x1_set, t + 1)
                    sp.dma_start(x1[rows(t)], y[:, :]).then_inc(x1_stored, 16)

            pieces_left = iter(range(2, len(pieces)))
            for at, entry in enumerate(W_FIRST):
                if isinstance(entry, int):
                    for _, n in zip(range(entry), pieces_left):
                        load_piece(n)
                else:
                    step(*entry)
                if at == 0:
                    sp.dma_start(b1g_c[:, :], b1g).then_inc(biases, 16)
                    sp.dma_start(b1u_c[:, :], b1u).then_inc(biases, 16)
                    load_piece(0)
                    load_piece(1)
            for n in pieces_left:
                load_piece(n)
            step("fetch", TPC)

            def finish(c):
                sp.wait_ge(x1_stored, 16 * TPC * (c + 1))
                for r in range(TPC):
                    t = c * TPC + r
                    sp.wait_ge(out_set, t + 1)
                    sp.dma_start(x1_in[:, :], x1[rows(t)]).then_inc(x1_loaded, 16)
                    sp.wait_ge(out_set, t + 2)
                    sp.dma_start(out[rows(t)], yo[:, r % 2, :]).then_inc(out_stored[r % 2], 16)

            def chunk(c, more):
                for f in range(-2, FT + 1):
                    for name, r in w_steps(f):
                        step(name, (c + 1) * TPC + r)
                if more:
                    step("fetch", (c + 2) * TPC)
                finish(c)

            with sp.Fori(0, NCH - 2) as c:
                chunk(c, True)
            chunk(NCH - 2, False)
            finish(NCH - 1)
            for i in range(2):
                sp.wait_ge(out_stored[i], 16 * (TT // 2) + 16)

        @block.gpsimd
        def _(pool):
            nc.gpsimd.memset(ident2[:, :], 0.0).then_inc(pool_chain, 1)
            pool.wait_ge(pool_chain, 1)
            nc.gpsimd.affine_select(out=ident2[:, :], in_=ident2[:, :], compare_op=ALU.not_equal, fill=1.0,
                                    base=0, pattern=[[-1, P]], channel_multiplier=1).then_inc(pool_chain, 1)
            for c, value in ((neg_half2, -0.5), (eps_c, EPS), (minus_one, -1.0)):
                nc.gpsimd.memset(c[:, :], value).then_inc(pool_chain, 1)
            pool.wait_ge(pool_chain, 5)
            nc.gpsimd.sem_inc(out_set, 1)
            for i in range(2):
                nc.gpsimd.sem_inc(out_stored[i], 16)

            def rstd(n, t, b=0):
                _, mv, rs = ln[n][b]
                s = ln_rstd[n]
                pool.wait_ge(ln_stats[n], t + 1)
                nc.gpsimd.tensor_tensor(rs[:, 0:1], mv[:, 1:2], eps_c[:, :], ALU.add).then_inc(s, 1)
                pool.wait_ge(s, 4 * t + 1)
                nc.gpsimd.tensor_tensor(rs[:, 1:2], rs[:, 0:1], neg_half2[:, :], ALU.pow).then_inc(s, 1)
                pool.wait_ge(s, 4 * t + 2)
                nc.gpsimd.tensor_tensor(rs[:, 2:3], mv[:, 0:1], rs[:, 1:2], ALU.mult).then_inc(s, 1)
                pool.wait_ge(s, 4 * t + 3)
                nc.gpsimd.tensor_tensor(rs[:, 3:4], rs[:, 2:3], minus_one[:, :], ALU.mult).then_inc(s, 1)

            def step(name, t):
                if name == "fetch":
                    pool.wait_ge(attn_loaded, 16 * (t + 1))
                    nc.gpsimd.tensor_tensor(at_in[:, 0, :], at_in[:, 0, :], bv_b[:, :], ALU.add) \
                        .then_inc(attn_biased, 1)
                if name == "y":
                    rstd("y", t)
                if name == "add":
                    rstd("x1", t)

            for entry in W_FIRST:
                if not isinstance(entry, int):
                    step(*entry)
            step("fetch", TPC)

            def chunk(c, more):
                for f in range(-2, FT + 1):
                    for name, r in w_steps(f):
                        step(name, (c + 1) * TPC + r)
                if more:
                    step("fetch", (c + 2) * TPC)
                finish(c)

            def finish(c):
                for r in range(TPC):
                    t = c * TPC + r
                    rstd("out", t, r % 2)
                    pool.wait_ge(yo_normed, t + 1)
                    pool.wait_ge(x1_loaded, 16 * (t + 1))
                    nc.gpsimd.tensor_tensor(yo[:, r % 2, :], yo[:, r % 2, :], x1_in[:, :], ALU.add) \
                        .then_inc(out_set, 1)

            with pool.Fori(0, NCH - 2) as c:
                chunk(c, True)
            chunk(NCH - 2, False)
            finish(NCH - 1)

        @block.scalar
        def _(act):
            def split(n):
                hi, _, _, k, cols, rws = pieces[n]
                act.wait_ge(raw_loaded[n % 2], 16 * (n // 2 + 1))
                nc.scalar.activation(hi, raw[0:rws, n % 2, 0:k * cols].rearrange("p (k n) -> p k n", k=k),
                                     ACT.Copy, scale=WS).then_inc(piece_hi, 1)

            def step(name, t, r):
                if name in ("turn", "back"):
                    act.wait_ge(turn_psum if name == "turn" else back_psum, t + 1)
                    dst, s = (turned(t)["hi"], at_hi) if name == "turn" else (x1t["hi"], x1t_hi)
                    cols = slice(0, P) if name == "turn" else slice(r * P, (r + 1) * P)
                    for h in range(2):
                        nc.scalar.activation(dst[:, 4 * h:4 * h + 4, cols],
                                             w_banks(name, t)[h][:, :].rearrange("p (k n) -> p k n", k=4),
                                             ACT.Copy).then_inc(s, 1)
                if name == "add":
                    act.wait_ge(ln_rstd["y"], 4 * t + 4)
                    nc.scalar.activation(y[:, :], y[:, :], ACT.Identity, bias=ln["y"][0][2][:, 3:4],
                                         scale=ln["y"][0][2][:, 1:2]).then_inc(y_normed, 1)
                if name == "norm":
                    act.wait_ge(ln_rstd["x1"], 4 * t + 4)
                    if not (isinstance(t, int) and t == 0):
                        act.wait_ge(back_psum, t)
                    nc.scalar.activation(xn1[:, :], y[:, :], ACT.Identity, bias=ln["x1"][0][2][:, 3:4],
                                         scale=ln["x1"][0][2][:, 1:2]).then_inc(x1_normed, 1)

            pieces_left = iter(range(len(pieces)))
            for entry in W_FIRST:
                if isinstance(entry, int):
                    for _, n in zip(range(entry), pieces_left):
                        split(n)
                else:
                    step(*entry, entry[1])
            for n in pieces_left:
                split(n)
            act.wait_ge(biases, 16 * 2)
            nc.scalar.activation(b1u_c[:, :], b1u_c[:, :], ACT.Copy, scale=WS * WS).then_inc(bias_scaled, 1)

            def chunk(c, more):
                def w_at(f):
                    if more:
                        for name, r in w_steps(f):
                            step(name, (c + 1) * TPC + r, r)

                w_at(-2)
                for r in range(RC):
                    act.wait_ge(p1_psum, RC * c + r + 1)
                    nc.scalar.activation(p1t["hi"][:, r, :], zp[r][:, :], ACT.Copy).then_inc(p1_hi, 1)
                w_at(-1)

                def high(f):
                    act.wait_ge(a32_set, FT * c + f + 1)
                    m = inner(f)
                    nc.scalar.activation(act_t["hi"][0:m, f % 3, :], a32[0:m, f % 3, :], ACT.Copy,
                                         scale=1.0 / WS).then_inc(act_hi_set, 1)

                for f in range(FT):
                    m = inner(f)
                    act.wait_ge(pair_psum, PAIR_USES * c + f + 1)
                    nc.scalar.activation(sg[0:m, f % 2, :], pair[f % 2][0][0:m, :], ACT.Silu,
                                         bias=b1g_c[0:m, f:f + 1], scale=1.0 / (WS * WS)).then_inc(sg_set, 1)
                    if f:
                        high(f - 1)
                    w_at(f)
                high(FT - 1)
                act.wait_ge(z_psum, c + 1)
                for r in range(RC):
                    nc.scalar.activation(zt["hi"][:, r, :], zp[r][:, :], ACT.Copy, scale=1.0 / WS).then_inc(z_hi, 1)
                w_at(FT)
                for r in range(TPC):
                    act.wait_ge(ln_rstd["out"], 4 * (c * TPC + r) + 4)
                    nc.scalar.activation(yo[:, r % 2, :], yo[:, r % 2, :], ACT.Identity,
                                         bias=ln["out"][r % 2][2][:, 3:4], scale=ln["out"][r % 2][2][:, 1:2]) \
                        .then_inc(yo_normed, 1)

            with act.Fori(0, NCH - 1) as c:
                chunk(c, True)
            chunk(NCH - 1, False)

        @block.vector
        def _(dve):
            nc.vector.sem_inc(out_taken, TPC)

            def split(n):
                hi, lo, _, k, cols, rws = pieces[n]
                dve.wait_ge(piece_hi, n + 1)
                nc.vector.scalar_tensor_tensor(
                    out=lo, in0=raw[0:rws, n % 2, 0:k * cols].rearrange("p (k n) -> p k n", k=k), scalar=WS,
                    in1=hi, op0=ALU.mult, op1=ALU.subtract).then_inc(piece_lo, 1)

            def evacuate(banks, dst, bias, s):
                for h in range(2):
                    ins = nc.vector.scalar_tensor_tensor(
                        out=dst[:, h * CH:(h + 1) * CH], in0=banks[h][:, :], scalar=1.0 / (WS * WS),
                        in1=bias[:, h * CH:(h + 1) * CH], op0=ALU.mult, op1=ALU.add)
                ins.then_inc(s, 1)

            def statistics(n, t, src, b=0):
                stt, mv, _ = ln[n][b]
                for h in range(2):
                    ins = nc.vector.bn_stats(stt[:, h, :], src[:, h * CH:(h + 1) * CH])
                ins.then_inc(ln_chain[n], 1)
                dve.wait_ge(ln_chain[n], t + 1)
                nc.vector.sem_inc(wait_carrier, 1)
                nc.vector.bn_aggr(mv[:, :], stt[:, :, :].rearrange("p a b -> p (a b)")).then_inc(ln_stats[n], 1)

            def step(name, t, r):
                if name in ("turn", "back"):
                    dst, s = (turned(t), at_hi) if name == "turn" else (x1t, x1t_hi)
                    cols = slice(0, P) if name == "turn" else slice(r * P, (r + 1) * P)
                    for h in range(2):
                        dve.wait_ge(s, 2 * t + h + 1)
                        ins = nc.vector.tensor_tensor(dst["lo"][:, 4 * h:4 * h + 4, cols],
                                                      w_banks(name, t)[h][:, :].rearrange("p (k n) -> p k n", k=4),
                                                      dst["hi"][:, 4 * h:4 * h + 4, cols], ALU.subtract)
                    ins.then_inc(turn_taken if name == "turn" else back_taken, 1)
                if name == "y":
                    dve.wait_ge(project_psum, t + 1)
                    if not (isinstance(t, int) and t == 0):
                        dve.wait_ge(x1_normed, t)
                        dve.wait_ge(x1_stored, 16 * t)
                    evacuate(w_banks("project", t), y, bo_b, y_taken)
                    dve.wait_ge(y_taken, t + 1)
                    statistics("y", t, y)
                if name == "add":
                    dve.wait_ge(y_normed, t + 1)
                    dve.wait_ge(x_loaded2, 16 * (t + 1))
                    nc.vector.tensor_tensor(y[:, :], y[:, :], x_in[:, :], ALU.add).then_inc(x1_set, 1)
                    dve.wait_ge(x1_set, t + 1)
                    statistics("x1", t, y)

            pieces_left = iter(range(len(pieces)))
            for entry in W_FIRST:
                if isinstance(entry, int):
                    for _, n in zip(range(entry), pieces_left):
                        split(n)
                else:
                    step(*entry, entry[1])
            for n in pieces_left:
                split(n)
            dve.wait_ge(bias_scaled, 1)

            def chunk(c, more):
                def w_at(f):
                    if more:
                        for name, r in w_steps(f):
                            step(name, (c + 1) * TPC + r, r)

                w_at(-2)
                for r in range(RC):
                    dve.wait_ge(p1_hi, RC * c + r + 1)
                    nc.vector.tensor_tensor(p1t["lo"][:, r, :], zp[r][:, :], p1t["hi"][:, r, :],
                                            ALU.subtract).then_inc(p1_lo, 1)
                w_at(-1)

                def low(f):
                    dve.wait_ge(act_hi_set, FT * c + f + 1)
                    m = inner(f)
                    nc.vector.scalar_tensor_tensor(out=act_t["lo"][0:m, f % 3, :], in0=a32[0:m, f % 3, :],
                                                   scalar=1.0 / WS, in1=act_t["hi"][0:m, f % 3, :],
                                                   op0=ALU.mult, op1=ALU.subtract).then_inc(act_lo_set, 1)

                for f in range(FT):
                    m = inner(f)
                    dve.wait_ge(sg_set, FT * c + f + 1)
                    nc.vector.scalar_tensor_tensor(out=a32[0:m, f % 3, :], in0=pair[f % 2][1][0:m, :],
                                                   scalar=b1u_c[0:m, f:f + 1], in1=sg[0:m, f % 2, :],
                                                   op0=ALU.add, op1=ALU.mult).then_inc(a32_set, 1)
                    if f:
                        low(f - 1)
                    w_at(f)
                low(FT - 1)
                for r in range(RC):
                    dve.wait_ge(z_hi, RC * c + r + 1)
                    nc.vector.scalar_tensor_tensor(out=zt["lo"][:, r, :], in0=zp[r][:, :], scalar=1.0 / WS,
                                                   in1=zt["hi"][:, r, :], op0=ALU.mult,
                                                   op1=ALU.subtract).then_inc(z_lo, 1)
                w_at(FT)
                for r in range(TPC):
                    t = c * TPC + r
                    dve.wait_ge(pair_psum, PAIR_USES * c + FT + r + 1)
                    dve.wait_ge(out_stored[r % 2], 16 * (c * (TPC // 2) + r // 2) + 16)
                    evacuate(pair[r % 2], yo[:, r % 2, :], b2_b, out_taken)
                    dve.wait_ge(out_taken, t + 1 + TPC)
                    statistics("out", t, yo[:, r % 2, :], r % 2)

            with dve.Fori(0, NCH - 1) as c:
                chunk(c, True)
            chunk(NCH - 1, False)

        @block.tensor
        def _(pe):
            pe.wait_ge(pool_chain, 2)
            parts = [("hi", "hi"), ("hi", "lo"), ("lo", "hi")]

            def step(name, t):
                if name == "project":
                    pe.wait_ge(turn_taken, t + 1)
                    if isinstance(t, int) and 2 <= t < TPC:
                        pe.wait_ge(y_taken, t - 1)
                    for h in range(2):
                        for a, b in parts:
                            for k in range(KC):
                                ins = nc.tensor.matmul(w_banks(name, t)[h][:, :], turned(t)[a][:, k, :],
                                                       w["wo"][b][:, k, h * CH:(h + 1) * CH],
                                                       start=(a, b, k) == ("hi", "hi", 0),
                                                       stop=(a, b, k) == ("lo", "hi", KC - 1))
                    ins.then_inc(project_psum, 1)
                if name in ("turn", "back"):
                    pe.wait_ge(attn_biased if name == "turn" else x1_normed, t + 1)
                    if not (isinstance(t, int) and t == 0):
                        first = isinstance(t, int) and t < TPC
                        pe.wait_ge(turn_taken if first and name == "turn" else back_taken, t)
                    src = at_in[:, 0, :] if name == "turn" else xn1[:, :]
                    for k in range(KC):
                        ins = nc.tensor.transpose(w_banks(name, t)[k // 4][:, (k % 4) * P:(k % 4 + 1) * P],
                                                  src[:, k * P:(k + 1) * P], ident2[:, :])
                    ins.then_inc(turn_psum if name == "turn" else back_psum, 1)

            for entry in W_FIRST:
                if not isinstance(entry, int):
                    step(*entry)

            def chunk(c, more):
                def w_at(f):
                    if more:
                        for name, r in w_steps(f):
                            step(name, (c + 1) * TPC + r)

                w_at(-2)
                pe.wait_ge(back_taken, (c + 1) * TPC)
                for r in range(RC):
                    for a, b in parts:
                        for k in range(KC):
                            ins = nc.tensor.matmul(zp[r][:, :], w["u1"][b][:, k, r * P:(r + 1) * P],
                                                   x1t[a][:, k, :], start=(a, b, k) == ("hi", "hi", 0),
                                                   stop=(a, b, k) == ("lo", "hi", KC - 1))
                    ins.then_inc(p1_psum, 1)
                w_at(-1)
                pe.wait_ge(p1_lo, RC * (c + 1))

                def gate_up(f):
                    m = inner(f)
                    if f >= 2:
                        pe.wait_ge(a32_set, FT * c + f - 1)
                    else:
                        pe.wait_ge(out_taken, TPC * c + 3 + f)
                    pe.wait_ge(piece_lo, 2 * ((f * P + m - 1) // (PIECE // 2) + 1))
                    for i, base in enumerate((0, INTER)):
                        for a, b in parts:
                            for k in range(RC):
                                ins = nc.tensor.matmul(pair[f % 2][i][0:m, :],
                                                       w["v1"][b][:, k, base + f * P:base + f * P + m],
                                                       p1t[a][:, k, :], start=(a, b, k) == ("hi", "hi", 0),
                                                       stop=(a, b, k) == ("lo", "hi", RC - 1))
                    ins.then_inc(pair_psum, 1)

                def down(f):
                    m = inner(f)
                    pe.wait_ge(act_lo_set, FT * c + f + 1)
                    for r in range(RC):
                        for a, b in parts:
                            ins = nc.tensor.matmul(zp[r][:, :], w["u2"][b][0:m, f, r * P:(r + 1) * P],
                                                   act_t[a][0:m, f % 3, :], start=f == 0 and (a, b) == parts[0],
                                                   stop=f == FT - 1 and (a, b) == parts[-1])
                    if f == FT - 1:
                        ins.then_inc(z_psum, 1)

                for f in range(FT):
                    gate_up(f)
                    if f >= Z_LAG:
                        down(f - Z_LAG)
                    w_at(f)
                for f in range(FT - Z_LAG, FT):
                    down(f)
                w_at(FT)
                pe.wait_ge(z_lo, RC * (c + 1))
                pe.wait_ge(piece_lo, len(pieces))
                for r in range(TPC):
                    if r < 2:
                        pe.wait_ge(a32_set, FT * c + FT - 1 + r)
                    else:
                        pe.wait_ge(out_taken, TPC * c + r - 1 + TPC)
                    for h in range(2):
                        for a, b in parts:
                            for k in range(RC):
                                ins = nc.tensor.matmul(pair[r % 2][h][:, :], zt[a][:, k, r * P:(r + 1) * P],
                                                       w["v2"][b][:, k, h * CH:(h + 1) * CH],
                                                       start=(a, b, k) == ("hi", "hi", 0),
                                                       stop=(a, b, k) == ("lo", "hi", RC - 1))
                    ins.then_inc(pair_psum, 1)

            with pe.Fori(0, NCH - 1) as c:
                chunk(c, True)
            chunk(NCH - 1, False)


def block_kernel(nc, x, wq, bq, wk, bk, wv, bv, wo, bo, u1, v1, u2, v2, b1g, b1u, b2, out):
    attn = nc.dram_tensor("attn_scratch", (S, D), F32).ap()
    x1 = nc.dram_tensor("x1_scratch", (S, D), F32).ap()
    dram = {"wo": wo, "u1": u1, "v1": v1, "u2": u2, "v2": v2}
    with ExitStack() as ctx:
        shared = ctx.enter_context(nc.sbuf_tensor("shared", [P, 2 * KC * S], F16))
        vectors = ctx.enter_context(nc.sbuf_tensor("vectors", [P, 3 * D], F32))
        attention_phase(nc, shared, vectors, x, wq, wk, wv, bq, bk, attn, dram, (bv, bo, b2))
        ffn_phase(nc, shared, vectors, x, attn, dram, b1g, b1u, x1, out)


def kernel(L0_attn_x, L0_attn_Wq, L0_attn_bq, L0_attn_Wk, L0_attn_bk, L0_attn_Wv, L0_attn_bv, L0_attn_Wo,
           L0_attn_bo, L0_ffn_U1, L0_ffn_V1, L0_ffn_U2, L0_ffn_V2, L0_ffn_b1, L0_ffn_b2):
    import numpy as np
    import concourse.bacc as bacc
    from concourse.bass_utils import run_bass_kernel_spmd

    def by_group(w):
        w = np.asarray(w).T.reshape(KC, P, NG, P)
        return np.ascontiguousarray(w.transpose(2, 1, 0, 3).reshape(NG, P, KC * P))

    def columns(b):
        padded = np.zeros(FT * P, b.dtype)
        padded[:INTER] = b
        return np.ascontiguousarray(padded.reshape(FT, P).T)

    b1 = np.asarray(L0_ffn_b1)
    arrays = {
        "x": np.asarray(L0_attn_x).reshape(S, D),
        "wq": by_group(L0_attn_Wq), "bq": np.asarray(L0_attn_bq).reshape(NG, P, 1),
        "wk": by_group(L0_attn_Wk), "bk": np.asarray(L0_attn_bk).reshape(NG, P, 1),
        "wv": by_group(L0_attn_Wv), "bv": np.asarray(L0_attn_bv).reshape(1, D),
        "wo": np.ascontiguousarray(np.asarray(L0_attn_Wo).T), "bo": np.asarray(L0_attn_bo).reshape(1, D),
        "u1": np.asarray(L0_ffn_U1), "v1": np.asarray(L0_ffn_V1),
        "u2": np.asarray(L0_ffn_U2), "v2": np.asarray(L0_ffn_V2),
        "b1g": columns(b1[:INTER]), "b1u": columns(b1[INTER:]), "b2": np.asarray(L0_ffn_b2).reshape(1, D),
    }
    arrays = {n: np.ascontiguousarray(a) for n, a in arrays.items()}
    nc = bacc.Bacc("TRN2", target_bir_lowering=False, num_devices=1)
    args = {n: nc.dram_tensor(f"in_{n}", a.shape, mybir.dt.from_np(a.dtype), kind="ExternalInput").ap()
            for n, a in arrays.items()}
    out = nc.dram_tensor("out", (S, D), F32, kind="ExternalOutput").ap()
    block_kernel(nc, **args, out=out)
    r = run_bass_kernel_spmd(nc, [{f"in_{n}": a for n, a in arrays.items()}], core_ids=[0])
    return r.results[0]["out"].reshape(1, S, D)
```

```python
from contextlib import ExitStack

import concourse.bass as bass
from concourse import mybir

F32 = mybir.dt.float32
F16 = mybir.dt.float16
BF16 = mybir.dt.bfloat16
ALU = mybir.AluOpType
ACT = mybir.ActivationFunctionType
AX = mybir.AxisListType

P = 128
S = 2048
D = 1024
NH = 32
HD = D // NH
GH = P // HD
NG = NH // GH
KC = D // P
TT = S // P
CH = 512
NCH = S // CH
TPC = CH // P
RANK = 256
RC = RANK // P
INTER = 2752
FT = -(-INTER // P)
FLAST = INTER - (FT - 1) * P
EPS = 1e-5

WS = 16.0
MROW = 2048.0
EXP_SCALE = 1.0 / (WS * WS * HD ** 0.5)
NEG = -1e30

VW = 2 * HD + 1
STK = 3 * HD
ROWS = STK + 2

BLOCKS = []
for qc in range(NCH):
    for kt in range(TPC * (qc + 1)):
        q0 = max(CH * qc, P * kt)
        BLOCKS.append((qc, kt, q0, CH * (qc + 1) - q0, kt >= TPC * qc))
NB = len(BLOCKS)
GB = GH * NB
MBLOCKS = [(t, c, min(CH, (t + 1) * P - c * CH), c == t // TPC) for t in range(TT) for c in range(t // TPC + 1)]
MR = len(MBLOCKS) + 1
MSPAN = 35
LAG = 5
RING = 8
ST_BANKS = 3
MX_BANKS = 3

QK_START, QK_EVERY, QK_SPAN = 6, 13, 8
V_START, V_EVERY, V_SPAN = 113, 12, 8
PER_GROUP = 2 * NCH + NCH
SPLIT_AT = {0: 0, 1: 30, 2: 60}


def hi_on_dve(s):
    return s % 4 == 2


def hi_on_act(s):
    return not hi_on_dve(s)


def lo_on_dve(s):
    return s % 4 == 3


def lo_on_pool(s):
    return not lo_on_dve(s)


def count(which, s):
    per = sum(map(which, range(GB)))
    return per * (s // GB) + sum(map(which, range(s % GB + 1)))


def same_bank_before(s, banks, uses):
    return s - banks if s >= banks else max(x for x in range(uses) if x % banks == s % banks) - uses


EARLY = sum((t < TT - TPC) for t, _, _, _ in MBLOCKS)
EARLY_PER = EARLY // 3
assert EARLY % 3 == 0 and GH == NCH


def early_at(n):
    return 4 + 7 * n


def max_blocks_at(i):
    return [a for a in range(len(MBLOCKS)) if a * MSPAN // len(MBLOCKS) == i]


def projections():
    out = [("qk"[n // NCH], n % NCH, QK_START + QK_EVERY * n, QK_SPAN) for n in range(2 * NCH)]
    return out + [("v", n, V_START + V_EVERY * n, V_SPAN) for n in range(NCH)]


PROJ = projections()

ENDS = [NB * j + max(i for i, bl in enumerate(BLOCKS) if bl[0] == qc) for j in range(GH) for qc in range(NCH)]


def values_at(s):
    at = [v + LAG + (BLOCKS[v % NB][1] == 0) for v in range(GB)]
    return [v for v in range(GB) if at[v] == s or (s == GB and at[v] > s)]


def chunks_at(s, delay):
    return [c for c, e in enumerate(ENDS) if e + delay == s]


def chunks_after(delay, last):
    return [c for c, e in enumerate(ENDS) if e + delay > last]


def steps_of(kind):
    parts = [("hi", "hi"), ("hi", "lo"), ("lo", "hi")]
    if kind == "v":
        return [(r, p, k) for r in range(TPC) for p in parts for k in range(KC)]
    return [(None, p, k) for p in parts for k in range(KC)]


def attention_phase(nc, shared, vectors, x, wq, wk, wv, bq, bk, attn, later, later_biases):
    ctx = ExitStack()
    with ctx:
        def sb(name, shape, dt):
            return ctx.enter_context(nc.sbuf_tensor(name, shape, dt))

        def ps(name, shape, dt=F32):
            return ctx.enter_context(nc.psum_tensor(name, shape, dt))

        def sem(name):
            return ctx.enter_context(nc.semaphore(name))

        ident = sb("ident", [P, P], F32)
        ident_h = sb("ident_h", [P, P], F16)
        ident_b = sb("ident_b", [P, P], BF16)
        mask_qk = sb("mask_qk", [P, P], BF16)
        mask_kq = sb("mask_kq", [P, P], BF16)
        neg_half = sb("neg_half", [P, 1], F32)
        xt = {h: shared[:, n * KC * S:(n + 1) * KC * S].rearrange("p (k n) -> p k n", k=KC)
              for n, h in enumerate(("hi", "lo"))}
        stats = sb("stats", [P, 2, 2, 6], F32)
        mv = sb("mv", [P, 2, 2], F32)
        rs = sb("rs", [P, 2, 4], F32)
        w_raw = [sb(f"w_raw{i}", [P, KC * P], F32) for i in range(3)]
        w_all = vectors[:, :].bitcast(F16).rearrange("p (i h k n) -> p i h k n", i=3, h=2, k=KC)
        w = [{h: w_all[:, i, n, :, :] for n, h in enumerate(("hi", "lo"))} for i in range(3)]
        b_raw = [sb(f"b_raw{i}", [P, 1], F32) for i in range(2)]
        b_sc = [sb(f"b_sc{i}", [P, 1], F32) for i in range(2)]
        nat = [{h: sb(f"nat_{h}{i}", [P, S], F16) for h in ("hi", "lo")} for i in range(2)]
        q_st = [sb(f"q_st{j}", [P, S], F16) for j in range(GH)]
        k_st = [sb(f"k_st{j}", [P, S], F16) for j in range(GH)]
        v_next = sb("v_next", [P, GH, TT, VW], F16)
        v_cur = sb("v_cur", [P, GH, TT, VW], F16)
        p32 = sb("p32", [P, RING, CH], F32)
        p_hi = sb("p_hi", [P, RING, CH], F16)
        p_lo = sb("p_lo", [P, RING, CH], F16)
        m_part = sb("m_part", [P, TT, NCH], F32)
        m_all = sb("m_all", [P, TT], F32)
        m_cols = sb("m_cols", [P, 2 * TT], F16)
        m_rows = sb("m_rows", [2 * TT, P], F16)
        o_cp = sb("o_cp", [P, 2, TPC, VW], F32)
        o_rd = sb("o_rd", [P, 2, TPC], F32)
        o_sum = sb("o_sum", [P, 2, TPC, HD], F32)
        attn_g = sb("attn_g", [P, TT, P], F32)

        xin = p32[:, 0:3 * D // CH, :].rearrange("p (t h) n -> p t (h n)", t=3)
        xn = attn_g[:, :, :].rearrange("p (t a) n -> p t (a n)", t=2)

        st = [ps(f"st{i}", [P, CH]) for i in range(ST_BANKS)]
        mx = [ps(f"mx{i}", [P, CH]) for i in range(MX_BANKS)]
        av = ps("av", [P, CH])
        pj = ps("pj", [P, CH])

        consts = sem("consts")
        consts_dve = sem("consts_dve")
        x_loaded = [sem(f"x_loaded{i}") for i in range(3)]
        x_stats = sem("x_stats")
        dve_step = sem("dve_step")
        pool_step = sem("pool_step")
        x_rstd = sem("x_rstd")
        x_normed = sem("x_normed")
        xt_psum = sem("xt_psum")
        xt_hi = sem("xt_hi")
        xt_lo = sem("xt_lo")
        w_loaded = [sem(f"w_loaded{i}") for i in range(3)]
        w_hi = [sem(f"w_hi{i}") for i in range(3)]
        w_lo = [sem(f"w_lo{i}") for i in range(3)]
        proj_psum = sem("proj_psum")
        proj_hi = sem("proj_hi")
        proj_lo = sem("proj_lo")
        stack_set = [sem(f"stack_set{j}") for j in range(GH)]
        stack_early = sem("stack_early")
        v_set = [sem(f"v_set{j}") for j in range(GH)]
        m_psum = sem("m_psum")
        m_done = sem("m_done")
        m_chain = sem("m_chain")
        m_cols_set = sem("m_cols_set")
        m_rows_set = sem("m_rows_set")
        m_in_stack = sem("m_in_stack")
        st_psum = sem("st_psum")
        p32_set = sem("p32_set")
        hi_act = sem("hi_act")
        hi_dve = sem("hi_dve")
        lo_dve = sem("lo_dve")
        lo_pool = sem("lo_pool")
        av_psum = sem("av_psum")
        av_used = sem("av_used")
        rd_set = sem("rd_set")
        o_added = sem("o_added")
        o_done = sem("o_done")
        attn_free = sem("attn_free")

        early_loaded = [sem(f"early_loaded{i}") for i in range(3)]
        early_hi = sem("early_hi")
        early_lo = sem("early_lo")
        biases_loaded = sem("biases_loaded")

        early = early_pieces(weights_in(shared), later)
        x_t = x.rearrange("(t p) d -> t p d", p=P)
        attn_v = attn.rearrange("(t p) f -> p t f", p=P)
        w_dram = [wq, wk, wv]
        b_dram = [bq, bk]

        def proj_no(g, n):
            return g * PER_GROUP + n

        FIRST = [(kind, c) for c in range(NCH) for kind in "qkv"]
        first_banks = [pj, st[0], st[1]]
        turn = [[mx[0], mx[1]], [mx[2], av]]

        def xt_after(no):
            c, a = no // 3, no % 3
            if c == NCH - 1:
                return []
            return [TPC * (c + 1) + n for n in ((0, 1), (2, 3), ())[a]]

        block = ctx.enter_context(nc.Block())

        @block.sync
        def _(sp):
            def load_w(i, g):
                sp.dma_start(w_raw[i][:, :], w_dram[i][bass.ds(g, 1), :, :].rearrange("a p n -> (a p) n")) \
                    .then_inc(w_loaded[i], 16)
                if i < 2:
                    sp.dma_start(b_raw[i][:, :], b_dram[i][bass.ds(g, 1), :, :].rearrange("a p n -> (a p) n")) \
                        .then_inc(w_loaded[i], 16)

            def set_stack(j, cols=slice(0, S), s=None):
                s = s or stack_set[j]
                for r, (a, b) in enumerate((("hi", "hi"), ("hi", "lo"), ("lo", "hi"))):
                    sp.dma_start(q_st[j][HD * r:HD * (r + 1), cols], nat[0][a][HD * j:HD * (j + 1), cols]) \
                        .then_inc(s, 16)
                    sp.dma_start(k_st[j][HD * r:HD * (r + 1), cols], nat[1][b][HD * j:HD * (j + 1), cols]) \
                        .then_inc(s, 16)

            def set_max_rows(no, j):
                sp.wait_ge(m_rows_set, no + 1)
                for part in range(2):
                    sp.dma_start(q_st[j][STK + part:STK + part + 1, :].rearrange("a (t p) -> a t p", p=P),
                                 m_rows[TT * part:TT * (part + 1), :]) \
                        .then_inc(m_in_stack, 16)

            def set_v(j):
                sp.dma_start(v_cur[:, j, :, :], v_next[:, j, :, :]).then_inc(v_set[j], 16)

            sp.dma_start(xin[:, 0, :], x_t[0]).then_inc(x_loaded[0], 16)
            load_w(0, 0)
            sp.dma_start(xin[:, 1, :], x_t[1]).then_inc(x_loaded[1], 16)
            load_w(1, 0)
            sp.dma_start(xin[:, 2, :], x_t[2]).then_inc(x_loaded[2], 16)
            load_w(2, 0)
            for t in range(3, TT):
                sp.wait_ge(x_normed, t - 2)
                sp.dma_start(xin[:, t % 3, :], x_t[t]).then_inc(x_loaded[t % 3], 16)
            for i in range(3):
                sp.wait_ge(w_lo[i], 1)
                load_w(i, 1)
            sp.wait_ge(proj_lo, PER_GROUP - 4)
            set_stack(0, slice(0, S - CH), stack_early)
            sp.wait_ge(proj_lo, PER_GROUP - 1)
            set_stack(0, slice(S - CH, S), stack_set[0])
            for j in range(1, GH):
                set_stack(j)
            sp.wait_ge(proj_lo, PER_GROUP)
            for j in range(GH):
                set_v(j)
            set_max_rows(0, 0)

            def group(g, more):
                def load_next(i):
                    sp.wait_ge(w_lo[i], g + 2)
                    load_w(i, g + 2)

                if not more:
                    last_group()
                    return
                if more == 2:
                    load_next(0)
                set_max_rows(g * GH + 1, 1)
                if more == 2:
                    load_next(1)
                    load_next(2)
                set_max_rows(g * GH + 2, 2)
                if more:
                    sp.wait_ge(proj_lo, proj_no(g + 1, 2 * NCH))
                    set_stack(0)
                set_max_rows(g * GH + 3, 3)
                if more:
                    set_stack(1)
                    sp.wait_ge(st_psum, g * GB + 3 * NB)
                    set_stack(2)
                    set_max_rows(g * GH + 4, 0)
                    sp.wait_ge(proj_lo, proj_no(g + 2, 0))
                    for j in range(GH - 1):
                        set_v(j)
                    sp.wait_ge(st_psum, g * GB + 4 * NB)
                    set_stack(3)
                    sp.wait_ge(av_psum, g * GH * NCH + GH * NCH)
                    set_v(GH - 1)
                sp.wait_ge(o_done, g * GH * NCH + GH * NCH + 2)
                sp.dma_start(attn_v[:, :, bass.ds(g * P, P)], attn_g[:, :, :]).then_inc(attn_free, 16)

            def last_group():
                def load_early(n):
                    if n >= 3:
                        sp.wait_ge(early_lo, n - 2)
                    _, _, src, k, cols, rws = early[n]
                    sp.dma_start(w_raw[n % 3][0:rws, 0:k * cols].rearrange("p (k n) -> p k n", k=k), src) \
                        .then_inc(early_loaded[n % 3], 16)

                g = NG - 1
                for n in range(3):
                    load_early(n)
                for n, bias in enumerate(later_biases):
                    sp.dma_start(vectors[:, n * D:(n + 1) * D], bias.broadcast_to([P, D])).then_inc(biases_loaded, 16)
                for s in range(GB):
                    for n in range(3, len(early)):
                        if early_at(n - 3) == s:
                            load_early(n)
                    if s % NB == MSPAN + 1 and s < GB - NB:
                        set_max_rows(g * GH + s // NB + 1, s // NB + 1)
                sp.wait_ge(biases_loaded, 16 * len(later_biases))
                sp.wait_ge(o_done, GH * NCH * NG + 2)
                sp.dma_start(attn_v[:, :, g * P:(g + 1) * P], attn_g[:, :, :]).then_inc(attn_free, 16)

            with sp.Fori(0, NG - 2) as g:
                group(g, 2)
            group(NG - 2, 1)
            group(NG - 1, 0)
            sp.wait_ge(attn_free, 16 * NG + 16)

        @block.gpsimd
        def _(pool):
            n_step = [0]

            def step(ins):
                n_step[0] += 1
                ins.then_inc(pool_step, 1)
                pool.wait_ge(pool_step, n_step[0])

            for m in (ident, ident_h, ident_b):
                step(nc.gpsimd.memset(m[:, :], 0.0))
                step(nc.gpsimd.affine_select(out=m[:, :], in_=m[:, :], compare_op=ALU.not_equal, fill=1.0,
                                             base=0, pattern=[[-1, P]], channel_multiplier=1))
            for m, sign in ((mask_qk, 1), (mask_kq, -1)):
                step(nc.gpsimd.memset(m[:, :], 0.0))
                step(nc.gpsimd.affine_select(out=m[:, :], in_=m[:, :], compare_op=ALU.is_ge, fill=NEG,
                                             base=0, pattern=[[-sign, P]], channel_multiplier=sign))
            step(nc.gpsimd.memset(neg_half[:, :], -0.5))
            nc.gpsimd.memset(v_next[:, :, :, HD:HD + 1], 1.0).then_inc(consts, 1)
            for t in range(TT):
                b = t % 2
                pool.wait_ge(x_stats, t + 1)
                if t >= 2:
                    pool.wait_ge(x_normed, t - 1)
                step(nc.gpsimd.tensor_scalar(rs[:, b, 0:1], mv[:, b, 1:2], EPS, None, ALU.add))
                step(nc.gpsimd.tensor_tensor(rs[:, b, 1:2], rs[:, b, 0:1], neg_half[:, :], ALU.pow))
                step(nc.gpsimd.tensor_tensor(rs[:, b, 2:3], mv[:, b, 0:1], rs[:, b, 1:2], ALU.mult))
                nc.gpsimd.tensor_scalar(rs[:, b, 3:4], rs[:, b, 2:3], -1.0, None, ALU.mult).then_inc(x_rstd, 1)

            nc.gpsimd.sem_inc(o_done, 2)
            nc.gpsimd.sem_inc(attn_free, 16)

            def group(g):
                def low_part(s):
                    if hi_on_dve(s):
                        pool.wait_ge(hi_dve, g * count(hi_on_dve, GB - 1) + count(hi_on_dve, s))
                    else:
                        pool.wait_ge(hi_act, g * count(hi_on_act, GB - 1) + count(hi_on_act, s) + ST_BANKS)
                    wd = BLOCKS[s % NB][3]
                    r = s % RING
                    nc.gpsimd.tensor_tensor(p_lo[:, r, 0:wd], p32[:, r, 0:wd], p_hi[:, r, 0:wd],
                                            ALU.subtract).then_inc(lo_pool, 1)

                def output(c):
                    j, qc = c // NCH, c % NCH
                    no = g * GH * NCH + c
                    b = c % 2
                    pool.wait_ge(rd_set, no + 1)
                    if c == 0:
                        pool.wait_ge(attn_free, 16 * g + 16)
                    nc.gpsimd.tensor_tensor(o_sum[:, b, :, :], o_cp[:, b, :, 0:HD], o_cp[:, b, :, HD + 1:VW],
                                            ALU.add).then_inc(o_added, 1)
                    pool.wait_ge(o_added, no + 1)
                    rd = o_rd[:, b, :].rearrange("p (r a) -> p r a", a=1).broadcast_to([P, TPC, HD])
                    nc.gpsimd.tensor_tensor(attn_g[:, qc * TPC:(qc + 1) * TPC, j * HD:(j + 1) * HD],
                                            o_sum[:, b, :, :], rd, ALU.mult).then_inc(o_done, 1)

                for s in range(GB + 1):
                    if s and not lo_on_dve(s - 1):
                        low_part(s - 1)
                    for c in chunks_at(s, LAG + 3):
                        output(c)
                for c in chunks_after(LAG + 3, GB):
                    output(c)

            with pool.Fori(0, NG) as g:
                group(g)

        @block.scalar
        def _(act):
            def split_w(i, g):
                act.wait_ge(w_loaded[i], (g + 1) * (32 if i < 2 else 16))
                if not (isinstance(g, int) and g == 0):
                    act.wait_ge(proj_lo, proj_no(g, 0))
                nc.scalar.activation(w[i]["hi"][:, :, :].rearrange("p k n -> p (k n)"), w_raw[i][:, :],
                                     ACT.Copy, scale=WS).then_inc(w_hi[i], 1)
                if i < 2:
                    nc.scalar.activation(b_sc[i][:, :], b_raw[i][:, :], ACT.Copy, scale=WS).then_inc(w_hi[i], 1)

            def take_proj(kind, c, bank, no):
                act.wait_ge(proj_psum, no + 1)
                if kind == "v":
                    o = v_next[:, :, c * TPC:(c + 1) * TPC, 0:HD].rearrange("p j t f -> p t j f")
                    i_ = bank[:, :].rearrange("p (t j f) -> p t j f", t=TPC, j=GH)
                    nc.scalar.activation(o, i_, ACT.Copy).then_inc(proj_hi, 1)
                else:
                    i = "qk".index(kind)
                    nc.scalar.activation(nat[i]["hi"][:, c * CH:(c + 1) * CH], bank[:, :], ACT.Identity,
                                         bias=b_sc[i][:, 0:1]).then_inc(proj_hi, 1)

            act.wait_ge(consts, 1)

            def norm_tile(t):
                act.wait_ge(x_rstd, t + 1)
                if t >= 2:
                    act.wait_ge(xt_psum, t - 1)
                nc.scalar.activation(xn[:, t % 2, :], xin[:, t % 3, :], ACT.Identity, bias=rs[:, t % 2, 3:4],
                                     scale=rs[:, t % 2, 1:2]).then_inc(x_normed, 1)

            def take_xt(t):
                act.wait_ge(xt_psum, t + 1)
                for h in range(2):
                    bank = turn[t % 2][h]
                    ins = nc.scalar.activation(xt["hi"][:, 4 * h:4 * h + 4, t * P:(t + 1) * P],
                                               bank[:, :].rearrange("p (k n) -> p k n", k=4), ACT.Copy)
                ins.then_inc(xt_hi, 1)

            for i in range(3):
                if i == 0:
                    norm_tile(0)
                split_w(i, 0)
            for t in range(1, TPC + 1):
                norm_tile(t)
                take_xt(t - 1)
            for c in range(NCH):
                for a in range(3):
                    no = 3 * c + a
                    take_proj(*FIRST[no], first_banks[no % 3], no)
                    for t in xt_after(no):
                        if t + 1 < TT:
                            norm_tile(t + 1)
                        take_xt(t)

            def group(g, more):
                def exps(s):
                    wd = BLOCKS[s % NB][3]
                    r = s % RING
                    act.wait_ge(st_psum, g * GB + s + 1)
                    nc.scalar.activation(p32[:, r, 0:wd], st[s % ST_BANKS][:, 0:wd], ACT.Exp,
                                         scale=EXP_SCALE).then_inc(p32_set, 1)
                    if hi_on_act(s):
                        nc.scalar.activation(p_hi[:, r, 0:wd], st[s % ST_BANKS][:, 0:wd], ACT.Exp,
                                             scale=EXP_SCALE).then_inc(hi_act, 1)

                def copy_out(c):
                    no = g * GH * NCH + c
                    act.wait_ge(av_psum, no + 1)
                    act.wait_ge(o_done, no + 1)
                    nc.scalar.activation(o_cp[:, c % 2, :, :].rearrange("p t f -> p (t f)"),
                                         av[:, 0:TPC * VW], ACT.Copy).then_inc(av_used, 1)

                for s in range(GB):
                    if more:
                        for i, at in SPLIT_AT.items():
                            if at == s:
                                split_w(i, g + 1)
                    for c in chunks_at(s, LAG + 1):
                        copy_out(c)
                    exps(s)
                    if more:
                        for n, (kind, c, start, span) in enumerate(PROJ):
                            if start + span == s:
                                if (kind, c) in (("q", 0), ("v", 0)):
                                    for j in range(GH):
                                        act.wait_ge((v_set if kind == "v" else stack_set)[j],
                                                    (16 if kind == "v" else 96) * (g + 1))
                                take_proj(kind, c, pj, proj_no(g + 1, n))
                for c in chunks_after(LAG + 1, GB - 1):
                    copy_out(c)

            nc.scalar.sem_inc(p32_set, ST_BANKS)
            nc.scalar.sem_inc(hi_act, ST_BANKS)
            nc.scalar.sem_inc(av_used, 1)
            with act.Fori(0, NG - 1) as g:
                group(g, True)
            group(NG - 1, False)

        @block.vector
        def _(dve):
            n_step = [0]

            def step(ins):
                n_step[0] += 1
                ins.then_inc(dve_step, 1)
                dve.wait_ge(dve_step, n_step[0])

            def split_w(i, g):
                dve.wait_ge(w_hi[i], (g + 1) * (2 if i < 2 else 1))
                nc.vector.scalar_tensor_tensor(out=w[i]["lo"][:, :, :].rearrange("p k n -> p (k n)"),
                                               in0=w_raw[i][:, :], scalar=WS,
                                               in1=w[i]["hi"][:, :, :].rearrange("p k n -> p (k n)"),
                                               op0=ALU.mult, op1=ALU.subtract).then_inc(w_lo[i], 1)

            def take_proj(kind, c, bank, no):
                dve.wait_ge(proj_hi, no + 1)
                if kind == "v":
                    o = v_next[:, :, c * TPC:(c + 1) * TPC, HD + 1:VW].rearrange("p j t f -> p t j f")
                    h = v_next[:, :, c * TPC:(c + 1) * TPC, 0:HD].rearrange("p j t f -> p t j f")
                    i_ = bank[:, :].rearrange("p (t j f) -> p t j f", t=TPC, j=GH)
                    nc.vector.tensor_tensor(o, i_, h, ALU.subtract).then_inc(proj_lo, 1)
                else:
                    i = "qk".index(kind)
                    nc.vector.scalar_tensor_tensor(out=nat[i]["lo"][:, c * CH:(c + 1) * CH], in0=bank[:, :],
                                                   scalar=b_sc[i][:, 0:1], in1=nat[i]["hi"][:, c * CH:(c + 1) * CH],
                                                   op0=ALU.add, op1=ALU.subtract).then_inc(proj_lo, 1)


            def stats_tile(t):
                dve.wait_ge(x_loaded[t % 3], 16 * (t // 3 + 1))
                if t >= 2:
                    dve.wait_ge(x_rstd, t - 1)
                for h in range(2):
                    ins = nc.vector.bn_stats(stats[:, t % 2, h, :], xin[:, t % 3, h * CH:(h + 1) * CH])
                step(ins)
                nc.vector.bn_aggr(mv[:, t % 2, :], stats[:, t % 2, :, :].rearrange("p a b -> p (a b)")) \
                    .then_inc(x_stats, 1)

            def take_xt(t):
                dve.wait_ge(xt_hi, t + 1)
                for h in range(2):
                    bank = turn[t % 2][h]
                    ins = nc.vector.tensor_tensor(xt["lo"][:, 4 * h:4 * h + 4, t * P:(t + 1) * P],
                                                  bank[:, :].rearrange("p (k n) -> p k n", k=4),
                                                  xt["hi"][:, 4 * h:4 * h + 4, t * P:(t + 1) * P], ALU.subtract)
                ins.then_inc(xt_lo, 1)

            stats_tile(0)
            nc.vector.memset(m_part[:, :, :], -3e38).then_inc(consts_dve, 1)
            for i in range(3):
                split_w(i, 0)
            stats_tile(1)
            for t in range(TPC):
                stats_tile(t + 2)
                take_xt(t)
            def max_columns(no):
                dve.wait_ge(m_done, (no + 1) * len(MBLOCKS))
                nc.vector.tensor_reduce(m_all[:, :], m_part[:, :, :], AX.X, ALU.max).then_inc(m_chain, 1)
                dve.wait_ge(m_chain, 2 * no + 1)
                nc.vector.tensor_scalar(m_cols[:, 0:TT], m_all[:, :], -1.0 / MROW, None, ALU.mult).then_inc(m_chain, 1)
                dve.wait_ge(m_chain, 2 * no + 2)
                nc.vector.scalar_tensor_tensor(out=m_cols[:, TT:2 * TT], in0=m_all[:, :], scalar=-1.0 / MROW,
                                               in1=m_cols[:, 0:TT], op0=ALU.mult, op1=ALU.subtract) \
                    .then_inc(m_cols_set, 1)

            def block_max(n, a, use0):
                t, c, wd, _ = MBLOCKS[a]
                dve.wait_ge(m_psum, use0 + a + 1)
                nc.vector.tensor_reduce(m_part[:, t, c:c + 1], mx[(n + a) % MX_BANKS][:, 0:wd], AX.X, ALU.max) \
                    .then_inc(m_done, 1)

            def head_max(n, i, use0, no):
                for a in max_blocks_at(i):
                    block_max(n, a, use0)
                if i == MSPAN:
                    max_columns(no)
                if i == MSPAN + 1:
                    dve.wait_ge(m_psum, use0 + MR)
                    if not (isinstance(no, int) and no == 0):
                        dve.wait_ge(m_in_stack, 32 * no)
                    bank = mx[(n + MR - 1) % MX_BANKS][0:2 * TT, 0:P // 2].bitcast(F16)
                    nc.vector.tensor_copy(m_rows[:, :], bank).then_inc(m_rows_set, 1)

            for c in range(NCH):
                if c == NCH - 1:
                    dve.wait_ge(consts_dve, 2 * GH + 1)
                for a in range(3):
                    no = 3 * c + a
                    if c == NCH - 1:
                        for b in range(a * EARLY_PER, (a + 1) * EARLY_PER):
                            block_max((GH - 1) * MR, b, 0)
                    take_proj(*FIRST[no], first_banks[no % 3], no)
                    for t in xt_after(no):
                        if t + 2 < TT:
                            stats_tile(t + 2)
                        take_xt(t)
                for j in range(GH):
                    if c < NCH - 1 and j % (NCH - 1) == c:
                        nc.vector.memset(q_st[j][STK:P, :], 0.0).then_inc(consts_dve, 1)
                        nc.vector.memset(k_st[j][STK:P, :], MROW).then_inc(consts_dve, 1)

            for a in range(EARLY, len(MBLOCKS)):
                block_max((GH - 1) * MR, a, 0)
            for i in (MSPAN, MSPAN + 1):
                head_max((GH - 1) * MR, i, 0, 0)

            def group(g, more):
                def cast(s):
                    dve.wait_ge(p32_set, g * GB + s + 1 + ST_BANKS)
                    wd = BLOCKS[s % NB][3]
                    r = s % RING
                    nc.vector.tensor_copy(p_hi[:, r, 0:wd], p32[:, r, 0:wd]).then_inc(hi_dve, 1)

                def low_part(s):
                    dve.wait_ge(hi_act, g * count(hi_on_act, GB - 1) + count(hi_on_act, s) + ST_BANKS)
                    wd = BLOCKS[s % NB][3]
                    r = s % RING
                    nc.vector.tensor_tensor(p_lo[:, r, 0:wd], p32[:, r, 0:wd], p_hi[:, r, 0:wd],
                                            ALU.subtract).then_inc(lo_dve, 1)

                def reciprocal(c):
                    no = g * GH * NCH + c
                    dve.wait_ge(av_used, no + 1 + 1)
                    nc.vector.reciprocal(o_rd[:, c % 2, :], o_cp[:, c % 2, :, HD]).then_inc(rd_set, 1)

                def split_early(n):
                    hi, lo, _, k, cols, rws = early[n]
                    raw = w_raw[n % 3][0:rws, 0:k * cols].rearrange("p (k n) -> p k n", k=k)
                    dve.wait_ge(early_loaded[n % 3], 16 * (n // 3 + 1))
                    nc.vector.tensor_scalar(hi, raw, WS, None, ALU.mult).then_inc(early_hi, 1)
                    dve.wait_ge(early_hi, n + 1)
                    nc.vector.scalar_tensor_tensor(out=lo, in0=raw, scalar=WS, in1=hi, op0=ALU.mult,
                                                   op1=ALU.subtract).then_inc(early_lo, 1)

                for s in range(GB + 1):
                    j, i = s // NB, s % NB
                    if not more:
                        for n in range(len(early)):
                            if early_at(n) == s:
                                split_early(n)
                        if s == GB - NB:
                            dve.wait_ge(biases_loaded, 16 * len(later_biases))
                            nc.vector.tensor_scalar(vectors[:, 0:D], vectors[:, 0:D], WS, None, ALU.mult)
                    if s < GB and more and s - 1 in SPLIT_AT.values():
                        split_w({v: k for k, v in SPLIT_AT.items()}[s - 1], g + 1)
                    if s < GB and (more or j < GH - 1):
                        head_max(j * MR, i, MR + g * GH * MR + j * MR, g * GH + j + 1)
                    if s and hi_on_dve(s - 1):
                        cast(s - 1)
                    if s and lo_on_dve(s - 1):
                        low_part(s - 1)
                    if more:
                        for n, (kind, c, start, span) in enumerate(PROJ):
                            if start + span + 1 == s:
                                take_proj(kind, c, pj, proj_no(g + 1, n))
                    for c in chunks_at(s, LAG + 2):
                        reciprocal(c)
                for c in chunks_after(LAG + 2, GB):
                    reciprocal(c)

            with dve.Fori(0, NG - 1) as g:
                group(g, True)
            group(NG - 1, False)

        @block.tensor
        def _(pe):
            def transpose_x(t):
                pe.wait_ge(x_normed, t + 1)
                if t >= 2:
                    pe.wait_ge(xt_lo, t - 1)
                for k in range(KC):
                    ins = nc.tensor.transpose(turn[t % 2][k // 4][:, (k % 4) * P:(k % 4 + 1) * P],
                                              xn[:, t % 2, k * P:(k + 1) * P], ident[:, :])
                ins.then_inc(xt_psum, 1)

            def project(kind, c, bank, lo, hi):
                i = "qkv".index(kind)
                steps = steps_of(kind)
                for m in range(lo, min(hi, len(steps))):
                    r, (a, b), k = steps[m]
                    first, last = (a, b, k) == ("hi", "hi", 0), (a, b, k) == ("lo", "hi", KC - 1)
                    if kind == "v":
                        t = c * TPC + r
                        ins = nc.tensor.matmul(bank[:, r * P:(r + 1) * P], xt[a][:, k, t * P:(t + 1) * P],
                                               w[i][b][:, k, :], start=first, stop=last)
                    else:
                        ins = nc.tensor.matmul(bank[:, :], w[i][b][:, k, :], xt[a][:, k, c * CH:(c + 1) * CH],
                                               start=first, stop=last)
                    if m == len(steps) - 1:
                        ins.then_inc(proj_psum, 1)

            def block_scores(n, a, j, no):
                t, c, wd, diagonal = MBLOCKS[a]
                back, b = divmod(same_bank_before(n + a, MX_BANKS, GH * MR), MR)
                head = no + back - n // MR
                if not (isinstance(head, int) and head < 0):
                    if b < MR - 1:
                        pe.wait_ge(m_done, head * len(MBLOCKS) + b + 1)
                    else:
                        pe.wait_ge(m_rows_set, head + 1)
                bank = mx[(n + a) % MX_BANKS]
                ins = nc.tensor.matmul(bank[:, 0:wd], q_st[j][0:STK, t * P:(t + 1) * P],
                                       k_st[j][0:STK, c * CH:c * CH + wd], start=True, stop=not diagonal)
                if diagonal:
                    ins = nc.tensor.matmul(bank[:, wd - P:wd], ident_b[:, :], mask_qk[:, :],
                                           start=False, stop=True)
                ins.then_inc(m_psum, 1)

            def head_max(n, i, j, no):
                for a in max_blocks_at(i):
                    block_scores(n, a, j, no)
                if i == MSPAN + 1:
                    pe.wait_ge(m_cols_set, no + 1)
                    nc.tensor.transpose(mx[(n + MR - 1) % MX_BANKS][0:2 * TT, 0:P // 2].bitcast(F16), m_cols[:, :],
                                        ident_h[:, :]).then_inc(m_psum, 1)

            pe.wait_ge(consts, 1)
            for t in range(TPC):
                transpose_x(t)
            for c in range(NCH):
                pe.wait_ge(xt_lo, TPC * (c + 1))
                for a in range(3):
                    no = 3 * c + a
                    kind, _ = FIRST[no]
                    if c == 0:
                        pe.wait_ge(w_lo[a], 1)
                    if no >= 3:
                        pe.wait_ge(proj_lo, no - 2)
                    if c < NCH - 1:
                        project(kind, c, first_banks[no % 3], 0, 1 << 30)
                    else:
                        per = len(steps_of(kind)) // EARLY_PER
                        if a == 0:
                            pe.wait_ge(stack_early, 96)
                        for n in range(EARLY_PER):
                            project(kind, c, first_banks[no % 3], n * per, (n + 1) * per)
                            block_scores((GH - 1) * MR, a * EARLY_PER + n, 0, 0)
                    for t in xt_after(no):
                        transpose_x(t)
            pe.wait_ge(consts_dve, 2 * GH + 1)
            pe.wait_ge(stack_set[0], 96)
            for a in range(EARLY, len(MBLOCKS)):
                block_scores((GH - 1) * MR, a, 0, 0)
            head_max((GH - 1) * MR, MSPAN + 1, 0, 0)

            def group(g, more):
                def scores(s):
                    j, i = s // NB, s % NB
                    qc, kt, q0, wd, diagonal = BLOCKS[i]
                    if i == 0:
                        pe.wait_ge(m_in_stack, 32 * (g * GH + j + 1))
                    before = same_bank_before(s, ST_BANKS, GB)
                    if hi_on_dve(before):
                        pe.wait_ge(p32_set, g * GB + before + 1 + ST_BANKS)
                    else:
                        pe.wait_ge(hi_act, g * count(hi_on_act, GB - 1) + count(hi_on_act, before) + ST_BANKS)
                    bank = st[s % ST_BANKS]
                    ins = nc.tensor.matmul(bank[:, 0:wd], k_st[j][0:ROWS, kt * P:(kt + 1) * P],
                                           q_st[j][0:ROWS, q0:q0 + wd], start=True, stop=not diagonal)
                    if diagonal:
                        ins = nc.tensor.matmul(bank[:, 0:P], ident_b[:, :], mask_kq[:, :], start=False, stop=True)
                    ins.then_inc(st_psum, 1)

                def values(s):
                    j, i = s // NB, s % NB
                    qc, kt, q0, wd, _ = BLOCKS[i]
                    r = s % RING
                    c = j * NCH + qc
                    if i == 0:
                        pe.wait_ge(v_set[j], 16 * (g + 1))
                    if kt == 0:
                        pe.wait_ge(av_used, g * GH * NCH + c + 1)
                    if lo_on_dve(s):
                        pe.wait_ge(lo_dve, g * count(lo_on_dve, GB - 1) + count(lo_on_dve, s))
                    else:
                        pe.wait_ge(lo_pool, g * count(lo_on_pool, GB - 1) + count(lo_on_pool, s))
                    first = True
                    for n in range(wd // P):
                        t = (q0 + n * P) // P - qc * TPC
                        o = av[:, t * VW:(t + 1) * VW]
                        stop = kt == qc * TPC + t
                        nc.tensor.matmul(o, p_hi[:, r, n * P:(n + 1) * P], v_cur[:, j, kt, :],
                                         start=(kt == 0 and n == 0), stop=False, skip_group_check=True)
                        ins = nc.tensor.matmul(o[:, 0:HD + 1], p_lo[:, r, n * P:(n + 1) * P],
                                               v_cur[:, j, kt, 0:HD + 1], start=False, stop=stop,
                                               skip_group_check=True)
                    if s in ENDS:
                        ins.then_inc(av_psum, 1)

                for s in range(GB):
                    j, i = s // NB, s % NB
                    scores(s)
                    if more or j < GH - 1:
                        jn = (j + 1) % GH
                        if i == 0:
                            pe.wait_ge(stack_set[jn], 96 * (g + 1 if jn else g + 2))
                        head_max(j * MR, i, jn, g * GH + j + 1)
                    if more:
                        for n, (kind, c, start, span) in enumerate(PROJ):
                            if start <= s < start + span:
                                per = len(steps_of(kind)) // span
                                if s == start:
                                    pe.wait_ge(proj_lo, proj_no(g + 1, n))
                                    if c == 0:
                                        pe.wait_ge(w_lo["qkv".index(kind)], g + 2)
                                project(kind, c, pj, per * (s - start), per * (s - start + 1))
                    for v in values_at(s):
                        values(v)
                for v in values_at(GB):
                    values(v)

            with pe.Fori(0, NG - 1) as g:
                group(g, True)
            group(NG - 1, False)


W_STEPS = ("turn", "project", "y", "add", "norm", "back")
W_START = [-1, 5, 10, 15]
W_FIRST = [("fetch", 0), ("turn", 0), ("fetch", 1), ("turn", 1), ("fetch", 2), ("project", 0), ("turn", 2),
           ("fetch", 3), 3, ("y", 0), 1, ("add", 0), 2, ("norm", 0),
           ("project", 1), ("turn", 3), ("y", 1), 1, ("add", 1), ("fetch", 4), 1, ("norm", 1), 1,
           ("project", 2), ("back", 0), ("y", 2), ("take", 0), ("add", 2), 1, ("norm", 2),
           ("project", 3), ("turn", 4), ("back", 1), ("y", 3), ("take", 1), ("add", 3), 1, ("norm", 3), 1,
           ("project", 4), ("back", 2), ("take", 2), ("back", 3), ("take", 3)]
Z_LAG = 2
PAIR_USES = FT + TPC
assert RC % 2 == FT % 2 == TPC % 2 == 0
PIECE = 1024


def weights_in(shared):
    flat = shared[:, :]
    w, at = {}, 0
    for name, k, n in (("wo", KC, D), ("u1", KC, RANK), ("u2", FT, RANK)):
        w[name] = {}
        for h in ("hi", "lo"):
            w[name][h] = flat[:, at:at + k * n].rearrange("p (k n) -> p k n", k=k)
            at += k * n
    return w


def early_pieces(w, dram):
    out = []

    def add(name, index, src, shape):
        rows, k, n = shape
        out.append((w[name]["hi"][index], w[name]["lo"][index], src, k, n, rows))

    wo, u1, u2 = (dram[n] for n in ("wo", "u1", "u2"))
    for k in range(KC):
        add("wo", (slice(0, P), slice(k, k + 1), slice(0, D)),
            wo[k * P:(k + 1) * P, :].rearrange("(k p) n -> p k n", p=P), (P, 1, D))
    for k in range(0, KC, 4):
        add("u1", (slice(0, P), slice(k, k + 4), slice(0, RANK)),
            u1[k * P:(k + 4) * P, :].rearrange("(k p) n -> p k n", p=P), (P, 4, RANK))
    for f in range(0, FT - 1, 4):
        n = min(4, FT - 1 - f)
        add("u2", (slice(0, P), slice(f, f + n), slice(0, RANK)),
            u2[f * P:(f + n) * P, :].rearrange("(k p) n -> p k n", p=P), (P, n, RANK))
    add("u2", (slice(0, FLAST), slice(FT - 1, FT), slice(0, RANK)),
        u2[(FT - 1) * P:INTER, :].rearrange("(k p) n -> p k n", p=FLAST), (FLAST, 1, RANK))
    return out


def late_pieces(w, dram):
    out = []

    def add(name, index, src, shape):
        rows, k, n = shape
        out.append((w[name]["hi"][index], w[name]["lo"][index], src, k, n, rows))

    v1, v2 = dram["v1"], dram["v2"]
    for at in range(0, INTER, PIECE // 2):
        n = min(PIECE // 2, INTER - at)
        for base in (0, INTER):
            add("v1", (slice(0, P), slice(0, RC), slice(base + at, base + at + n)),
                v1[:, base + at:base + at + n].rearrange("(k p) n -> p k n", p=P), (P, RC, n))
    for k in range(RC):
        add("v2", (slice(0, P), slice(k, k + 1), slice(0, D)),
            v2[k * P:(k + 1) * P, :].rearrange("(k p) n -> p k n", p=P), (P, 1, D))
    return out


def ffn_phase(nc, shared, vectors, x, attn, dram, b1g, b1u, x1, out):
    ctx = ExitStack()
    with ctx:
        def sb(name, shape, dt):
            return ctx.enter_context(nc.sbuf_tensor(name, shape, dt))

        def ps(name, shape, dt=F32):
            return ctx.enter_context(nc.psum_tensor(name, shape, dt))

        def sem(name):
            return ctx.enter_context(nc.semaphore(name))

        w = weights_in(shared)
        for name, shape in (("v1", [P, RC, 2 * INTER]), ("v2", [P, RC, D])):
            w[name] = {h: sb(f"{name}_{h}", shape, F16) for h in ("hi", "lo")}
        pieces = late_pieces(w, dram)
        v1_pieces = 2 * (-(-INTER // (PIECE // 2)))
        raw = sb("raw", [P, 2, PIECE], F32)
        ident2 = sb("ident2", [P, P], F32)
        neg_half2 = sb("neg_half2", [P, 1], F32)
        eps_c = sb("eps_c", [P, 1], F32)
        minus_one = sb("minus_one", [P, 1], F32)
        bv_b, bo_b, b2_b = (vectors[:, n * D:(n + 1) * D] for n in range(3))
        b1g_c = sb("b1g_c", [P, FT], F32)
        b1u_c = sb("b1u_c", [P, FT], F32)
        at_in = sb("at_in", [P, 1, D], F32)
        at_t = {h: sb(f"at_{h}", [P, KC, P], F16) for h in ("hi", "lo")}
        x_in = sb("x_in", [P, D], F32)
        y = sb("y", [P, D], F32)
        xn1 = sb("xn1", [P, D], F32)
        x1t = {h: sb(f"x1t_{h}", [P, KC, CH], F16) for h in ("hi", "lo")}
        spare = shared[:, 2 * KC * S - RC * CH:].rearrange("p (k n) -> p k n", k=RC)
        p1t = {"hi": spare, "lo": sb("p1t_lo", [P, RC, CH], F16)}
        sg = sb("sg", [P, 2, CH], F32)
        a32 = sb("a32", [P, 3, CH], F32)
        act_t = {h: sb(f"act_{h}", [P, 3, CH], F16) for h in ("hi", "lo")}
        zt = {h: sb(f"zt_{h}", [P, RC, CH], F16) for h in ("hi", "lo")}
        yo_mem = sb("yo", [P, 2, D], F32)
        yo = [yo_mem[:, 0, :], yo_mem[:, 1, :], raw[:, 0, :], raw[:, 1, :]]
        x1_in = sb("x1_in", [P, D], F32)
        x1_last = [x1_in[:, :], x_in[:, :], y[:, :], xn1[:, :]]
        ln = {n: [(sb(f"st_{n}{i}", [P, 2, 6], F32), sb(f"mv_{n}{i}", [P, 2], F32), sb(f"rs_{n}{i}", [P, 4], F32))
                  for i in range(TPC if n == "out" else 1)] for n in ("y", "x1", "out")}

        pair = [[ps(f"pair{i}{h}", [P, CH]) for h in range(2)] for i in range(2)]
        wp = [ps(f"wp{h}", [P, CH]) for h in range(2)]
        zp = [ps(f"zp{r}", [P, CH]) for r in range(RC)]

        pool_chain = sem("pool_chain")
        biases = sem("biases")
        bias_scaled = sem("bias_scaled")
        raw_loaded = [sem(f"raw_loaded{i}") for i in range(2)]
        piece_hi = sem("piece_hi")
        piece_lo = sem("piece_lo")
        attn_loaded = sem("attn_loaded")
        attn_biased = sem("attn_biased")
        x_loaded2 = sem("x_loaded2")
        turn_psum = sem("turn_psum")
        turn_taken = sem("turn_taken")
        project_psum = sem("project_psum")
        y_taken = sem("y_taken")
        back_psum = sem("back_psum")
        back_taken = sem("back_taken")
        at_hi = sem("at_hi")
        ln_stats = {n: sem(f"ln_stats_{n}") for n in ln}
        wait_carrier = sem("wait_carrier")
        ln_chain = {n: sem(f"ln_chain_{n}") for n in ln}
        ln_rstd = {n: sem(f"ln_rstd_{n}") for n in ln}
        y_normed = sem("y_normed")
        x1_set = sem("x1_set")
        x1_stored = sem("x1_stored")
        x1_normed = sem("x1_normed")
        x1t_hi = sem("x1t_hi")
        p1_psum = sem("p1_psum")
        pair_psum = sem("pair_psum")
        p1_lo = sem("p1_lo")
        out_taken = sem("out_taken")
        p1_hi = sem("p1_hi")
        sg_set = sem("sg_set")
        a32_set = sem("a32_set")
        act_hi_set = sem("act_hi_set")
        act_lo_set = sem("act_lo_set")
        z_psum = sem("z_psum")
        z_hi = sem("z_hi")
        z_lo = sem("z_lo")
        yo_normed = sem("yo_normed")
        x1_loaded = sem("x1_loaded")
        out_set = sem("out_set")
        out_stored = [sem(f"out_stored{i}") for i in range(TPC)]

        def rows(t):
            return (bass.ds(t * P, P), slice(0, D))

        def inner(f):
            return FLAST if f == FT - 1 else P

        def w_steps(f, more):
            if not more:
                return []
            found = [(name, r) for r, at in enumerate(W_START) for n, name in enumerate(W_STEPS)
                     if at + n == f and (r or n >= 2)]
            found += [("fetch", r + 1) for r in range(TPC) if r + 1 < TPC + more - 1 and W_START[r] + 2 == f]
            return found + ([(W_STEPS[f - FT + 1], TPC)] if more == 2 and f >= FT - 1 else [])

        def alone(t):
            return isinstance(t, int) and t <= TPC

        def w_banks(name, t):
            if alone(t) and (name == "turn" or (name != "project" and t >= 2)):
                return zp
            return pair[t % 2] if name == "project" and alone(t) and t < TPC else wp

        def transposed_before(entry):
            past = [e for e in W_FIRST[:W_FIRST.index(entry)] if not isinstance(e, int) and e[0] in ("turn", "back")
                    and w_banks(*e) is w_banks(*entry)]
            return (turn_taken if past[-1][0] == "turn" else back_taken, past[-1][1] + 1) if past else None

        def y_of(t):
            return yo[0] if isinstance(t, int) and t < TPC and t % 2 else y[:, :]

        def xn_of(t):
            return yo[1] if isinstance(t, int) and t < TPC and t % 2 else xn1[:, :]

        def before(t):
            return max(t - 1, 0) if isinstance(t, int) and t < TPC else t

        def turned(t):
            if alone(t) and t % 2:
                return {h: x1t[h][:, :, CH - P:CH] for h in ("hi", "lo")}
            return {h: at_t[h][:, :, :] for h in ("hi", "lo")}

        block = ctx.enter_context(nc.Block())

        @block.sync
        def _(sp):
            def load_piece(n):
                hi, lo, src, k, cols, rws = pieces[n]
                if n >= 2:
                    sp.wait_ge(piece_lo, n - 1)
                sp.dma_start(raw[0:rws, n % 2, 0:k * cols].rearrange("p (k n) -> p k n", k=k), src) \
                    .then_inc(raw_loaded[n % 2], 16)

            def step(name, t):
                if name == "fetch":
                    if not (isinstance(t, int) and t == 0):
                        sp.wait_ge(turn_psum, t)
                    sp.dma_start(at_in[:, 0, :], attn[rows(t)]).then_inc(attn_loaded, 16)
                if name == "y":
                    if not (isinstance(t, int) and t == 0):
                        sp.wait_ge(x1_set, t)
                    sp.dma_start(x_in[:, :], x[rows(t)]).then_inc(x_loaded2, 16)
                if name == "norm":
                    sp.wait_ge(x1_set, t + 1)
                    sp.dma_start(x1[rows(t)], y_of(t)).then_inc(x1_stored, 16)

            pieces_left = iter(range(2, len(pieces)))
            for at, entry in enumerate(W_FIRST):
                if isinstance(entry, int):
                    for _, n in zip(range(entry), pieces_left):
                        load_piece(n)
                else:
                    step(*entry)
                if at == 0:
                    sp.dma_start(b1g_c[:, :], b1g).then_inc(biases, 16)
                    sp.dma_start(b1u_c[:, :], b1u).then_inc(biases, 16)
                    load_piece(0)
                    load_piece(1)
            for n in pieces_left:
                load_piece(n)

            def finish(c, more):
                sp.wait_ge(x1_stored, 16 * TPC * (c + 1))
                if not more:
                    sp.wait_ge(out_set, c * TPC + 1)
                    sp.wait_ge(x1_normed, TT)
                    sp.wait_ge(back_psum, TT)
                    for r in range(TPC):
                        sp.dma_start(x1_last[r], x1[rows(c * TPC + r)]).then_inc(x1_loaded, 16)
                for r in range(TPC):
                    t = c * TPC + r
                    if more:
                        sp.wait_ge(out_set, t + 1)
                        sp.dma_start(x1_in[:, :], x1[rows(t)]).then_inc(x1_loaded, 16)
                    sp.wait_ge(out_set, t + 2)
                    sp.dma_start(out[rows(t)], yo[r]).then_inc(out_stored[r], 16)

            def chunk(c, more):
                for f in range(FT + 1):
                    for name, r in w_steps(f, more):
                        step(name, (c + 1) * TPC + r)
                finish(c, more)

            with sp.Fori(0, NCH - 2) as c:
                chunk(c, 2)
            chunk(NCH - 2, 1)
            chunk(NCH - 1, 0)
            for r in range(TPC):
                sp.wait_ge(out_stored[r], 16 * NCH + 16)

        @block.gpsimd
        def _(pool):
            nc.gpsimd.memset(ident2[:, :], 0.0).then_inc(pool_chain, 1)
            pool.wait_ge(pool_chain, 1)
            nc.gpsimd.affine_select(out=ident2[:, :], in_=ident2[:, :], compare_op=ALU.not_equal, fill=1.0,
                                    base=0, pattern=[[-1, P]], channel_multiplier=1).then_inc(pool_chain, 1)
            for c, value in ((neg_half2, -0.5), (eps_c, EPS), (minus_one, -1.0)):
                nc.gpsimd.memset(c[:, :], value).then_inc(pool_chain, 1)
            pool.wait_ge(pool_chain, 5)
            nc.gpsimd.sem_inc(out_set, 1)
            for r in range(TPC):
                nc.gpsimd.sem_inc(out_stored[r], 16)

            def rstd(n, t, b=0):
                _, mv, rs = ln[n][b]
                s = ln_rstd[n]
                pool.wait_ge(ln_stats[n], t + 1)
                nc.gpsimd.tensor_tensor(rs[:, 0:1], mv[:, 1:2], eps_c[:, :], ALU.add).then_inc(s, 1)
                pool.wait_ge(s, 4 * t + 1)
                nc.gpsimd.tensor_tensor(rs[:, 1:2], rs[:, 0:1], neg_half2[:, :], ALU.pow).then_inc(s, 1)
                pool.wait_ge(s, 4 * t + 2)
                nc.gpsimd.tensor_tensor(rs[:, 2:3], mv[:, 0:1], rs[:, 1:2], ALU.mult).then_inc(s, 1)
                pool.wait_ge(s, 4 * t + 3)
                nc.gpsimd.tensor_tensor(rs[:, 3:4], rs[:, 2:3], minus_one[:, :], ALU.mult).then_inc(s, 1)

            def step(name, t):
                if name == "fetch":
                    pool.wait_ge(attn_loaded, 16 * (t + 1))
                    nc.gpsimd.tensor_tensor(at_in[:, 0, :], at_in[:, 0, :], bv_b[:, :], ALU.add) \
                        .then_inc(attn_biased, 1)
                if name == "y":
                    rstd("y", t)
                if name == "add":
                    rstd("x1", t)

            for entry in W_FIRST:
                if not isinstance(entry, int):
                    step(*entry)

            def chunk(c, more):
                for f in range(FT + 1):
                    for name, r in w_steps(f, more):
                        step(name, (c + 1) * TPC + r)
                finish(c, more)

            def finish(c, more):
                def add(r):
                    t = c * TPC + r
                    pool.wait_ge(yo_normed, t + 1)
                    pool.wait_ge(x1_loaded, 16 * (t + 1))
                    nc.gpsimd.tensor_tensor(yo[r], yo[r], x1_in[:, :], ALU.add).then_inc(out_set, 1)

                for r in range(TPC):
                    rstd("out", c * TPC + r, r)
                    if more and r == 1:
                        add(0)
                if more:
                    for r in range(1, TPC):
                        add(r)

            with pool.Fori(0, NCH - 2) as c:
                chunk(c, 2)
            chunk(NCH - 2, 1)
            chunk(NCH - 1, 0)

        @block.scalar
        def _(act):
            def split(n):
                hi, _, _, k, cols, rws = pieces[n]
                act.wait_ge(raw_loaded[n % 2], 16 * (n // 2 + 1))
                nc.scalar.activation(hi, raw[0:rws, n % 2, 0:k * cols].rearrange("p (k n) -> p k n", k=k),
                                     ACT.Copy, scale=WS).then_inc(piece_hi, 1)

            def step(name, t, r):
                if name in ("turn", "take"):
                    act.wait_ge(turn_psum if name == "turn" else back_psum, t + 1)
                    dst, s = (turned(t)["hi"], at_hi) if name == "turn" else (x1t["hi"], x1t_hi)
                    cols = slice(0, P) if name == "turn" else slice(r * P, (r + 1) * P)
                    for h in range(2):
                        nc.scalar.activation(dst[:, 4 * h:4 * h + 4, cols],
                                             w_banks(name, t)[h][:, :].rearrange("p (k n) -> p k n", k=4),
                                             ACT.Copy).then_inc(s, 1)
                if name == "add":
                    act.wait_ge(ln_rstd["y"], 4 * t + 4)
                    nc.scalar.activation(y_of(t), y_of(t), ACT.Identity, bias=ln["y"][0][2][:, 3:4],
                                         scale=ln["y"][0][2][:, 1:2]).then_inc(y_normed, 1)
                if name == "norm":
                    act.wait_ge(ln_rstd["x1"], 4 * t + 4)
                    if not (isinstance(t, int) and t < 2):
                        act.wait_ge(back_psum, before(t))
                    nc.scalar.activation(xn_of(t), y_of(t), ACT.Identity, bias=ln["x1"][0][2][:, 3:4],
                                         scale=ln["x1"][0][2][:, 1:2]).then_inc(x1_normed, 1)

            pieces_left = iter(range(len(pieces)))
            for entry in W_FIRST:
                if isinstance(entry, int):
                    for _, n in zip(range(entry), pieces_left):
                        split(n)
                else:
                    step(*entry, entry[1])
            for n in pieces_left:
                split(n)
            act.wait_ge(biases, 16 * 2)
            nc.scalar.activation(b1u_c[:, :], b1u_c[:, :], ACT.Copy, scale=WS * WS).then_inc(bias_scaled, 1)

            def chunk(c, more):
                def w_at(f):
                    for name, r in w_steps(f, more):
                        step("take" if name == "back" else name, (c + 1) * TPC + r, r)

                for r in range(RC):
                    act.wait_ge(p1_psum, RC * c + r + 1)
                    nc.scalar.activation(p1t["hi"][:, r, :], zp[r][:, :], ACT.Copy).then_inc(p1_hi, 1)

                def high(f):
                    act.wait_ge(a32_set, FT * c + f + 1)
                    m = inner(f)
                    nc.scalar.activation(act_t["hi"][0:m, f % 3, :], a32[0:m, f % 3, :], ACT.Copy,
                                         scale=1.0 / WS).then_inc(act_hi_set, 1)

                for f in range(FT):
                    m = inner(f)
                    act.wait_ge(pair_psum, PAIR_USES * c + f + 1)
                    nc.scalar.activation(sg[0:m, f % 2, :], pair[f % 2][0][0:m, :], ACT.Silu,
                                         bias=b1g_c[0:m, f:f + 1], scale=1.0 / (WS * WS)).then_inc(sg_set, 1)
                    if f:
                        high(f - 1)
                    w_at(f)
                high(FT - 1)
                act.wait_ge(z_psum, c + 1)
                for r in range(RC):
                    nc.scalar.activation(zt["hi"][:, r, :], zp[r][:, :], ACT.Copy, scale=1.0 / WS).then_inc(z_hi, 1)
                w_at(FT)
                for r in range(TPC):
                    act.wait_ge(ln_rstd["out"], 4 * (c * TPC + r) + 4)
                    nc.scalar.activation(yo[r], yo[r], ACT.Identity,
                                         bias=ln["out"][r][2][:, 3:4], scale=ln["out"][r][2][:, 1:2]) \
                        .then_inc(yo_normed, 1)

            with act.Fori(0, NCH - 2) as c:
                chunk(c, 2)
            chunk(NCH - 2, 1)
            chunk(NCH - 1, 0)

        @block.vector
        def _(dve):
            nc.vector.sem_inc(out_taken, TPC)

            def split(n):
                hi, lo, _, k, cols, rws = pieces[n]
                dve.wait_ge(piece_hi, n + 1)
                nc.vector.scalar_tensor_tensor(
                    out=lo, in0=raw[0:rws, n % 2, 0:k * cols].rearrange("p (k n) -> p k n", k=k), scalar=WS,
                    in1=hi, op0=ALU.mult, op1=ALU.subtract).then_inc(piece_lo, 1)

            def evacuate(banks, dst, bias, s):
                for h in range(2):
                    ins = nc.vector.scalar_tensor_tensor(
                        out=dst[:, h * CH:(h + 1) * CH], in0=banks[h][:, :], scalar=1.0 / (WS * WS),
                        in1=bias[:, h * CH:(h + 1) * CH], op0=ALU.mult, op1=ALU.add)
                ins.then_inc(s, 1)

            def statistics(n, t, src, b=0):
                stt, mv, _ = ln[n][b]
                for h in range(2):
                    ins = nc.vector.bn_stats(stt[:, h, :], src[:, h * CH:(h + 1) * CH])
                ins.then_inc(ln_chain[n], 1)
                dve.wait_ge(ln_chain[n], t + 1)
                nc.vector.sem_inc(wait_carrier, 1)
                nc.vector.bn_aggr(mv[:, :], stt[:, :, :].rearrange("p a b -> p (a b)")).then_inc(ln_stats[n], 1)

            def step(name, t, r):
                if name in ("turn", "take"):
                    dst, s = (turned(t), at_hi) if name == "turn" else (x1t, x1t_hi)
                    cols = slice(0, P) if name == "turn" else slice(r * P, (r + 1) * P)
                    for h in range(2):
                        dve.wait_ge(s, 2 * t + h + 1)
                        ins = nc.vector.tensor_tensor(dst["lo"][:, 4 * h:4 * h + 4, cols],
                                                      w_banks(name, t)[h][:, :].rearrange("p (k n) -> p k n", k=4),
                                                      dst["hi"][:, 4 * h:4 * h + 4, cols], ALU.subtract)
                    ins.then_inc(turn_taken if name == "turn" else back_taken, 1)
                if name == "y":
                    dve.wait_ge(project_psum, t + 1)
                    if not (isinstance(t, int) and t < 2):
                        dve.wait_ge(x1_normed, before(t))
                        dve.wait_ge(x1_stored, 16 * before(t))
                    evacuate(w_banks("project", t), y_of(t), bo_b, y_taken)
                    dve.wait_ge(y_taken, t + 1)
                    statistics("y", t, y_of(t))
                if name == "add":
                    dve.wait_ge(y_normed, t + 1)
                    dve.wait_ge(x_loaded2, 16 * (t + 1))
                    nc.vector.tensor_tensor(y_of(t), y_of(t), x_in[:, :], ALU.add).then_inc(x1_set, 1)
                    dve.wait_ge(x1_set, t + 1)
                    statistics("x1", t, y_of(t))

            pieces_left = iter(range(len(pieces)))
            for entry in W_FIRST:
                if isinstance(entry, int):
                    for _, n in zip(range(entry), pieces_left):
                        split(n)
                else:
                    step(*entry, entry[1])
            for n in pieces_left:
                split(n)
            dve.wait_ge(bias_scaled, 1)

            def chunk(c, more):
                def w_at(f):
                    for name, r in w_steps(f, more):
                        step("take" if name == "back" else name, (c + 1) * TPC + r, r)

                for r in range(RC):
                    dve.wait_ge(p1_hi, RC * c + r + 1)
                    nc.vector.tensor_tensor(p1t["lo"][:, r, :], zp[r][:, :], p1t["hi"][:, r, :],
                                            ALU.subtract).then_inc(p1_lo, 1)

                def low(f):
                    dve.wait_ge(act_hi_set, FT * c + f + 1)
                    m = inner(f)
                    nc.vector.scalar_tensor_tensor(out=act_t["lo"][0:m, f % 3, :], in0=a32[0:m, f % 3, :],
                                                   scalar=1.0 / WS, in1=act_t["hi"][0:m, f % 3, :],
                                                   op0=ALU.mult, op1=ALU.subtract).then_inc(act_lo_set, 1)

                for f in range(FT):
                    m = inner(f)
                    dve.wait_ge(sg_set, FT * c + f + 1)
                    nc.vector.scalar_tensor_tensor(out=a32[0:m, f % 3, :], in0=pair[f % 2][1][0:m, :],
                                                   scalar=b1u_c[0:m, f:f + 1], in1=sg[0:m, f % 2, :],
                                                   op0=ALU.add, op1=ALU.mult).then_inc(a32_set, 1)
                    if f:
                        low(f - 1)
                    w_at(f)
                low(FT - 1)
                for r in range(RC):
                    dve.wait_ge(z_hi, RC * c + r + 1)
                    nc.vector.scalar_tensor_tensor(out=zt["lo"][:, r, :], in0=zp[r][:, :], scalar=1.0 / WS,
                                                   in1=zt["hi"][:, r, :], op0=ALU.mult,
                                                   op1=ALU.subtract).then_inc(z_lo, 1)
                w_at(FT)
                def add(r):
                    t = c * TPC + r
                    dve.wait_ge(yo_normed, t + 1)
                    dve.wait_ge(x1_loaded, 16 * TT)
                    nc.vector.tensor_tensor(yo[r], yo[r], x1_last[r], ALU.add).then_inc(out_set, 1)

                for r in range(TPC):
                    t = c * TPC + r
                    dve.wait_ge(pair_psum, PAIR_USES * c + FT + r + 1)
                    dve.wait_ge(out_stored[r], 16 * c + 16)
                    evacuate(pair[r % 2], yo[r], b2_b, out_taken)
                    dve.wait_ge(out_taken, t + 1 + TPC)
                    statistics("out", t, yo[r], r)
                    if not more and r:
                        add(r - 1)
                if not more:
                    add(TPC - 1)

            with dve.Fori(0, NCH - 2) as c:
                chunk(c, 2)
            chunk(NCH - 2, 1)
            chunk(NCH - 1, 0)

        @block.tensor
        def _(pe):
            pe.wait_ge(pool_chain, 2)
            parts = [("hi", "hi"), ("hi", "lo"), ("lo", "hi")]

            def step(name, t):
                if name == "project":
                    pe.wait_ge(turn_taken, t + 1)
                    if alone(t) and 2 <= t < TPC:
                        pe.wait_ge(y_taken, t - 1)
                    if alone(t) and t == TPC:
                        pe.wait_ge(*transposed_before((name, t)))
                    for h in range(2):
                        for a, b in parts:
                            for k in range(KC):
                                ins = nc.tensor.matmul(w_banks(name, t)[h][:, :], turned(t)[a][:, k, :],
                                                       w["wo"][b][:, k, h * CH:(h + 1) * CH],
                                                       start=(a, b, k) == ("hi", "hi", 0),
                                                       stop=(a, b, k) == ("lo", "hi", KC - 1))
                    ins.then_inc(project_psum, 1)
                if name in ("turn", "back"):
                    pe.wait_ge(attn_biased if name == "turn" else x1_normed, t + 1)
                    if not alone(t):
                        pe.wait_ge(back_taken, t)
                    elif transposed_before((name, t)):
                        pe.wait_ge(*transposed_before((name, t)))
                    src = at_in[:, 0, :] if name == "turn" else xn_of(t)
                    for k in range(KC):
                        ins = nc.tensor.transpose(w_banks(name, t)[k // 4][:, (k % 4) * P:(k % 4 + 1) * P],
                                                  src[:, k * P:(k + 1) * P], ident2[:, :])
                    ins.then_inc(turn_psum if name == "turn" else back_psum, 1)

            for entry in W_FIRST:
                if not isinstance(entry, int):
                    step(*entry)

            def chunk(c, more):
                def w_at(f):
                    for name, r in w_steps(f, more):
                        step(name, (c + 1) * TPC + r)

                pe.wait_ge(back_taken, (c + 1) * TPC)
                for r in range(RC):
                    for a, b in parts:
                        for k in range(KC):
                            ins = nc.tensor.matmul(zp[r][:, :], w["u1"][b][:, k, r * P:(r + 1) * P],
                                                   x1t[a][:, k, :], start=(a, b, k) == ("hi", "hi", 0),
                                                   stop=(a, b, k) == ("lo", "hi", KC - 1))
                    ins.then_inc(p1_psum, 1)
                pe.wait_ge(p1_lo, RC * (c + 1))

                def gate_up(f):
                    m = inner(f)
                    if f >= 2:
                        pe.wait_ge(a32_set, FT * c + f - 1)
                    else:
                        pe.wait_ge(out_taken, TPC * c + 3 + f)
                    pe.wait_ge(piece_lo, 2 * ((f * P + m - 1) // (PIECE // 2) + 1))
                    for i, base in enumerate((0, INTER)):
                        for a, b in parts:
                            for k in range(RC):
                                ins = nc.tensor.matmul(pair[f % 2][i][0:m, :],
                                                       w["v1"][b][:, k, base + f * P:base + f * P + m],
                                                       p1t[a][:, k, :], start=(a, b, k) == ("hi", "hi", 0),
                                                       stop=(a, b, k) == ("lo", "hi", RC - 1))
                    ins.then_inc(pair_psum, 1)

                def down(f):
                    m = inner(f)
                    pe.wait_ge(act_lo_set, FT * c + f + 1)
                    for r in range(RC):
                        for a, b in parts:
                            ins = nc.tensor.matmul(zp[r][:, :], w["u2"][b][0:m, f, r * P:(r + 1) * P],
                                                   act_t[a][0:m, f % 3, :], start=f == 0 and (a, b) == parts[0],
                                                   stop=f == FT - 1 and (a, b) == parts[-1])
                    if f == FT - 1:
                        ins.then_inc(z_psum, 1)

                for f in range(FT):
                    gate_up(f)
                    if f >= Z_LAG:
                        down(f - Z_LAG)
                    w_at(f)
                for f in range(FT - Z_LAG, FT):
                    down(f)
                w_at(FT)
                pe.wait_ge(z_lo, RC * (c + 1))
                pe.wait_ge(piece_lo, len(pieces))
                for r in range(TPC):
                    if r < 2:
                        pe.wait_ge(a32_set, FT * c + FT - 1 + r)
                    else:
                        pe.wait_ge(out_taken, TPC * c + r - 1 + TPC)
                    for h in range(2):
                        for a, b in parts:
                            for k in range(RC):
                                ins = nc.tensor.matmul(pair[r % 2][h][:, :], zt[a][:, k, r * P:(r + 1) * P],
                                                       w["v2"][b][:, k, h * CH:(h + 1) * CH],
                                                       start=(a, b, k) == ("hi", "hi", 0),
                                                       stop=(a, b, k) == ("lo", "hi", RC - 1))
                    ins.then_inc(pair_psum, 1)

            with pe.Fori(0, NCH - 2) as c:
                chunk(c, 2)
            chunk(NCH - 2, 1)
            chunk(NCH - 1, 0)


def block_kernel(nc, x, wq, bq, wk, bk, wv, bv, wo, bo, u1, v1, u2, v2, b1g, b1u, b2, out):
    attn = nc.dram_tensor("attn_scratch", (S, D), F32).ap()
    x1 = nc.dram_tensor("x1_scratch", (S, D), F32).ap()
    dram = {"wo": wo, "u1": u1, "v1": v1, "u2": u2, "v2": v2}
    with ExitStack() as ctx:
        shared = ctx.enter_context(nc.sbuf_tensor("shared", [P, 2 * KC * S], F16))
        vectors = ctx.enter_context(nc.sbuf_tensor("vectors", [P, 3 * D], F32))
        attention_phase(nc, shared, vectors, x, wq, wk, wv, bq, bk, attn, dram, (bv, bo, b2))
        ffn_phase(nc, shared, vectors, x, attn, dram, b1g, b1u, x1, out)


def kernel(L0_attn_x, L0_attn_Wq, L0_attn_bq, L0_attn_Wk, L0_attn_bk, L0_attn_Wv, L0_attn_bv, L0_attn_Wo,
           L0_attn_bo, L0_ffn_U1, L0_ffn_V1, L0_ffn_U2, L0_ffn_V2, L0_ffn_b1, L0_ffn_b2):
    import numpy as np
    import concourse.bacc as bacc
    from concourse.bass_utils import run_bass_kernel_spmd

    def by_group(w):
        w = np.asarray(w).T.reshape(KC, P, NG, P)
        return np.ascontiguousarray(w.transpose(2, 1, 0, 3).reshape(NG, P, KC * P))

    def columns(b):
        padded = np.zeros(FT * P, b.dtype)
        padded[:INTER] = b
        return np.ascontiguousarray(padded.reshape(FT, P).T)

    b1 = np.asarray(L0_ffn_b1)
    arrays = {
        "x": np.asarray(L0_attn_x).reshape(S, D),
        "wq": by_group(L0_attn_Wq), "bq": np.asarray(L0_attn_bq).reshape(NG, P, 1),
        "wk": by_group(L0_attn_Wk), "bk": np.asarray(L0_attn_bk).reshape(NG, P, 1),
        "wv": by_group(L0_attn_Wv), "bv": np.asarray(L0_attn_bv).reshape(1, D),
        "wo": np.ascontiguousarray(np.asarray(L0_attn_Wo).T), "bo": np.asarray(L0_attn_bo).reshape(1, D),
        "u1": np.asarray(L0_ffn_U1), "v1": np.asarray(L0_ffn_V1),
        "u2": np.asarray(L0_ffn_U2), "v2": np.asarray(L0_ffn_V2),
        "b1g": columns(b1[:INTER]), "b1u": columns(b1[INTER:]), "b2": np.asarray(L0_ffn_b2).reshape(1, D),
    }
    arrays = {n: np.ascontiguousarray(a) for n, a in arrays.items()}
    nc = bacc.Bacc("TRN2", target_bir_lowering=False, num_devices=1)
    args = {n: nc.dram_tensor(f"in_{n}", a.shape, mybir.dt.from_np(a.dtype), kind="ExternalInput").ap()
            for n, a in arrays.items()}
    out = nc.dram_tensor("out", (S, D), F32, kind="ExternalOutput").ap()
    block_kernel(nc, **args, out=out)
    r = run_bass_kernel_spmd(nc, [{f"in_{n}": a for n, a in arrays.items()}], core_ids=[0])
    return r.results[0]["out"].reshape(1, S, D)
```
